# Optimizing a Trainium2 kernel written in Bass

```python
import numpy as np
import jax
import jax.numpy as jnp

def _softmax(x, axis=-1):
    return jax.nn.softmax(x, axis=axis)

def _gelu(x):
    return jax.nn.gelu(x, approximate=True)

def _silu(x):
    return jax.nn.silu(x)

def _sigmoid(x):
    return jax.nn.sigmoid(x)

def _layernorm(x, axis=-1, eps=1e-05):
    m = jnp.mean(x, axis=axis, keepdims=True)
    v = jnp.var(x, axis=axis, keepdims=True)
    return (x - m) / jnp.sqrt(v + eps)

def _scatter_add(tgt, idx, src, axis=0):
    return tgt.at[idx].add(src)

def _segment_sum(src, seg, n):
    return jax.ops.segment_sum(src, seg, n)
kernel_name = 'mk_seq_postln_d2_jaxref_r8_493234'

def setup_inputs(seed: int=0):
    np.random.seed(seed)
    _w = jnp.asarray

    def _L0_attn_setup():
        import jax, jax.numpy as jnp
        import numpy as np
        from jax import lax
        B, L, D_MODEL = (2, 256, 128)
        EXPAND = 2
        D_INNER = D_MODEL * EXPAND
        D_STATE = 16
        D_CONV = 4
        DT_RANK = (D_MODEL + 15) // 16
        EPS = 1e-05

        def _mamba_params(key, pfx, scale=0.02):
            ks = jax.random.split(key, 6)
            return {pfx + '_Win': jax.random.normal(ks[0], (D_MODEL, 2 * D_INNER), jnp.float32) * scale, pfx + '_convw': jax.random.normal(ks[1], (D_INNER, D_CONV), jnp.float32) * scale, pfx + '_convb': jnp.zeros((D_INNER,), jnp.float32), pfx + '_Wx': jax.random.normal(ks[2], (D_INNER, DT_RANK + 2 * D_STATE), jnp.float32) * scale, pfx + '_Wdt': jax.random.normal(ks[3], (DT_RANK, D_INNER), jnp.float32) * scale, pfx + '_bdt': jax.random.uniform(ks[4], (D_INNER,), jnp.float32, -4.0, -2.0), pfx + '_Alog': jnp.log(jnp.broadcast_to(jnp.arange(1, D_STATE + 1, dtype=jnp.float32), (D_INNER, D_STATE))).copy(), pfx + '_D': jnp.ones((D_INNER,), jnp.float32), pfx + '_Wout': jax.random.normal(ks[5], (D_INNER, D_MODEL), jnp.float32) * scale}

        def _layernorm(x, w, b):
            mu = x.mean(-1, keepdims=True)
            xc = x - mu
            v = (xc * xc).mean(-1, keepdims=True)
            return xc * lax.rsqrt(v + EPS) * w + b

        def _causal_dwconv(x, w, b):
            xc = x.transpose(0, 2, 1)
            out = lax.conv_general_dilated(xc, w[:, None, :], window_strides=(1,), padding=[(D_CONV - 1, 0)], feature_group_count=D_INNER, dimension_numbers=('NCH', 'OIH', 'NCH'))
            return (out + b[None, :, None]).transpose(0, 2, 1)

        def _selective_scan(u, dt, A, Bm, Cm, Dp):
            h0 = jnp.zeros((u.shape[0], D_INNER, D_STATE), u.dtype)

            def step(h, inp):
                u_t, dt_t, B_t, C_t = inp
                dA = jnp.exp(dt_t[:, :, None] * A)
                h = dA * h + (dt_t * u_t)[:, :, None] * B_t[:, None, :]
                y = jnp.einsum('bds,bs->bd', h, C_t)
                return (h, y)
            _, ys = lax.scan(step, h0, (u.transpose(1, 0, 2), dt.transpose(1, 0, 2), Bm.transpose(1, 0, 2), Cm.transpose(1, 0, 2)))
            return ys.transpose(1, 0, 2) + u * Dp

        def _mamba(x, Win, convw, convb, Wx, Wdt, bdt, Alog, Dp, Wout):
            xz = x @ Win
            xi, z = jnp.split(xz, 2, axis=-1)
            xi = jax.nn.silu(_causal_dwconv(xi, convw, convb))
            xdbc = xi @ Wx
            dt_in = xdbc[..., :DT_RANK]
            Bm = xdbc[..., DT_RANK:DT_RANK + D_STATE]
            Cm = xdbc[..., DT_RANK + D_STATE:]
            dt = jax.nn.softplus(dt_in @ Wdt + bdt)
            A = -jnp.exp(Alog)
            y = _selective_scan(xi, dt, A, Bm, Cm, Dp)
            return y * jax.nn.silu(z) @ Wout
        key = jax.random.key(seed)
        k = jax.random.split(key, 6)
        inp = {'x': jax.random.normal(k[0], (B, L, D_MODEL), jnp.float32)}
        inp.update(_mamba_params(k[1], 'fw'))
        inp.update(_mamba_params(k[2], 'bw'))
        inp.update({'fwn_w': jnp.ones((D_MODEL,), jnp.float32), 'fwn_b': jnp.zeros((D_MODEL,), jnp.float32), 'fin_w': jnp.ones((D_MODEL,), jnp.float32), 'fin_b': jnp.zeros((D_MODEL,), jnp.float32), 'ff_W1': jax.random.normal(k[3], (D_MODEL, D_MODEL * EXPAND), jnp.float32) * 0.02, 'ff_b1': jnp.zeros((D_MODEL * EXPAND,), jnp.float32), 'ff_W2': jax.random.normal(k[4], (D_MODEL * EXPAND, D_MODEL), jnp.float32) * 0.02, 'ff_b2': jnp.zeros((D_MODEL,), jnp.float32)})
        return inp
    _L0_attn_in = _L0_attn_setup()

    def _L0_ffn_setup():
        import jax, jax.numpy as jnp
        import numpy as np
        D_IN, D_HID = (128, 512)

        def _ternary(key, shape):
            return jax.random.randint(key, shape, -1, 2).astype(jnp.float32)

        def _tlin(x, w, s):
            return jnp.einsum('bsi,oi->bso', x, w) * s
        key = jax.random.key(seed)
        ks = jax.random.split(key, 12)
        inv = lambda fan: 1.0 / np.sqrt(fan).astype(np.float32)
        return {'x': jax.random.normal(ks[0], (4, 256, D_IN), dtype=jnp.float32), 'w1_w': _ternary(ks[1], (D_HID, D_IN)), 'w1_s': jax.random.uniform(ks[2], (D_HID,), dtype=jnp.float32) * inv(D_IN), 'w2_w': _ternary(ks[3], (D_HID, D_IN)), 'w2_s': jax.random.uniform(ks[4], (D_HID,), dtype=jnp.float32) * inv(D_IN), 'h1_w': _ternary(ks[5], (D_HID, D_HID)), 'h1_s': jax.random.uniform(ks[6], (D_HID,), dtype=jnp.float32) * inv(D_HID), 'h2_w': _ternary(ks[7], (D_HID, D_HID)), 'h2_s': jax.random.uniform(ks[8], (D_HID,), dtype=jnp.float32) * inv(D_HID), 'w3_w': _ternary(ks[9], (D_IN, D_HID)), 'w3_s': jax.random.uniform(ks[10], (D_IN,), dtype=jnp.float32) * inv(D_HID)}
    _L0_ffn_in = _L0_ffn_setup()

    def _L1_attn_setup():
        import jax, jax.numpy as jnp
        import numpy as np
        D_MODEL, N_HEADS, N_KV, HEAD_DIM, D_LAT = (128, 8, 2, 128, 32)
        N_REP = N_HEADS // N_KV
        B, T = (2, 256)
        key = jax.random.key(seed)
        ks = jax.random.split(key, 8)
        s = lambda fan_in: 1.0 / np.sqrt(fan_in)
        return {'x': jax.random.normal(ks[0], (B, T, D_MODEL), jnp.float32), 'wq': jax.random.normal(ks[1], (D_MODEL, N_HEADS * HEAD_DIM), jnp.float32) * s(D_MODEL), 'wk_down': jax.random.normal(ks[2], (D_MODEL, N_KV * D_LAT), jnp.float32) * s(D_MODEL), 'wv_down': jax.random.normal(ks[3], (D_MODEL, N_KV * D_LAT), jnp.float32) * s(D_MODEL), 'wk_up': jax.random.normal(ks[4], (D_LAT, HEAD_DIM), jnp.float32) * s(D_LAT), 'wv_up': jax.random.normal(ks[5], (D_LAT, HEAD_DIM), jnp.float32) * s(D_LAT), 'wo': jax.random.normal(ks[6], (N_HEADS * HEAD_DIM, D_MODEL), jnp.float32) * s(N_HEADS * HEAD_DIM)}
    _L1_attn_in = _L1_attn_setup()

    def _L1_ffn_setup():
        import jax, jax.numpy as jnp
        import numpy as np
        B, S, D = (4, 256, 128)
        E, H, TOP_K = (8, 256, 2)
        key = jax.random.key(seed)
        k_x, k_g, k_w1, k_w2, k_w3 = jax.random.split(key, 5)
        s_d = 1.0 / np.sqrt(D)
        s_h = 1.0 / np.sqrt(H)
        return {'x': jax.random.normal(k_x, (B, S, D), dtype=jnp.float32), 'w_gate': jax.random.normal(k_g, (D, E), dtype=jnp.float32) * s_d, 'w1': jax.random.normal(k_w1, (E, D, H), dtype=jnp.float32) * s_d, 'w3': jax.random.normal(k_w3, (E, D, H), dtype=jnp.float32) * s_d, 'w2': jax.random.normal(k_w2, (E, H, D), dtype=jnp.float32) * s_h}
    _L1_ffn_in = _L1_ffn_setup()
    _d = {'L0_attn_x': _L0_attn_in['x'], 'L0_attn_fw_Win': _L0_attn_in['fw_Win'], 'L0_attn_fw_convw': _L0_attn_in['fw_convw'], 'L0_attn_fw_convb': _L0_attn_in['fw_convb'], 'L0_attn_fw_Wx': _L0_attn_in['fw_Wx'], 'L0_attn_fw_Wdt': _L0_attn_in['fw_Wdt'], 'L0_attn_fw_bdt': _L0_attn_in['fw_bdt'], 'L0_attn_fw_Alog': _L0_attn_in['fw_Alog'], 'L0_attn_fw_D': _L0_attn_in['fw_D'], 'L0_attn_fw_Wout': _L0_attn_in['fw_Wout'], 'L0_attn_bw_Win': _L0_attn_in['bw_Win'], 'L0_attn_bw_convw': _L0_attn_in['bw_convw'], 'L0_attn_bw_convb': _L0_attn_in['bw_convb'], 'L0_attn_bw_Wx': _L0_attn_in['bw_Wx'], 'L0_attn_bw_Wdt': _L0_attn_in['bw_Wdt'], 'L0_attn_bw_bdt': _L0_attn_in['bw_bdt'], 'L0_attn_bw_Alog': _L0_attn_in['bw_Alog'], 'L0_attn_bw_D': _L0_attn_in['bw_D'], 'L0_attn_bw_Wout': _L0_attn_in['bw_Wout'], 'L0_attn_fwn_w': _L0_attn_in['fwn_w'], 'L0_attn_fwn_b': _L0_attn_in['fwn_b'], 'L0_attn_fin_w': _L0_attn_in['fin_w'], 'L0_attn_fin_b': _L0_attn_in['fin_b'], 'L0_attn_ff_W1': _L0_attn_in['ff_W1'], 'L0_attn_ff_b1': _L0_attn_in['ff_b1'], 'L0_attn_ff_W2': _L0_attn_in['ff_W2'], 'L0_attn_ff_b2': _L0_attn_in['ff_b2'], 'L0_ffn_w1_w': _L0_ffn_in['w1_w'], 'L0_ffn_w1_s': _L0_ffn_in['w1_s'], 'L0_ffn_w2_w': _L0_ffn_in['w2_w'], 'L0_ffn_w2_s': _L0_ffn_in['w2_s'], 'L0_ffn_h1_w': _L0_ffn_in['h1_w'], 'L0_ffn_h1_s': _L0_ffn_in['h1_s'], 'L0_ffn_h2_w': _L0_ffn_in['h2_w'], 'L0_ffn_h2_s': _L0_ffn_in['h2_s'], 'L0_ffn_w3_w': _L0_ffn_in['w3_w'], 'L0_ffn_w3_s': _L0_ffn_in['w3_s'], 'L1_attn_wq': _L1_attn_in['wq'], 'L1_attn_wk_down': _L1_attn_in['wk_down'], 'L1_attn_wv_down': _L1_attn_in['wv_down'], 'L1_attn_wk_up': _L1_attn_in['wk_up'], 'L1_attn_wv_up': _L1_attn_in['wv_up'], 'L1_attn_wo': _L1_attn_in['wo'], 'L1_ffn_w_gate': _L1_ffn_in['w_gate'], 'L1_ffn_w1': _L1_ffn_in['w1'], 'L1_ffn_w3': _L1_ffn_in['w3'], 'L1_ffn_w2': _L1_ffn_in['w2']}
    _x0 = _d['L0_attn_x']
    _d['L0_attn_x'] = jax.random.normal(jax.random.fold_in(jax.random.key(seed), 1), (8, 512, 128), dtype=_x0.dtype)
    del _x0
    return _d

def reference(L0_attn_x, L0_attn_fw_Win, L0_attn_fw_convw, L0_attn_fw_convb, L0_attn_fw_Wx, L0_attn_fw_Wdt, L0_attn_fw_bdt, L0_attn_fw_Alog, L0_attn_fw_D, L0_attn_fw_Wout, L0_attn_bw_Win, L0_attn_bw_convw, L0_attn_bw_convb, L0_attn_bw_Wx, L0_attn_bw_Wdt, L0_attn_bw_bdt, L0_attn_bw_Alog, L0_attn_bw_D, L0_attn_bw_Wout, L0_attn_fwn_w, L0_attn_fwn_b, L0_attn_fin_w, L0_attn_fin_b, L0_attn_ff_W1, L0_attn_ff_b1, L0_attn_ff_W2, L0_attn_ff_b2, L0_ffn_w1_w, L0_ffn_w1_s, L0_ffn_w2_w, L0_ffn_w2_s, L0_ffn_h1_w, L0_ffn_h1_s, L0_ffn_h2_w, L0_ffn_h2_s, L0_ffn_w3_w, L0_ffn_w3_s, L1_attn_wq, L1_attn_wk_down, L1_attn_wv_down, L1_attn_wk_up, L1_attn_wv_up, L1_attn_wo, L1_ffn_w_gate, L1_ffn_w1, L1_ffn_w3, L1_ffn_w2):

    def _L0_attn_ref(x, fw_Win, fw_convw, fw_convb, fw_Wx, fw_Wdt, fw_bdt, fw_Alog, fw_D, fw_Wout, bw_Win, bw_convw, bw_convb, bw_Wx, bw_Wdt, bw_bdt, bw_Alog, bw_D, bw_Wout, fwn_w, fwn_b, fin_w, fin_b, ff_W1, ff_b1, ff_W2, ff_b2):
        import jax, jax.numpy as jnp
        import numpy as np
        from jax import lax
        B, L, D_MODEL = (2, 256, 128)
        EXPAND = 2
        D_INNER = D_MODEL * EXPAND
        D_STATE = 16
        D_CONV = 4
        DT_RANK = (D_MODEL + 15) // 16
        EPS = 1e-05

        def _mamba_params(key, pfx, scale=0.02):
            ks = jax.random.split(key, 6)
            return {pfx + '_Win': jax.random.normal(ks[0], (D_MODEL, 2 * D_INNER), jnp.float32) * scale, pfx + '_convw': jax.random.normal(ks[1], (D_INNER, D_CONV), jnp.float32) * scale, pfx + '_convb': jnp.zeros((D_INNER,), jnp.float32), pfx + '_Wx': jax.random.normal(ks[2], (D_INNER, DT_RANK + 2 * D_STATE), jnp.float32) * scale, pfx + '_Wdt': jax.random.normal(ks[3], (DT_RANK, D_INNER), jnp.float32) * scale, pfx + '_bdt': jax.random.uniform(ks[4], (D_INNER,), jnp.float32, -4.0, -2.0), pfx + '_Alog': jnp.log(jnp.broadcast_to(jnp.arange(1, D_STATE + 1, dtype=jnp.float32), (D_INNER, D_STATE))).copy(), pfx + '_D': jnp.ones((D_INNER,), jnp.float32), pfx + '_Wout': jax.random.normal(ks[5], (D_INNER, D_MODEL), jnp.float32) * scale}

        def _layernorm(x, w, b):
            mu = x.mean(-1, keepdims=True)
            xc = x - mu
            v = (xc * xc).mean(-1, keepdims=True)
            return xc * lax.rsqrt(v + EPS) * w + b

        def _causal_dwconv(x, w, b):
            xc = x.transpose(0, 2, 1)
            out = lax.conv_general_dilated(xc, w[:, None, :], window_strides=(1,), padding=[(D_CONV - 1, 0)], feature_group_count=D_INNER, dimension_numbers=('NCH', 'OIH', 'NCH'))
            return (out + b[None, :, None]).transpose(0, 2, 1)

        def _selective_scan(u, dt, A, Bm, Cm, Dp):
            h0 = jnp.zeros((u.shape[0], D_INNER, D_STATE), u.dtype)

            def step(h, inp):
                u_t, dt_t, B_t, C_t = inp
                dA = jnp.exp(dt_t[:, :, None] * A)
                h = dA * h + (dt_t * u_t)[:, :, None] * B_t[:, None, :]
                y = jnp.einsum('bds,bs->bd', h, C_t)
                return (h, y)
            _, ys = lax.scan(step, h0, (u.transpose(1, 0, 2), dt.transpose(1, 0, 2), Bm.transpose(1, 0, 2), Cm.transpose(1, 0, 2)))
            return ys.transpose(1, 0, 2) + u * Dp

        def _mamba(x, Win, convw, convb, Wx, Wdt, bdt, Alog, Dp, Wout):
            xz = x @ Win
            xi, z = jnp.split(xz, 2, axis=-1)
            xi = jax.nn.silu(_causal_dwconv(xi, convw, convb))
            xdbc = xi @ Wx
            dt_in = xdbc[..., :DT_RANK]
            Bm = xdbc[..., DT_RANK:DT_RANK + D_STATE]
            Cm = xdbc[..., DT_RANK + D_STATE:]
            dt = jax.nn.softplus(dt_in @ Wdt + bdt)
            A = -jnp.exp(Alog)
            y = _selective_scan(xi, dt, A, Bm, Cm, Dp)
            return y * jax.nn.silu(z) @ Wout
        yf = _mamba(x, fw_Win, fw_convw, fw_convb, fw_Wx, fw_Wdt, fw_bdt, fw_Alog, fw_D, fw_Wout)
        yf = _layernorm(yf + x, fwn_w, fwn_b)
        yb = _mamba(jnp.flip(x, 1), bw_Win, bw_convw, bw_convb, bw_Wx, bw_Wdt, bw_bdt, bw_Alog, bw_D, bw_Wout)
        yb = _layernorm(jnp.flip(yb, 1) + x, fwn_w, fwn_b)
        y = yf + yb
        ff = jax.nn.relu(y @ ff_W1 + ff_b1) @ ff_W2 + ff_b2
        return _layernorm(ff + y, fin_w, fin_b)

    def _L0_ffn_ref(x, w1_w, w1_s, w2_w, w2_s, h1_w, h1_s, h2_w, h2_s, w3_w, w3_s):
        import jax, jax.numpy as jnp
        import numpy as np
        D_IN, D_HID = (128, 512)

        def _ternary(key, shape):
            return jax.random.randint(key, shape, -1, 2).astype(jnp.float32)

        def _tlin(x, w, s):
            return jnp.einsum('bsi,oi->bso', x, w) * s
        h = jax.nn.silu(_tlin(x, w1_w, w1_s)) * _tlin(x, w2_w, w2_s)
        h = jax.nn.gelu(_tlin(h, h1_w, h1_s), approximate=False)
        h = jax.nn.gelu(_tlin(h, h2_w, h2_s), approximate=False)
        return _tlin(h, w3_w, w3_s)

    def _L1_attn_ref(x, wq, wk_down, wv_down, wk_up, wv_up, wo):
        import jax, jax.numpy as jnp
        import numpy as np
        D_MODEL, N_HEADS, N_KV, HEAD_DIM, D_LAT = (128, 8, 2, 128, 32)
        N_REP = N_HEADS // N_KV
        B, T = (2, 256)
        Bq, Tq, _ = x.shape
        scale = HEAD_DIM ** (-0.5)
        q = (x @ wq).reshape(Bq, Tq, N_KV, N_REP, HEAD_DIM)
        k_lat = (x @ wk_down).reshape(Bq, Tq, N_KV, D_LAT)
        v_lat = (x @ wv_down).reshape(Bq, Tq, N_KV, D_LAT)
        k = jnp.einsum('bkhl,ld->bkhd', k_lat, wk_up)
        v = jnp.einsum('bkhl,ld->bkhd', v_lat, wv_up)
        scores = jnp.einsum('bqhrd,bkhd->bhrqk', q, k) * scale
        causal = jnp.tril(jnp.ones((Tq, Tq), dtype=bool))
        scores = jnp.where(causal, scores, jnp.finfo(scores.dtype).min)
        probs = jax.nn.softmax(scores, axis=-1)
        y = jnp.einsum('bhrqk,bkhd->bqhrd', probs, v)
        y = y.reshape(Bq, Tq, N_HEADS * HEAD_DIM)
        return y @ wo

    def _L1_ffn_ref(x, w_gate, w1, w3, w2):
        import jax, jax.numpy as jnp
        import numpy as np
        B, S, D = (4, 256, 128)
        E, H, TOP_K = (8, 256, 2)
        bsz, seq_len, embed_dim = x.shape
        xt = x.reshape(-1, embed_dim)
        T = xt.shape[0]
        logits = xt @ w_gate
        top_logits, sel = jax.lax.top_k(logits, TOP_K)
        probs = jax.nn.softmax(top_logits, axis=-1).astype(x.dtype)
        h = jax.nn.silu(jnp.einsum('td,edh->eth', xt, w1)) * jnp.einsum('td,edh->eth', xt, w3)
        y = jnp.einsum('eth,ehd->etd', h, w2)
        t_idx = jnp.arange(T)
        yk = y[sel.T, t_idx[None, :], :]
        out = jnp.einsum('ktd,tk->td', yk, probs)
        return out.reshape(bsz, seq_len, embed_dim)
    x = L0_attn_x
    x = _layernorm(x + _L0_attn_ref(x, L0_attn_fw_Win, L0_attn_fw_convw, L0_attn_fw_convb, L0_attn_fw_Wx, L0_attn_fw_Wdt, L0_attn_fw_bdt, L0_attn_fw_Alog, L0_attn_fw_D, L0_attn_fw_Wout, L0_attn_bw_Win, L0_attn_bw_convw, L0_attn_bw_convb, L0_attn_bw_Wx, L0_attn_bw_Wdt, L0_attn_bw_bdt, L0_attn_bw_Alog, L0_attn_bw_D, L0_attn_bw_Wout, L0_attn_fwn_w, L0_attn_fwn_b, L0_attn_fin_w, L0_attn_fin_b, L0_attn_ff_W1, L0_attn_ff_b1, L0_attn_ff_W2, L0_attn_ff_b2), axis=-1)
    x = _layernorm(x + _L0_ffn_ref(x, L0_ffn_w1_w, L0_ffn_w1_s, L0_ffn_w2_w, L0_ffn_w2_s, L0_ffn_h1_w, L0_ffn_h1_s, L0_ffn_h2_w, L0_ffn_h2_s, L0_ffn_w3_w, L0_ffn_w3_s), axis=-1)
    x = _layernorm(x + _L1_attn_ref(x, L1_attn_wq, L1_attn_wk_down, L1_attn_wv_down, L1_attn_wk_up, L1_attn_wv_up, L1_attn_wo), axis=-1)
    x = _layernorm(x + _L1_ffn_ref(x, L1_ffn_w_gate, L1_ffn_w1, L1_ffn_w3, L1_ffn_w2), axis=-1)
    return x

_drawn_inputs = setup_inputs


def setup_inputs(seed=0):
    import zlib

    import numpy as np

    out = dict(_drawn_inputs(seed))
    spreads = {'L0_attn_fw_convb': (0.0, 0.8),
     'L0_attn_fw_D': (1.0, 0.6),
     'L0_attn_bw_convb': (0.0, 0.663),
     'L0_attn_bw_D': (1.0, 0.6),
     'L0_attn_fwn_w': (1.0, 0.2),
     'L0_attn_fwn_b': (0.0, 0.1),
     'L0_attn_fin_w': (1.0, 0.2),
     'L0_attn_fin_b': (0.0, 0.1),
     'L0_attn_ff_b1': (0.0, 0.285),
     'L0_attn_ff_b2': (0.0, 0.1)}
    factors = {'L0_attn_fw_Win': 8.0,
     'L0_attn_fw_convw': 8.0,
     'L0_attn_fw_Wx': 8.0,
     'L0_attn_fw_Wdt': 8.0,
     'L0_attn_fw_bdt': 8.0,
     'L0_attn_fw_Alog': 8.0,
     'L0_attn_fw_Wout': 8.0,
     'L0_attn_bw_Win': 8.0,
     'L0_attn_bw_convw': 8.0,
     'L0_attn_bw_Wx': 8.0,
     'L0_attn_bw_Wdt': 8.0,
     'L0_attn_bw_bdt': 8.0,
     'L0_attn_bw_Alog': 8.0,
     'L0_attn_bw_Wout': 7.331,
     'L0_ffn_w1_w': 3.619,
     'L0_ffn_w1_s': 4.214,
     'L0_ffn_w2_w': 3.054,
     'L0_ffn_w2_s': 4.246,
     'L0_ffn_h1_w': 3.998,
     'L0_ffn_h1_s': 5.01,
     'L0_ffn_h2_w': 3.897,
     'L0_ffn_h2_s': 4.943,
     'L0_ffn_w3_w': 2.997,
     'L0_ffn_w3_s': 5.079}
    for name, (base, spread) in spreads.items():
        noise = np.random.default_rng([zlib.crc32(name.encode()), seed]).standard_normal(out[name].shape)
        drawn = base * np.exp(spread * noise) if base else spread * noise
        out[name] = jnp.asarray(drawn.astype(out[name].dtype))
    for name, factor in factors.items():
        out[name] = (out[name] * factor).astype(out[name].dtype)
    return out
```

```python
from contextlib import ExitStack

import numpy as np

import concourse.bass as bass
from concourse import mybir

F32 = mybir.dt.float32
BF16 = mybir.dt.bfloat16
U32 = mybir.dt.uint32
ALU = mybir.AluOpType
ACT = mybir.ActivationFunctionType
AX = mybir.AxisListType

P = 128
T = 512
TT = T // P
D = 128
DI = 256
NH = DI // P
S = 16
R = 8
CU = P // S
NJ = 32 // CU
KC = 4
NU = NH * 16
HID = 512
NC = HID // P
HEADS, KV, LAT = 8, 2, 32
REP = HEADS // KV
E, EH = 8, 256
EPS = 1e-5
SMALL = 0.008
MASKED = -3.0e38

C_ID, C_CEN, C_MEAN, C_RED, C_MASK, C_LT, C_SEL = 0, 128, 256, 384, 512, 640, 704
C_END = C_SEL + NJ * P


def constants():
    c = np.zeros((P, C_END), np.float32)
    p = np.arange(P)
    c[:, C_ID:C_ID + P] = np.eye(P)
    c[:, C_CEN:C_CEN + P] = np.eye(P) - 1.0 / P
    c[:, C_MEAN:C_MEAN + P] = 1.0 / P
    for j in range(NJ):
        for part in range(3):
            c[part * 32 + CU * j + p // S, C_SEL + j * P + p] = 1.0
        c[p, C_RED + j * 32 + CU * j + p // S] = 1.0
    c[:, C_MASK:C_MASK + P] = np.where(p[None, :] > p[:, None], MASKED, 0.0)
    c[:, C_LT:C_LT + E * E] = np.tril(np.ones((E, E)), -1).reshape(-1)
    return c


PER = dict(
    x_in=16, stacked=16 * 48, stored=16,
    full=0, dt_full=64, du_full=64, y_red=16, att=32,
    xT=1, xTr=1, xi=4, z=4, conv=2, u=2, dtin=2, brep=2, crep=2, absd=4, rpos=4, expd=4, third=4, logd=4,
    series=4, dt=4, du=4, hi=4, res=4, mid=4, lo=4,
    dA=64, dbu=64, scan=64, hc=64, yskip=4, gated=4, resid=5, sq=6, rstd=6, norm=6,
    y=1, relu=2, x1=1, a1=4, h0=4, g1=4, g2=4,
    qT=2, kT=2, vlat=1, smax=32, pexp=32, rz=32, pn=32, pt=32, yT=2,
    x3=1, lg=1, gmax=1, gexp=1, gates=1, ea=16, eh=16, eo=8, acc=8, mv=1, trs=1, outn=1,
)


def stack_uses():
    uses = [("xT", "xT", 1)]
    for d in range(2):
        uses += [(f"xi{d}{h}", "xi", 2 * d + h + 1) for h in range(NH)]
        uses += [(f"z{d}{h}", "z", 2 * d + h + 1) for h in range(NH)]
    for d in range(2):
        uses += [(f"dtin{d}", "dtin", d + 1), (f"B{d}", "brep", d + 1), (f"C{d}", "crep", d + 1)]
    uses += [(f"dtp{hf}", "rpos", hf + 1) for hf in range(2 * NH)]

    def norm(n):
        return [(f"cen{n}", "norm", n + 1), (f"var{n}", "rstd", n + 1)]

    for d in range(2):
        uses += [(f"mo{d}", "resid", d + 1)] + norm(d)
    uses += [("ff0", "relu", 1), ("ff1", "relu", 2), ("ffo", "resid", 3)] + norm(2) + norm(3)
    for c in range(NC):
        uses += [(f"a{c}", "a1", c + 1), (f"b{c}", "h0", c + 1)]
    uses += [(f"g1_{c}", "g1", c + 1) for c in range(NC)]
    uses += [(f"g2_{c}", "g2", c + 1) for c in range(NC)]
    uses += [("fo", "resid", 4)] + norm(4)
    for k in range(KV):
        uses += [(f"q{k}", "qT", k + 1), (f"k{k}", "kT", k + 1)]
    uses += [("v", "vlat", 1)]
    for i in range(HEADS * TT + 1):
        if i < HEADS * TT:
            uses += [(f"s{i}", "pexp", i + 1)]
        if i >= 1:
            uses += [(f"t{i - 1}", "pt", i)]
    uses += [("ao", "resid", 5)] + norm(5)
    uses += [("x3", "x3", 1), ("lg", "lg", 1)]
    for e in range(E):
        for c in range(2):
            uses += [(f"ea{e}{c}", "ea", 2 * e + c + 1), (f"eb{e}{c}", "eh", 2 * e + c + 1)]
        uses += [(f"eo{e}", "eo", e + 1)]
    return uses


USES = stack_uses()
USE = {name: i for i, (name, _, _) in enumerate(USES)}
PER["full"] = len(USES)
NBANK = 3
STEP2, STEP3 = (4, 6, 8, 10), (20, 22, 24, 26)
ACT_LINKS, DVE_LINKS = 7, 25


def two_layer_kernel(nc, a, out):
    B = a["x"].shape[0]
    with ExitStack() as ctx:
        def sb(name, shape, dt=F32):
            return ctx.enter_context(nc.sbuf_tensor("sb_" + name, shape, dt))

        def psum(name):
            return ctx.enter_context(nc.psum_tensor("ps_" + name, [P, T], F32))

        ps_dt = [psum(f"dt{i}") for i in range(2)]
        ps_du = [psum(f"du{i}") for i in range(2)]
        ps_y = psum("y")
        bank = [psum(f"g{i}") for i in range(NBANK)]

        const = sb("const", [P, C_SEL])
        ident = const[:, C_ID:C_ID + P]
        center = const[:, C_CEN:C_CEN + P]
        mean = const[:, C_MEAN:C_MEAN + P]
        sel = sb("sel", [P, NJ, P], BF16)
        identb = sb("identb", [P, P], BF16)
        maskb = sb("maskb", [P, P], BF16)
        lower = const[:, C_LT:C_LT + E * E].rearrange("p (e j) -> p e j", e=E)
        eps = sb("eps", [P, 1])
        one = sb("one", [P, 1])
        mhalf = sb("mhalf", [P, 1])
        tick = sb("tick", [P, 1])

        win = [sb(f"win{d}", [P, 2 * DI]) for d in range(2)]
        convw = [sb(f"convw{d}", [P, NH, KC]) for d in range(2)]
        cols = [sb(f"cols{d}", [P, 3, NH]) for d in range(2)]
        wx = [sb(f"wx{d}", [P, NH, R + 2 * S]) for d in range(2)]
        wbc = [sb(f"wbc{d}", [P, NH, 2, P]) for d in range(2)]
        wdt = sb("wdt", [32 + R, DI])
        A = [sb(f"A{d}", [P, NU]) for d in range(2)]
        wout = [sb(f"wout{d}", [P, NH, D]) for d in range(2)]
        nrm = sb("nrm", [P, 4])
        fb = sb("fb", [P, 3])
        fwb2 = sb("fwb2", [P, 1])
        ffw1 = sb("ffw1", [P, 2 * D])
        ffw2 = sb("ffw2", [P, 2, D])
        w1T = sb("w1T", [P, HID])
        w2T = sb("w2T", [P, HID])
        h1T = sb("h1T", [P, NC, HID])
        h2T = sb("h2T", [P, NC, HID])
        w3T = sb("w3T", [P, NC, D])
        sc = sb("sc", [P, 4, NC])
        s3 = sb("s3", [P, 1])
        wkd = sb("wkd", [P, KV, LAT])
        wkrep = sb("wkrep", [P, KV, REP, LAT])
        wvd = sb("wvd", [P, KV * LAT])
        wup = sb("wup", [LAT, 2, P])
        wupT = sb("wupT", [P, 2, LAT])
        wqk = sb("wqk", [P, HEADS, LAT])
        wvo = sb("wvo", [P, KV, D])
        wgate = sb("wgate", [P, E])
        ew1 = sb("ew1", [P, E, EH])
        ew3 = sb("ew3", [P, E, EH])
        ew2 = sb("ew2", [P, E, 2, D])

        xtok = sb("xtok", [P, TT, D])
        xT = sb("xT", [P, T])
        xTr = sb("xTr", [P, T])
        xpad = sb("xpad", [P, NH, T + KC - 1])
        u = [sb(f"u{d}", [P, NH, T]) for d in range(2)]
        sz = [sb(f"sz{d}", [P, NH, T]) for d in range(2)]
        dtin = sb("dtin", [32 + R, T])
        brep = [sb(f"brep{d}", [P, T]) for d in range(2)]
        crep = [sb(f"crep{d}", [P, T]) for d in range(2)]
        texp = sb("texp", [P, T])
        tlog = sb("tlog", [P, T])
        tpos = sb("tpos", [P, T])
        tser = sb("tser", [P, T])
        tsel = sb("tsel", [P, T], U32)
        dd = sb("dd", [P, 2, T])
        dres = sb("dres", [P, 2, T])
        parts = sb("parts", [P, 3, 2, T], BF16)
        stk = sb("stk", [P, 2, 2, 4, T], BF16)
        dbu = sb("dbu", [P, 3, T])
        hst = sb("hst", [P, 3, T])
        hc = sb("hc", [P, 8, T])
        yg = sb("yg", [P, T])
        res = sb("res", [P, T])
        sq = sb("sq", [P, T])
        lnv = sb("lnv", [P, T])
        rstd = sb("rstd", [P, T])
        nf = sb("nf", [P, 2, T])
        yy = sb("yy", [P, T])
        hrel = sb("hrel", [P, 2, T])
        xn = sb("xn", [P, 3, T])
        a1 = sb("a1", [P, 2, T])
        h0 = hc[:, 0:4, :]
        g1 = hc[:, 4:8, :]
        qT, kT = g1[:, 0:KV, :], g1[:, KV:2 * KV, :]
        pexp, pn = h0[:, 0:2, :], h0[:, 2:4, :]
        pt, ea = a1, a1
        yT = hrel
        eh = h0.rearrange("p (e c) t -> p e c t", e=2)
        x3 = yy[:].rearrange("p (n d) -> p n d", n=TT)
        gy = nf[:].rearrange("p e (n d) -> p e n d", n=TT)
        acc = res[:].rearrange("p (n d) -> p n d", n=TT)
        gT = u
        rawh1 = hc[:, 0:4, :]
        rawh2 = hc[:, 4:8, :]
        raw = stk[:].rearrange("p a b c t -> p (a b c t)").bitcast(F32)
        raw1 = raw[:, 0:512].rearrange("p (c i) -> p c i", c=NC)
        raw2 = raw[:, 512:1024].rearrange("p (c i) -> p c i", c=NC)
        raw3 = raw[:, 1024:1536]
        wo = raw[:, 1536:2560].rearrange("p (h n) -> p h n", h=HEADS)
        wq = raw[:, 2560:3584]
        wqT = xn[:, 0:2, :].rearrange("p c (h n) -> p (c h) n", h=4)
        alog = [sq[0:NU, 0:P], sq[0:NU, P:2 * P]]
        vlat = sb("vlat", [P, TT, KV * LAT])
        nmax = sb("nmax", [P, HEADS * TT])
        zsum = sb("zsum", [P, HEADS * TT])
        rz = sb("rz", [P, HEADS * TT])
        lg = sb("lg", [P, TT, E])
        lmax = sb("lmax", [P, TT])
        lsh = sb("lsh", [P, TT, E])
        lexp = sb("lexp", [P, TT, E])
        cgt = sq[:, 0:TT * E * E].rearrange("p (n e j) -> p n e j", n=TT, e=E)
        ceq = sq[:, TT * E * E:2 * TT * E * E].rearrange("p (n e j) -> p n e j", n=TT, e=E)
        rank = sb("rank", [P, TT, E])
        gsel = sb("gsel", [P, TT, E])
        gsum = sb("gsum", [P, TT])
        gates = sb("gates", [P, TT, E])
        stats = sb("stats", [P, TT, 6])
        mv = sb("mv", [P, TT, 2])
        lnv4 = sb("lnv4", [P, TT])
        rst4 = sb("rst4", [P, TT])
        otok = lnv[:].rearrange("p (n d) -> p n d", n=TT)

        sem = {n: ctx.enter_context(nc.semaphore(n)) for n in PER}
        w_in = ctx.enter_context(nc.semaphore("w_in"))
        w_tp = ctx.enter_context(nc.semaphore("w_tp"))
        w_cp = ctx.enter_context(nc.semaphore("w_cp"))
        w_set = ctx.enter_context(nc.semaphore("w_set"))
        w_exp = ctx.enter_context(nc.semaphore("w_exp"))
        act_seq = ctx.enter_context(nc.semaphore("act_seq"))
        dve_seq = ctx.enter_context(nc.semaphore("dve_seq"))
        block = ctx.enter_context(nc.Block())

        all_banks = [*ps_dt, *ps_du, ps_y, *bank]

        def use(name):
            return bank[USE[name] % NBANK]

        def first(name):
            return 16 if name in ("x_in", "stacked", "stored") else 1

        def counts(b):
            def row(name, k):
                return b * PER[name] + k + first(name)
            return row

        def chainer(eng, semaphore, b, per):
            n = [0]

            def link(ins):
                n[0] += 1
                assert n[0] <= per
                ins.then_inc(semaphore, 1)
                eng.wait_ge(semaphore, b * per + n[0])
            return link, n

        def turned():
            yield from (("alog", d) for d in range(2))
            yield from (("w1", 0), ("w2", 0))
            yield from (("h1", c) for c in range(NC))
            yield from (("h2", c) for c in range(NC))
            yield from (("w3", 0), ("wq", 0), ("wq", 1), ("wup", 0), ("wqk", 0), ("wvo", 0), ("wvo", 1))

        TURNED = list(turned())
        TURN = {x: i for i, x in enumerate(TURNED)}
        W_LOADS = 55

        @block.sync
        def _(sp):
            loads = [(const[:], a["const"][:, 0:C_SEL]), (raw[:, 3584:4096], a["const"][:, C_SEL:C_END])]
            for d, pre in enumerate(("fw", "bw")):
                loads += [
                    (win[d][:], a[f"{pre}_Win"]),
                    (convw[d][:], a[f"{pre}_convw"].rearrange("(h p) k -> p h k", p=P)),
                    (wx[d][:], a[f"{pre}_Wx"].rearrange("(h p) k -> p h k", p=P)),
                    (wdt[32 * d:32 * d + R, :], a[f"{pre}_Wdt"]),
                    (alog[d], a[f"{pre}_Alog"].rearrange("(g c) s -> g (c s)", c=CU)),
                    (wout[d][:], a[f"{pre}_Wout"].rearrange("(h p) n -> p h n", p=P))]
                loads += [(cols[d][:, i, :], a[f"{pre}_{v}"].rearrange("(h p) -> p h", p=P))
                          for i, v in enumerate(("convb", "bdt", "D"))]
            loads += [(raw1, a["w1_w"].rearrange("(c p) i -> p c i", p=P)),
                      (raw2, a["w2_w"].rearrange("(c p) i -> p c i", p=P)),
                      (rawh1, a["h1_w"].rearrange("(c p) i -> p c i", p=P)),
                      (rawh2, a["h2_w"].rearrange("(c p) i -> p c i", p=P)),
                      (raw3, a["w3_w"]),
                      (wq, a["wq"]), (wup[:, 0, :], a["wk_up"]), (wup[:, 1, :], a["wv_up"]),
                      (wo, a["wo"].rearrange("(h p) n -> p h n", p=P)),
                      (wkd[:], a["wk_down"].rearrange("p (k l) -> p k l", k=KV)),
                      (wvd[:], a["wv_down"]), (wgate[:], a["w_gate"])]
            loads += [(nrm[:, i:i + 1], a[v].rearrange("(p o) -> p o", o=1))
                      for i, v in enumerate(("fwn_w", "fwn_b", "fin_w", "fin_b"))]
            loads += [(fb[:, 0:2], a["ff_b1"].rearrange("(h p) -> p h", p=P)),
                      (fb[:, 2:3], a["ff_b2"].rearrange("(p o) -> p o", o=1)),
                      (ffw1[:], a["ff_W1"]),
                      (ffw2[:], a["ff_W2"].rearrange("(h p) n -> p h n", p=P))]
            loads += [(sc[:, i, :], a[v].rearrange("(c p) -> p c", p=P))
                      for i, v in enumerate(("w1_s", "w2_s", "h1_s", "h2_s"))]
            loads += [(s3[:], a["w3_s"].rearrange("(p o) -> p o", o=1)),
                      (ew1[:], a["ew1"].rearrange("e p h -> p e h")),
                      (ew3[:], a["ew3"].rearrange("e p h -> p e h"))]
            loads += [(ew2[:, e, :, :], a["ew2"][e].rearrange("(c p) n -> p c n", p=P)) for e in range(E)]
            assert len(loads) == W_LOADS, len(loads)
            for name in PER:
                sp.sem_inc(sem[name], first(name))
            with nc.allow_non_contiguous_dma(reason="per-channel vectors, once"):
                for dst, src in loads:
                    sp.dma_start(dst, src).then_inc(w_in, 16)
            with sp.Fori(0, B) as b:
                for hf in range(2 * NH):
                    cut = b * PER["lo"] + hf + 1 + first("lo")
                    spread = b * PER["du_full"] + max(16 * (hf - 1), 0) + first("du_full")
                    sp.compute_val(cut)
                    sp.compute_val(spread)
                    sp.wait_ge(sem["lo"], cut)
                    sp.wait_ge(sem["du_full"], spread)
                    for part in range(3):
                        for q in range(4):
                            sp.dma_start(stk[32 * part:32 * part + 32, hf % 2, :, q, :],
                                         parts[32 * q:32 * q + 32, part, :, :]
                                         ).then_inc(sem["stacked"], 16)

        @block.tensor
        def _(pe):
            pe.wait_ge(w_in, 16 * W_LOADS)
            pe.wait_ge(w_set, 3)
            for i, (kind, c) in enumerate(TURNED):
                o = all_banks[i % 8]
                if i >= 8:
                    pe.wait_ge(w_cp, i - 7)
                if kind == "alog":
                    pe.wait_ge(w_exp, c + 1)
                    ins = pe.transpose(o[:, 0:NU], alog[c], ident[0:NU, 0:NU])
                elif kind in ("w1", "w2"):
                    src = raw1 if kind == "w1" else raw2
                    for k in range(NC):
                        ins = pe.transpose(o[:, k * P:(k + 1) * P], src[:, k, :], ident)
                elif kind in ("h1", "h2"):
                    src = rawh1 if kind == "h1" else rawh2
                    for k in range(NC):
                        ins = pe.transpose(o[:, k * P:(k + 1) * P], src[:, k, c * P:(c + 1) * P], ident)
                elif kind == "w3":
                    for k in range(NC):
                        ins = pe.transpose(o[:, k * P:(k + 1) * P], raw3[:, k * P:(k + 1) * P], ident)
                elif kind == "wq":
                    for k in range(NC):
                        h = 4 * c + k
                        ins = pe.transpose(o[:, k * P:(k + 1) * P], wq[:, h * P:(h + 1) * P], ident)
                elif kind == "wup":
                    for k in range(2):
                        ins = pe.transpose(o[:, k * LAT:(k + 1) * LAT], wup[:, k, :], ident[0:LAT, 0:LAT])
                elif kind == "wqk":
                    pe.wait_ge(w_cp, TURN["wup", 0] + 1)
                    for h in range(HEADS):
                        ins = pe.matmul(o[:, h * LAT:(h + 1) * LAT], wqT[:, h, :], wupT[:, 0, :],
                                        start=True, stop=True)
                elif kind == "wvo":
                    for r in range(REP):
                        ins = pe.matmul(o[LAT * r:LAT * (r + 1), 0:D], wupT[:, 1, :], wo[:, REP * c + r, :],
                                        start=True, stop=True)
                ins.then_inc(w_tp, 1)
            pe.wait_ge(w_cp, len(TURNED))

            with pe.Fori(0, B) as b:
                row = counts(b)

                def claim(name):
                    i = USE[name]
                    if i < NBANK:
                        pe.wait_ge(sem[USES[i - NBANK][1]], row(USES[i - NBANK][1], 0))
                    else:
                        pe.wait_ge(sem[USES[i - NBANK][1]], row(*USES[i - NBANK][1:]))
                    return use(name)

                def done(ins):
                    ins.then_inc(sem["full"], 1)

                def product(name, lhs, rhs, rows=slice(0, P)):
                    o = claim(name)
                    for i, (l, r) in enumerate(zip(lhs, rhs)):
                        ins = pe.matmul(o[rows, :], l, r, start=(i == 0), stop=(i == len(lhs) - 1))
                    done(ins)

                o = claim("xT")
                pe.wait_ge(sem["x_in"], row("x_in", 16))
                for n in range(TT):
                    ins = pe.transpose(o[:, n * P:(n + 1) * P], xtok[:, n, :], ident)
                done(ins)
                for d in range(2):
                    pe.wait_ge(sem["xT" if d == 0 else "xTr"], row("xT" if d == 0 else "xTr", 1))
                    src = xT if d == 0 else xTr
                    for h in range(NH):
                        product(f"xi{d}{h}", [win[d][:, h * P:(h + 1) * P]], [src[:]])
                    for h in range(NH):
                        product(f"z{d}{h}", [win[d][:, DI + h * P:DI + (h + 1) * P]], [src[:]])
                for d in range(2):
                    pe.wait_ge(sem["u"], row("u", d + 1))
                    uu = [u[d][:, h, :] for h in range(NH)]
                    product(f"dtin{d}", [wx[d][:, h, 0:R] for h in range(NH)], uu,
                            slice(32 * d, 32 * d + R))
                    product(f"B{d}", [wbc[d][:, h, 0, :] for h in range(NH)], uu)
                    product(f"C{d}", [wbc[d][:, h, 1, :] for h in range(NH)], uu)

                def dt_product(hf):
                    d, h = divmod(hf, NH)
                    pe.wait_ge(sem["dtin"], row("dtin", d + 1))
                    rows = slice(32 * d, 32 * d + R)
                    product(f"dtp{hf}", [wdt[rows, h * P:(h + 1) * P]], [dtin[rows, :]])

                dt_product(0)
                dt_product(1)

                def spread(n):
                    d, m = divmod(n, NU)
                    half, j, q = m // 16, m % 16 // 4, m % 4
                    if n % 16 == 0:
                        pe.wait_ge(sem["stacked"], row("stacked", 16 * 12 * (n // 16 + 1)))
                    pe.wait_ge(sem["scan"], row("scan", max(n - 1, 0)))
                    pe.matmul(ps_dt[n % 2][:], sel[0:96, j, :], stk[0:96, half, 0, q, :],
                              start=True, stop=True).then_inc(sem["dt_full"], 1)
                    pe.wait_ge(sem["dbu"], row("dbu", max(n - 1, 0)))
                    pe.matmul(ps_du[n % 2][:], sel[0:96, j, :], stk[0:96, half, 1, q, :],
                              start=True, stop=True).then_inc(sem["du_full"], 1)

                def reduce(k):
                    hf, j = divmod(k, 4)
                    if j == 0:
                        if hf == 0:
                            pe.wait_ge(sem["yT"], row("yT", 0))
                        else:
                            pe.wait_ge(sem["yskip"], row("yskip", hf))
                    pe.wait_ge(sem["hc"], row("hc", 4 * k + 4))
                    for q in range(4):
                        red = const[:, C_RED + 32 * j:C_RED + 32 * j + 32]
                        ins = pe.matmul(ps_y[32 * q:32 * q + 32, :], red, hc[:, (4 * k + q) % 8, :],
                                        start=(j == 0), stop=(j == 3))
                    ins.then_inc(sem["y_red"], 1)

                for n in range(2 * NU + 3):
                    if n in (STEP2[0], STEP3[0]):
                        dt_product(2 if n == STEP2[0] else 3)
                    if n < 2 * NU:
                        spread(n)
                    if n >= 6 and (n - 6) % 4 == 0:
                        reduce((n - 6) // 4)

                def norm(n, src_sem, k):
                    pe.wait_ge(sem[src_sem], row(src_sem, k))
                    product(f"cen{n}", [center], [res[:]])
                    pe.wait_ge(sem["sq"], row("sq", n + 1))
                    product(f"var{n}", [mean], [sq[:]])

                for d in range(2):
                    pe.wait_ge(sem["gated"], row("gated", 2 * d + 2))
                    product(f"mo{d}", [wout[d][:, h, :] for h in range(NH)], [gT[d][:, h, :] for h in range(NH)])
                    norm(d, "resid", d + 1)
                pe.wait_ge(sem["y"], row("y", 1))
                for h in range(2):
                    product(f"ff{h}", [ffw1[:, h * P:(h + 1) * P]], [yy[:]])
                pe.wait_ge(sem["relu"], row("relu", 2))
                product("ffo", [ffw2[:, h, :] for h in range(2)], [hrel[:, h, :] for h in range(2)])
                norm(2, "resid", 3)
                pe.wait_ge(sem["x1"], row("x1", 1))
                product("cen3", [center], [res[:]])
                pe.wait_ge(sem["sq"], row("sq", 4))
                product("var3", [mean], [sq[:]])

                pe.wait_ge(sem["norm"], row("norm", 4))
                for c in range(NC):
                    product(f"a{c}", [w1T[:, c * P:(c + 1) * P]], [xn[:, 0, :]])
                    product(f"b{c}", [w2T[:, c * P:(c + 1) * P]], [xn[:, 0, :]])
                for name, src, w in (("g1", "h0", h1T), ("g2", "g1", h2T)):
                    pe.wait_ge(sem[src], row(src, 4))
                    x_in = h0 if name == "g1" else g1
                    for c in range(NC):
                        product(f"{name}_{c}", [w[:, k, c * P:(c + 1) * P] for k in range(NC)],
                                [x_in[:, k, :] for k in range(NC)])
                pe.wait_ge(sem["g2"], row("g2", 4))
                product("fo", [w3T[:, k, :] for k in range(NC)], [h0[:, k, :] for k in range(NC)])
                norm(4, "resid", 4)

                pe.wait_ge(sem["norm"], row("norm", 5))
                for k in range(KV):
                    wqk_k = wqk[:, REP * k:REP * (k + 1), :].rearrange("p r l -> p (r l)")
                    product(f"q{k}", [wqk_k], [xn[:, 1, :]])
                    product(f"k{k}", [wkrep[:, k, :, :].rearrange("p r l -> p (r l)")], [xn[:, 1, :]])
                o = claim("v")
                for n in range(TT):
                    ins = pe.matmul(o[:, n * KV * LAT:(n + 1) * KV * LAT], xn[:, 1, n * P:(n + 1) * P],
                                    wvd[:], start=True, stop=True)
                done(ins)

                def head(i):
                    return i // (REP * TT), i // TT % REP, i % TT

                def scores(i):
                    k, r, t = head(i)
                    o = claim(f"s{i}")
                    if t == 0 and r == 0:
                        pe.wait_ge(sem["qT"], row("qT", k + 1))
                        pe.wait_ge(sem["kT"], row("kT", k + 1))
                    rows = slice(LAT * r, LAT * (r + 1))
                    pe.matmul(o[:, 0:(t + 1) * P], qT[rows, k, t * P:(t + 1) * P], kT[rows, k, 0:(t + 1) * P],
                              start=True, stop=False)
                    done(pe.matmul(o[:, t * P:(t + 1) * P], identb[:], maskb[:], start=False, stop=True))

                def turn(i):
                    t = head(i)[2]
                    o = claim(f"t{i}")
                    pe.wait_ge(sem["pn"], row("pn", i + 1))
                    for j in range(t + 1):
                        ins = pe.transpose(o[:, j * P:(j + 1) * P], pn[:, i % 2, j * P:(j + 1) * P], ident)
                    done(ins)

                def values(i):
                    k, r, t = head(i)
                    if i == 0:
                        pe.wait_ge(sem["yskip"], row("yskip", 4))
                        pe.wait_ge(sem["vlat"], row("vlat", 1))
                    if i == REP * TT:
                        pe.wait_ge(sem["yT"], row("yT", 1))
                    pe.wait_ge(sem["pt"], row("pt", i + 1))
                    for j in range(t + 1):
                        ins = pe.matmul(ps_y[LAT * r:LAT * (r + 1), t * P:(t + 1) * P],
                                        vlat[:, j, k * LAT:(k + 1) * LAT], pt[:, i % 2, j * P:(j + 1) * P],
                                        start=(j == 0), stop=(j == t))
                    ins.then_inc(sem["att"], 1)

                for i in range(HEADS * TT + 2):
                    if i < HEADS * TT:
                        scores(i)
                    if 1 <= i <= HEADS * TT:
                        turn(i - 1)
                    if i >= 2:
                        values(i - 2)
                pe.wait_ge(sem["yT"], row("yT", 2))
                product("ao", [wvo[:, k, :] for k in range(KV)], [yT[:, k, :] for k in range(KV)])
                norm(5, "resid", 5)

                pe.wait_ge(sem["norm"], row("norm", 6))
                o = claim("x3")
                for n in range(TT):
                    ins = pe.transpose(o[:, n * P:(n + 1) * P], xn[:, 2, n * P:(n + 1) * P], ident)
                done(ins)
                o = claim("lg")
                for n in range(TT):
                    ins = pe.matmul(o[:, n * E:(n + 1) * E], xn[:, 2, n * P:(n + 1) * P], wgate[:],
                                    start=True, stop=True)
                done(ins)

                def down(e):
                    o = claim(f"eo{e}")
                    pe.wait_ge(sem["eh"], row("eh", 2 * e + 2))
                    for n in range(TT):
                        for c in range(2):
                            ins = pe.matmul(o[:, n * D:(n + 1) * D], eh[:, e % 2, c, n * P:(n + 1) * P],
                                            ew2[:, e, c, :], start=(c == 0), stop=(c == 1))
                    done(ins)

                for e in range(E):
                    for c in range(2):
                        product(f"ea{e}{c}", [ew1[:, e, c * P:(c + 1) * P]], [xn[:, 2, :]])
                        product(f"eb{e}{c}", [ew3[:, e, c * P:(c + 1) * P]], [xn[:, 2, :]])
                    down(e)

        @block.scalar
        def _(act):
            act.wait_ge(w_in, 16 * W_LOADS)
            for d in range(2):
                act.activation(alog[d], alog[d], ACT.Exp).then_inc(w_exp, 1)
            act.wait_ge(w_set, 3)
            with act.Fori(0, B) as b:
                row = counts(b)
                link, links = chainer(act, act_seq, b, ACT_LINKS)

                def full(name):
                    act.wait_ge(sem["full"], row("full", USE[name] + 1))
                    return use(name)

                act.wait_ge(sem["xT"], row("xT", 0))
                act.dma_start(xtok[:], a["x"][bass.ds(b, 1)].rearrange("o (n p) d -> p (o n) d", p=P)
                              ).then_inc(sem["x_in"], 16)
                act.activation(xT[:], full("xT")[:], ACT.Copy).then_inc(sem["xT"], 1)
                for d in range(2):
                    act.wait_ge(sem["conv"], row("conv", d))
                    for h in range(NH):
                        act.activation(xpad[:, h, KC - 1:], full(f"xi{d}{h}")[:], ACT.Copy
                                       ).then_inc(sem["xi"], 1)
                    for h in range(NH):
                        act.activation(sz[d][:, h, :], full(f"z{d}{h}")[:], ACT.Silu).then_inc(sem["z"], 1)
                    act.wait_ge(sem["conv"], row("conv", d + 1))
                    act.activation(u[d][:], u[d][:], ACT.Silu).then_inc(sem["u"], 1)
                for d in range(2):
                    act.activation(brep[d][:], full(f"B{d}")[:], ACT.Copy).then_inc(sem["brep"], 1)
                    act.activation(crep[d][:], full(f"C{d}")[:], ACT.Copy).then_inc(sem["crep"], 1)

                def dt_step(hf, k):
                    d, h = divmod(hf, NH)
                    if k == 0:
                        act.wait_ge(sem["dt"], row("dt", hf))
                        act.activation(tlog[:], full(f"dtp{hf}")[:], ACT.Abs, bias=cols[d][:, 1, h:h + 1]
                                       ).then_inc(sem["absd"], 1)
                        act.wait_ge(sem["absd"], row("absd", hf + 1))
                        act.activation(texp[:], tlog[:], ACT.Exp, scale=-1.0).then_inc(sem["expd"], 1)
                        act.wait_ge(sem["expd"], row("expd", hf + 1))
                        act.activation(tser[:], texp[:], ACT.Identity, scale=1.0 / 3.0, bias=mhalf[:, 0:1]
                                       ).then_inc(sem["third"], 1)
                        act.activation(tlog[:], texp[:], ACT.Ln, bias=one[:, 0:1]).then_inc(sem["logd"], 1)
                    elif k == 2:
                        act.wait_ge(sem["du"], row("du", hf + 1))
                        act.wait_ge(sem["stacked"], row("stacked", 16 * 12 * hf))
                        act.activation(parts[:, 0, :, :], dd[:], ACT.Copy).then_inc(sem["hi"], 1)
                    elif k == 3:
                        act.wait_ge(sem["res"], row("res", hf + 1))
                        act.activation(parts[:, 1, :, :], dres[:], ACT.Copy).then_inc(sem["mid"], 1)

                for hf in range(2):
                    for k in range(4):
                        dt_step(hf, k)
                for n in range(2 * NU):
                    for hf, steps in ((2, STEP2), (3, STEP3)):
                        if n in steps:
                            dt_step(hf, steps.index(n))
                    d, m = divmod(n, NU)
                    half, j, q = m // 16, m % 16 // 4, m % 4
                    g = (4 * half + q) * NJ + j
                    act.wait_ge(sem["dt_full"], row("dt_full", n + 1))
                    act.activation(ps_dt[n % 2][:], ps_dt[n % 2][:], ACT.Exp, scale=A[d][:, g:g + 1]
                                   ).then_inc(sem["dA"], 1)

                def norm(n):
                    act.activation(sq[:], full(f"cen{n}")[:], ACT.Square).then_inc(sem["sq"], 1)
                    link(act.activation(lnv[:], full(f"var{n}")[:], ACT.Ln, bias=eps[:, 0:1]))
                    act.activation(rstd[:], lnv[:], ACT.Exp, scale=-0.5).then_inc(sem["rstd"], 1)

                norm(0)
                norm(1)
                for h in range(2):
                    act.activation(hrel[:, h, :], full(f"ff{h}")[:], ACT.Relu, bias=fb[:, h:h + 1]
                                   ).then_inc(sem["relu"], 1)
                norm(2)
                norm(3)
                for c in range(NC):
                    if c >= 2:
                        act.wait_ge(sem["h0"], row("h0", c - 1))
                    act.activation(a1[:, c % 2, :], full(f"a{c}")[:], ACT.Silu, scale=sc[:, 0, c:c + 1]
                                   ).then_inc(sem["a1"], 1)
                for c in range(NC):
                    act.activation(g1[:, c, :], full(f"g1_{c}")[:], ACT.Gelu, scale=sc[:, 2, c:c + 1]
                                   ).then_inc(sem["g1"], 1)
                for c in range(NC):
                    act.activation(h0[:, c, :], full(f"g2_{c}")[:], ACT.Gelu, scale=sc[:, 3, c:c + 1]
                                   ).then_inc(sem["g2"], 1)
                norm(4)
                for k in range(KV):
                    act.activation(qT[:, k, :], full(f"q{k}")[:], ACT.Copy, scale=float(D) ** -0.5
                                   ).then_inc(sem["qT"], 1)
                act.activation(vlat[:].rearrange("p n l -> p (n l)"), full("v")[:, 0:TT * KV * LAT], ACT.Copy
                               ).then_inc(sem["vlat"], 1)
                for i in range(HEADS * TT + 1):
                    if i < HEADS * TT:
                        w = (i % TT + 1) * P
                        act.wait_ge(sem["smax"], row("smax", i + 1))
                        if i >= 2:
                            act.wait_ge(sem["pn"], row("pn", i - 1))
                        act.activation(pexp[:, i % 2, 0:w], use(f"s{i}")[:, 0:w], ACT.Exp,
                                       bias=nmax[:, i:i + 1], accum_out=zsum[:, i:i + 1]
                                       ).then_inc(sem["pexp"], 1)
                    if i >= 1:
                        k = i - 1
                        w = (k % TT + 1) * P
                        if k >= 2:
                            act.wait_ge(sem["att"], row("att", k - 1))
                        act.activation(pt[:, k % 2, 0:w], full(f"t{k}")[:, 0:w], ACT.Copy).then_inc(sem["pt"], 1)
                norm(5)
                act.activation(x3.rearrange("p n d -> p (n d)"), full("x3")[:], ACT.Copy).then_inc(sem["x3"], 1)
                act.wait_ge(sem["gmax"], row("gmax", 1))
                act.activation(lexp[:], lsh[:], ACT.Exp).then_inc(sem["gexp"], 1)
                for i in range(2 * E):
                    if i >= 2:
                        act.wait_ge(sem["eh"], row("eh", i - 1))
                    act.activation(ea[:, i % 2, :], full(f"ea{i // 2}{i % 2}")[:], ACT.Silu).then_inc(sem["ea"], 1)
                act.wait_ge(sem["mv"], row("mv", 1))
                link(act.activation(lnv4[:], mv[:, :, 1], ACT.Ln, bias=eps[:, 0:1]))
                act.activation(rst4[:], lnv4[:], ACT.Exp, scale=-0.5).then_inc(sem["trs"], 1)
                act.wait_ge(sem["outn"], row("outn", 1))
                act.dma_start(out[bass.ds(b, 1)].rearrange("o (n p) d -> p (o n) d", p=P), otok
                              ).then_inc(sem["stored"], 16)
            act.wait_ge(sem["stored"], 16 * B + first("stored"))
            assert links[0] == ACT_LINKS, links

        @block.vector
        def _(dve):
            dve.memset(eps[:], EPS)
            dve.memset(mhalf[:], -0.5)
            dve.memset(one[:], 1.0).then_inc(w_set, 1)
            dve.wait_ge(w_in, 16 * W_LOADS)
            dve.tensor_copy(sel[:], raw[:, 3584:4096].rearrange("p (j m) -> p j m", j=NJ))
            dve.tensor_copy(identb[:], ident)
            dve.tensor_copy(maskb[:], const[:, C_MASK:C_MASK + P])
            for d in range(2):
                for w in range(2):
                    cut = wx[d][:, :, R + S * w:R + S * (w + 1)]
                    for h in range(NH):
                        dve.tensor_copy(wbc[d][:, h, w, :].rearrange("p (c s) -> p c s", c=CU),
                                        cut[:, h, :].unsqueeze(1).broadcast_to([P, CU, S]))
            for k in range(KV):
                dve.tensor_copy(wkrep[:, k, :, :], wkd[:, k, :].unsqueeze(1).broadcast_to([P, REP, LAT]))
            dve.tensor_scalar(fwb2[:], nrm[:, 1:2], 2.0, None, ALU.mult).then_inc(w_set, 1)
            for i, (kind, c) in enumerate(TURNED):
                o = all_banks[i % 8]
                dve.wait_ge(w_tp, i + 1)
                if kind == "alog":
                    ins = dve.tensor_scalar(A[c][:], o[:, 0:NU], -1.0, None, ALU.mult)
                else:
                    dst, n = {"w1": (w1T[:], HID), "w2": (w2T[:], HID), "h1": (h1T[:, c, :], HID),
                              "h2": (h2T[:, c, :], HID), "w3": (w3T[:].rearrange("p c n -> p (c n)"), HID),
                              "wq": (wqT[:, 4 * (c % 2):4 * (c % 2) + 4, :].rearrange("p h n -> p (h n)"), HID),
                              "wup": (wupT[:].rearrange("p a n -> p (a n)"), 2 * LAT),
                              "wqk": (wqk[:].rearrange("p h l -> p (h l)"), HEADS * LAT),
                              "wvo": (wvo[:, c % KV, :], D)}[kind]
                    ins = dve.tensor_copy(dst, o[:, 0:n])
                ins.then_inc(w_cp, 1)

            with dve.Fori(0, B) as b:
                row = counts(b)
                link, links = chainer(dve, dve_seq, b, DVE_LINKS)

                def full(name):
                    dve.wait_ge(sem["full"], row("full", USE[name] + 1))
                    return use(name)

                dve.wait_ge(sem["xT"], row("xT", 1))
                dve.tensor_copy(xTr[:, ::-1], xT[:]).then_inc(sem["xTr"], 1)
                for d in range(2):
                    dve.wait_ge(sem["xi"], row("xi", 2 * d + 2))
                    for k in range(KC):
                        for h in range(NH):
                            x_k = xpad[:, h, k:k + T]
                            if k == 0:
                                ins = dve.tensor_scalar(u[d][:, h, :], x_k, convw[d][:, h, 0:1], cols[d][:, 0, h:h + 1],
                                                        ALU.mult, ALU.add)
                            else:
                                ins = dve.scalar_tensor_tensor(u[d][:, h, :], x_k, convw[d][:, h, k:k + 1],
                                                               u[d][:, h, :], ALU.mult, ALU.add)
                        if k < KC - 1:
                            link(ins)
                    ins.then_inc(sem["conv"], 1)
                for d in range(2):
                    dve.tensor_copy(dtin[32 * d:32 * d + R, :], full(f"dtin{d}")[32 * d:32 * d + R, :]).then_inc(sem["dtin"], 1)

                def dt_step(hf, k):
                    d, h = divmod(hf, NH)
                    if k == 0:
                        dve.wait_ge(sem["absd"], row("absd", hf + 1))
                        dve.tensor_scalar(tpos[:], use(f"dtp{hf}")[:], cols[d][:, 1, h:h + 1], 0.0,
                                          ALU.add, ALU.max).then_inc(sem["rpos"], 1)
                        dve.wait_ge(sem["expd"], row("expd", hf + 1))
                        dve.tensor_scalar(tsel[:], texp[:], SMALL, None, ALU.is_gt)
                    elif k == 1:
                        dve.wait_ge(sem["series"], row("series", hf + 1))
                        link(dve.scalar_tensor_tensor(tser[:], tser[:], 1.0, texp[:], ALU.add, ALU.mult))
                        dve.wait_ge(sem["logd"], row("logd", hf + 1))
                        dve.memset(tick[:], 0.0)
                        link(dve.copy_predicated(tser[:], tsel[:], tlog[:]))
                        dve.wait_ge(sem["lo"], row("lo", hf))
                        dve.tensor_tensor(dd[:, 0, :], tser[:], tpos[:], ALU.add).then_inc(sem["dt"], 1)
                        dve.wait_ge(sem["dt"], row("dt", hf + 1))
                        dve.tensor_tensor(dd[:, 1, :], dd[:, 0, :], u[d][:, h, :], ALU.mult
                                          ).then_inc(sem["du"], 1)

                for hf in range(2):
                    for k in range(2):
                        dt_step(hf, k)

                def drive(n):
                    dve.wait_ge(sem["du_full"], row("du_full", n + 1))
                    dve.tensor_tensor(dbu[:, n % 3, :], ps_du[n % 2][:], brep[n // NU][:], ALU.mult
                                      ).then_inc(sem["dbu"], 1)

                def scan(n):
                    dve.wait_ge(sem["dbu"], row("dbu", n + 1))
                    dve.wait_ge(sem["dA"], row("dA", n + 1))
                    dve.wait_ge(sem["hc"], row("hc", max(n - 2, 0)))
                    dve.tensor_tensor_scan(hst[:, n % 3, :], ps_dt[n % 2][:], dbu[:, n % 3, :], 0.0,
                                           ALU.mult, ALU.add).then_inc(sem["scan"], 1)

                def gate(hf):
                    d, h = divmod(hf, NH)
                    dve.wait_ge(sem["y_red"], row("y_red", 4 * hf + 4))
                    dve.scalar_tensor_tensor(yg[:], u[d][:, h, :], cols[d][:, 2, h:h + 1], ps_y[:],
                                             ALU.mult, ALU.add).then_inc(sem["yskip"], 1)
                    dve.wait_ge(sem["yskip"], row("yskip", hf + 1))
                    o = gT[d][:, h, :] if d == 0 else gT[d][:, h, ::-1]
                    dve.tensor_tensor(o, yg[:], sz[d][:, h, :], ALU.mult).then_inc(sem["gated"], 1)

                for n in range(2 * NU + 1):
                    for hf, steps in ((2, STEP2), (3, STEP3)):
                        if n in steps:
                            dt_step(hf, steps.index(n))
                    if n < 2 * NU:
                        drive(n)
                    if n >= 1:
                        scan(n - 1)
                    if n > 16 and n % 16 == 6:
                        gate(n // 16 - 1)
                gate(3)

                def scaled(n, dst):
                    dve.wait_ge(sem["rstd"], row("rstd", n + 1))
                    return dve.tensor_tensor(dst, use(f"cen{n}")[:], rstd[:], ALU.mult).then_inc(sem["norm"], 1)

                for d in range(2):
                    dve.tensor_tensor(res[:], full(f"mo{d}")[:], xT[:], ALU.add).then_inc(sem["resid"], 1)
                    scaled(d, nf[:, d, :])
                dve.wait_ge(sem["norm"], row("norm", 2))
                link(dve.tensor_tensor(nf[:, 0, :], nf[:, 0, :], nf[:, 1, :], ALU.add))
                dve.tensor_scalar(yy[:], nf[:, 0, :], nrm[:, 0:1], fwb2[:, 0:1], ALU.mult, ALU.add
                                  ).then_inc(sem["y"], 1)
                dve.wait_ge(sem["y"], row("y", 1))
                dve.scalar_tensor_tensor(res[:], full("ffo")[:], fb[:, 2:3], yy[:], ALU.add, ALU.add
                                         ).then_inc(sem["resid"], 1)
                scaled(2, nf[:, 0, :])
                dve.wait_ge(sem["norm"], row("norm", 3))
                link(dve.tensor_scalar(nf[:, 1, :], nf[:, 0, :], nrm[:, 2:3], nrm[:, 3:4], ALU.mult, ALU.add))
                dve.tensor_tensor(res[:], nf[:, 1, :], xT[:], ALU.add).then_inc(sem["x1"], 1)
                scaled(3, xn[:, 0, :])
                for c in range(NC):
                    dve.wait_ge(sem["a1"], row("a1", c + 1))
                    dve.scalar_tensor_tensor(h0[:, c, :], full(f"b{c}")[:], sc[:, 1, c:c + 1], a1[:, c % 2, :],
                                             ALU.mult, ALU.mult).then_inc(sem["h0"], 1)
                dve.wait_ge(sem["norm"], row("norm", 4))
                dve.scalar_tensor_tensor(res[:], full("fo")[:], s3[:, 0:1], xn[:, 0, :], ALU.mult, ALU.add
                                         ).then_inc(sem["resid"], 1)
                scaled(4, xn[:, 1, :])
                for k in range(KV):
                    dve.tensor_copy(kT[:, k, :], full(f"k{k}")[:]).then_inc(sem["kT"], 1)
                for i in range(HEADS * TT + 1):
                    if i < HEADS * TT:
                        w = (i % TT + 1) * P
                        dve.tensor_reduce(nmax[:, i:i + 1], full(f"s{i}")[:, 0:w], AX.X, ALU.max, negate=True
                                          ).then_inc(sem["smax"], 1)
                    if i >= 1:
                        dve.wait_ge(sem["pexp"], row("pexp", i))
                        dve.reciprocal(rz[:, i - 1:i], zsum[:, i - 1:i]).then_inc(sem["rz"], 1)
                    if i == REP * TT + 2 or i == HEADS * TT:
                        k = 0 if i < HEADS * TT else 1
                        dve.wait_ge(sem["att"], row("att", REP * TT * (k + 1)))
                        dve.tensor_copy(yT[:, k, :], ps_y[:]).then_inc(sem["yT"], 1)
                dve.wait_ge(sem["norm"], row("norm", 5))
                dve.tensor_tensor(res[:], full("ao")[:], xn[:, 1, :], ALU.add).then_inc(sem["resid"], 1)
                scaled(5, xn[:, 2, :])

                dve.tensor_copy(lg[:].rearrange("p n e -> p (n e)"), full("lg")[:, 0:TT * E]).then_inc(sem["lg"], 1)
                dve.wait_ge(sem["lg"], row("lg", 1))
                l_e = lg[:].unsqueeze(3).broadcast_to([P, TT, E, E])
                l_j = lg[:].unsqueeze(2).broadcast_to([P, TT, E, E])
                link(dve.tensor_reduce(lmax[:], lg[:], AX.X, ALU.max))
                dve.tensor_tensor(lsh[:], lg[:], lmax[:].unsqueeze(2).broadcast_to([P, TT, E]), ALU.subtract
                                  ).then_inc(sem["gmax"], 1)
                dve.tensor_tensor(cgt, l_j, l_e, ALU.is_gt)
                link(dve.tensor_tensor(ceq, l_j, l_e, ALU.is_equal))
                for n in range(TT):
                    ins = dve.tensor_tensor(ceq[:, n, :, :], ceq[:, n, :, :], lower, ALU.mult)
                link(ins)
                link(dve.tensor_tensor(cgt, cgt, ceq, ALU.add))
                link(dve.tensor_reduce(rank[:], cgt, AX.X, ALU.add))
                dve.wait_ge(sem["gexp"], row("gexp", 1))
                link(dve.scalar_tensor_tensor(gsel[:], rank[:], 2.0, lexp[:], ALU.is_lt, ALU.mult))
                link(dve.tensor_reduce(gsum[:], gsel[:], AX.X, ALU.add))
                link(dve.reciprocal(gsum[:], gsum[:]))
                dve.tensor_tensor(gates[:], gsel[:], gsum[:].unsqueeze(2).broadcast_to([P, TT, E]), ALU.mult
                                  ).then_inc(sem["gates"], 1)
                dve.wait_ge(sem["gates"], row("gates", 1))
                for e in range(E):
                    for c in range(2):
                        i = 2 * e + c
                        dve.wait_ge(sem["ea"], row("ea", i + 1))
                        if c == 0 and e >= 2:
                            dve.wait_ge(sem["full"], row("full", USE[f"eo{e - 2}"] + 1))
                        dve.tensor_tensor(eh[:, e % 2, c, :], full(f"eb{e}{c}")[:], ea[:, i % 2, :], ALU.mult
                                          ).then_inc(sem["eh"], 1)
                    if e >= 2:
                        dve.wait_ge(sem["acc"], row("acc", e - 1))
                    gate_e = gates[:, :, e:e + 1].broadcast_to([P, TT, D])
                    dve.tensor_tensor(gy[:, e % 2, :, :], full(f"eo{e}")[:].rearrange("p (n d) -> p n d", n=TT),
                                      gate_e, ALU.mult).then_inc(sem["eo"], 1)
                dve.wait_ge(sem["acc"], row("acc", E))
                for n in range(TT):
                    ins = dve.bn_stats(stats[:, n, :], acc[:, n, :])
                link(ins)
                dve.memset(tick[:], 0.0)
                for n in range(TT):
                    ins = dve.bn_aggr(mv[:, n, :], stats[:, n, :])
                ins.then_inc(sem["mv"], 1)
                dve.wait_ge(sem["stored"], row("stored", 0))
                dve.wait_ge(sem["trs"], row("trs", 1))
                for n in range(TT):
                    ins = dve.tensor_scalar(otok[:, n, :], acc[:, n, :], mv[:, n, 0:1], rst4[:, n:n + 1],
                                            ALU.subtract, ALU.mult)
                ins.then_inc(sem["outn"], 1)
            assert links[0] == DVE_LINKS, links

        @block.gpsimd
        def _(pool):
            pool.memset(xpad[:, :, 0:KC - 1], 0.0).then_inc(w_set, 1)
            with pool.Fori(0, B) as b:
                row = counts(b)

                def dt_step(hf, k):
                    if k == 0:
                        pool.wait_ge(sem["third"], row("third", hf + 1))
                        pool.tensor_tensor(tser[:], tser[:], texp[:], ALU.mult).then_inc(sem["series"], 1)
                    elif k == 2:
                        pool.wait_ge(sem["hi"], row("hi", hf + 1))
                        pool.tensor_tensor(dres[:], dd[:], parts[:, 0, :, :], ALU.subtract
                                           ).then_inc(sem["res"], 1)
                    elif k == 3:
                        pool.wait_ge(sem["mid"], row("mid", hf + 1))
                        pool.tensor_tensor(parts[:, 2, :, :], dres[:], parts[:, 1, :, :], ALU.subtract
                                           ).then_inc(sem["lo"], 1)

                for hf in range(2):
                    for k in range(4):
                        dt_step(hf, k)
                for n in range(2 * NU):
                    for hf, steps in ((2, STEP2), (3, STEP3)):
                        if n in steps:
                            dt_step(hf, steps.index(n))
                    pool.wait_ge(sem["scan"], row("scan", n + 1))
                    pool.wait_ge(sem["y_red"], row("y_red", max((n - 8) // 4 + 1, 0)))
                    pool.tensor_tensor(hc[:, n % 8, :], hst[:, n % 3, :], crep[n // NU][:], ALU.mult
                                       ).then_inc(sem["hc"], 1)
                for i in range(HEADS * TT):
                    w = (i % TT + 1) * P
                    pool.wait_ge(sem["rz"], row("rz", i + 1))
                    if i >= 2:
                        pool.wait_ge(sem["full"], row("full", USE[f"t{i - 2}"] + 1))
                    pool.tensor_tensor(pn[:, i % 2, 0:w], pexp[:, i % 2, 0:w],
                                       rz[:, i:i + 1].broadcast_to([P, w]), ALU.mult).then_inc(sem["pn"], 1)
                for e in range(E):
                    if e == 0:
                        pool.wait_ge(sem["x3"], row("x3", 1))
                    else:
                        pool.wait_ge(sem["acc"], row("acc", e))
                    pool.wait_ge(sem["eo"], row("eo", e + 1))
                    pool.tensor_tensor(acc, gy[:, e % 2, :, :], x3 if e == 0 else acc, ALU.add
                                       ).then_inc(sem["acc"], 1)


_PRE = {"L0_attn_": "", "L0_ffn_": "", "L1_attn_": "", "L1_ffn_": ""}


def _short(name):
    for pre in _PRE:
        if name.startswith(pre):
            short = name[len(pre):]
            return "e" + short if pre == "L1_ffn_" and short in ("w1", "w2", "w3") else short
    return name


def kernel(**inputs):
    import numpy as _np
    import concourse.bacc as _bacc
    from concourse import mybir as _mybir
    from concourse.bass_utils import run_bass_kernel_spmd as _run

    nc = _bacc.Bacc("TRN2", target_bir_lowering=False, num_devices=1)
    arrays, args = {}, {}
    for name, value in list(inputs.items()) + [("const", constants())]:
        v = _np.ascontiguousarray(value)
        key = f"in_{name}_dram"
        arrays[key] = v
        args[_short(name)] = nc.dram_tensor(key, v.shape, _mybir.dt.from_np(v.dtype), kind="ExternalInput").ap()
    shape = inputs["L0_attn_x"].shape
    out = nc.dram_tensor("out_dram", shape, F32, kind="ExternalOutput").ap()
    two_layer_kernel(nc, args, out)
    r = _run(nc, [arrays], core_ids=[0])
    return r.results[0]["out_dram"]
```

```python
from contextlib import ExitStack

import numpy as np

import concourse.bass as bass
from concourse import mybir

F32 = mybir.dt.float32
BF16 = mybir.dt.bfloat16
U32 = mybir.dt.uint32
ALU = mybir.AluOpType
ACT = mybir.ActivationFunctionType
AX = mybir.AxisListType

P = 128
T = 512
TT = T // P
D = 128
DI = 256
NH = DI // P
S = 16
R = 8
CU = P // S
NJ = 32 // CU
KC = 4
NU = NH * 16
HID = 512
NC = HID // P
HEADS, KV, LAT = 8, 2, 32
REP = HEADS // KV
E, EH = 8, 256
EPS = 1e-5
SMALL = 0.008
MASKED = -3.0e38

C_ID, C_CEN, C_MEAN, C_RED, C_MASK, C_LT, C_SEL = 0, 128, 256, 384, 512, 640, 704
C_END = C_SEL + NJ * P


def constants():
    c = np.zeros((P, C_END), np.float32)
    p = np.arange(P)
    c[:, C_ID:C_ID + P] = np.eye(P)
    c[:, C_CEN:C_CEN + P] = np.eye(P) - 1.0 / P
    c[:, C_MEAN:C_MEAN + P] = 1.0 / P
    for j in range(NJ):
        for part in range(3):
            c[part * 32 + CU * j + p // S, C_SEL + j * P + p] = 1.0
        c[p, C_RED + j * 32 + CU * j + p // S] = 1.0
    c[:, C_MASK:C_MASK + P] = np.where(p[None, :] > p[:, None], MASKED, 0.0)
    c[:, C_LT:C_LT + E * E] = np.tril(np.ones((E, E)), -1).reshape(-1)
    return c


PER = dict(
    x_in=16, stacked=16 * 48, stored=16,
    full_m=0, full=0, dt_full=64, du_full=64, y_red=16, att=32,
    xT=1, xTr=1, xkeep=1, xi=4, z=4, conv=2, u=2, dtin=2, brep=2, crep=2, absd=4, rpos=4, expd=4, third=4,
    logd=4, series=4, dt=4, du=4, hi=4, res=4, mid=4, lo=4,
    dA=64, dbu=64, scan=64, hc=64, yskip=4, gated=4, resid=5, sq=6, rstd=6, norm=6,
    y=1, relu=2, x1=1, a1=4, h0=4, g1=4, g2=4,
    qT=2, kT=2, vlat=1, smax=32, pexp=32, rz=32, pn=32, pt=32, yT=2,
    x3=1, lg=1, gmax=1, gexp=1, gates=1, ea=16, eh=16, eo=8, acc=8, mv=1, trs=1, outn=1,
    logv=7, dve_m=14, dve_r=11,
)

PREP, UNITS = 12, 2 * NU
SLOTS = PREP + UNITS + 3
DTP_SLOT = (7, 8, PREP + 10, PREP + 26)
DT_SLOTS = ((7, 8, 9, 10), (PREP + 1, PREP + 2, PREP + 4, PREP + 5), (PREP + 12, PREP + 14, PREP + 16, PREP + 18),
            (PREP + 28, PREP + 30, PREP + 32, PREP + 34))
XKEEP_SLOT = PREP + 44


def mamba_uses():
    uses = [("xT", "xT", 1)]
    for d in range(2):
        uses += [(f"xi{d}{h}", "xi", 2 * d + h + 1) for h in range(NH)]
        uses += [(f"z{d}{h}", "z", 2 * d + h + 1) for h in range(NH)]
    uses += [("dtin0", "dtin", 1), ("B0", "brep", 1), ("C0", "crep", 1), ("dtp0", "rpos", 1)]
    uses += [("dtin1", "dtin", 2), ("B1", "brep", 2), ("C1", "crep", 2)]
    uses += [(f"dtp{hf}", "rpos", hf + 1) for hf in range(1, 2 * NH)]
    return uses


def rest_uses():
    def norm(n):
        return [(f"cen{n}", "norm", n + 1), (f"var{n}", "rstd", n + 1)]

    uses = [("mo0", "resid", 1), ("mo1", "resid", 2), ("cen0", "norm", 1), ("cen1", "norm", 2),
            ("var0", "rstd", 1), ("var1", "rstd", 2)]
    uses += [("ff0", "relu", 1), ("ff1", "relu", 2), ("ffo", "resid", 3)] + norm(2) + norm(3)
    for c in range(0, NC, 2):
        uses += [(f"a{c}", "a1", c + 1), (f"a{c + 1}", "a1", c + 2), (f"b{c}", "h0", c + 1), (f"b{c + 1}", "h0", c + 2)]
    uses += [(f"g1_{c}", "g1", c + 1) for c in range(NC)]
    uses += [(f"g2_{c}", "g2", c + 1) for c in range(NC)]
    uses += [("fo", "resid", 4)] + norm(4)
    for k in range(KV):
        uses += [(f"q{k}", "qT", k + 1), (f"k{k}", "kT", k + 1)]
    uses += [("v", "vlat", 1)]
    for j in range(HEADS * TT + 3):
        if j < HEADS * TT:
            uses += [(f"s{j}", "pexp", j + 1)]
        if 2 <= j < HEADS * TT + 2:
            uses += [(f"t{j - 2}", "pt", j - 1)]
        if j in (3, REP * TT + 3):
            uses += [(f"att{j // (REP * TT)}", "yT", j // (REP * TT) + 1)]
    uses += [("ao", "resid", 5)] + norm(5)
    uses += [("x3", "x3", 1), ("lg", "lg", 1)]
    for e in range(E + 1):
        if e < E:
            uses += [(f"ea{e}{c}", "ea", 2 * e + c + 1) for c in range(2)]
            uses += [(f"eb{e}{c}", "eh", 2 * e + c + 1) for c in range(2)]
        if e >= 1:
            uses += [(f"eo{e - 1}", "eo", e)]
    return uses


def place(uses, bank_of, before):
    placed, last, i = {}, dict(before), 0
    for name, semaphore, count in uses:
        bank = bank_of(i, name)
        placed[name] = (bank, last[bank], i)
        last[bank] = (semaphore, count)
        i += name[:3] != "att"
    return placed, last


def mamba_bank(i, name):
    return "gm" if name[:3] == "dtp" else ("dt0", "dt1", "du")[i % 3]


def rest_bank(i, name):
    if name[:3] == "att":
        return "att"
    if name[0] == "s" or name[0] == "t":
        return "g0" if name[0] == "s" else "g1"
    return ("g0", "g1", "att")[i % 3]


M_USE, M_LAST = place(mamba_uses(), mamba_bank, dict(gm=("rpos", 0), dt0=("scan", 0), dt1=("scan", 0), du=("dbu", 0)))
_, R_LAST = place(rest_uses(), rest_bank, dict(g0=None, g1=None, att=None))
R_USE, _ = place(rest_uses(), rest_bank, {bank: (semaphore, 0) for bank, (semaphore, _) in R_LAST.items()})
PER["full_m"], PER["full"] = len(M_USE), len(R_USE) - 2


def follow():
    rest = [4, 2, 1, 1, 2, 2] + [1] * 4 + [2] * 4 + [4] * 8 + [4, 1, 1, 2, 2, 1]
    rest += [2.2] * (HEADS * TT + 3) + [2, 1, 1, 1] + [2, 2] + [2, 2, 2] * (E - 1) + [2] + [1, 1]
    mamba = [0.5, 0.5, 2, 2, 2, 2, 5, 1, 5, 0.5, 0.5, 0.5] + [0.8] * (SLOTS - PREP)
    assert len(mamba) == SLOTS
    each = (sum(rest) + sum(mamba)) / SLOTS
    steps, done, k = [], 0.0, 0
    for n, m in enumerate(mamba):
        done += m
        steps.append(0)
        while k < len(rest) and (done + rest[k] / 2 <= each * (n + 1) or n == SLOTS - 1):
            done += rest[k]
            k += 1
            steps[-1] += 1
    return steps


FOLLOW = follow()


def side_by_side(mamba, rest):
    for steps in FOLLOW:
        next(mamba)
        for _ in range(steps):
            next(rest)


def alone(steps):
    for _ in steps:
        pass


def two_layer_kernel(nc, a, out):
    B = a["x"].shape[0]
    with ExitStack() as ctx:
        def sb(name, shape, dt=F32):
            return ctx.enter_context(nc.sbuf_tensor("sb_" + name, shape, dt))

        def psum(name):
            return ctx.enter_context(nc.psum_tensor("ps_" + name, [P, T], F32))

        bank = {name: psum(name) for name in ("dt0", "dt1", "du", "gm", "y", "g0", "g1", "att")}
        ps_dt, ps_du, ps_y, ps_att = [bank["dt0"], bank["dt1"]], bank["du"], bank["y"], bank["att"]

        const = sb("const", [P, C_SEL])
        ident = const[:, C_ID:C_ID + P]
        center = const[:, C_CEN:C_CEN + P]
        mean = const[:, C_MEAN:C_MEAN + P]
        sel = sb("sel", [P, NJ, P], BF16)
        identb = sb("identb", [P, P], BF16)
        maskb = sb("maskb", [P, P], BF16)
        lower = const[:, C_LT:C_LT + E * E].rearrange("p (e j) -> p e j", e=E)
        eps = sb("eps", [P, 1])
        one = sb("one", [P, 1])
        mhalf = sb("mhalf", [P, 1])
        tick = sb("tick", [P, 1])

        win = [sb(f"win{d}", [P, 2 * DI]) for d in range(2)]
        convw = [sb(f"convw{d}", [P, NH, KC]) for d in range(2)]
        cols = [sb(f"cols{d}", [P, 3, NH]) for d in range(2)]
        wx = [sb(f"wx{d}", [P, NH, R + 2 * S]) for d in range(2)]
        wbc = [sb(f"wbc{d}", [P, NH, 2, P]) for d in range(2)]
        wdt = sb("wdt", [32 + R, DI])
        A = [sb(f"A{d}", [P, NU]) for d in range(2)]
        wout = [sb(f"wout{d}", [P, NH, D]) for d in range(2)]
        nrm = sb("nrm", [P, 4])
        fb = sb("fb", [P, 3])
        fwb2 = sb("fwb2", [P, 1])
        ffw1 = sb("ffw1", [P, 2 * D])
        ffw2 = sb("ffw2", [P, 2, D])
        w1T = sb("w1T", [P, HID])
        w2T = sb("w2T", [P, HID])
        h1T = sb("h1T", [P, NC, HID])
        h2T = sb("h2T", [P, NC, HID])
        w3T = sb("w3T", [P, NC, D])
        sc = sb("sc", [P, 4, NC])
        s3 = sb("s3", [P, 1])
        wkd = sb("wkd", [P, KV, LAT])
        wkrep = sb("wkrep", [P, KV, REP, LAT])
        wvd = sb("wvd", [P, KV * LAT])
        wup = sb("wup", [LAT, 2, P])
        wupT = sb("wupT", [P, 2, LAT])
        wqk = sb("wqk", [P, HEADS, LAT])
        wvo = sb("wvo", [P, KV, D])
        wgate = sb("wgate", [P, E])
        ew1 = sb("ew1", [P, E, EH])
        ew3 = sb("ew3", [P, E, EH])
        ew2 = sb("ew2", [P, E, 2, D])

        xtok = sb("xtok", [P, TT, D])
        xT = sb("xT", [P, T])
        xTr = sb("xTr", [P, T])
        xkept = sb("xkept", [P, T])
        xpad = sb("xpad", [P, NH, T + KC - 1])
        u = [sb(f"u{d}", [P, NH, T]) for d in range(2)]
        sz = [sb(f"sz{d}", [P, NH, T]) for d in range(2)]
        dtin = sb("dtin", [32 + R, T])
        brep = [sb(f"brep{d}", [P, T]) for d in range(2)]
        crep = [sb(f"crep{d}", [P, T]) for d in range(2)]
        texp = sb("texp", [P, T])
        tlog = sb("tlog", [P, T])
        tpos = sb("tpos", [P, T])
        tser = sb("tser", [P, T])
        tsel = sb("tsel", [P, T], U32)
        dd = sb("dd", [P, 2, T])
        parts = sb("parts", [P, 3, 2, T], BF16)
        stk = sb("stk", [P, 2, 2, 4, T], BF16)
        dbu = sb("dbu", [P, 2, T])
        hst = sb("hst", [P, 3, T])
        hc = sb("hc", [P, 6, T])
        yg = tpos
        res = sb("res", [P, T])
        sq = sb("sq", [P, T])
        lnv = sb("lnv", [P, T])
        rstd = sb("rstd", [P, T])
        nf = sb("nf", [P, 2, T])
        yy = sb("yy", [P, T])
        xn = sb("xn", [P, 2, T])
        a1 = sb("a1", [P, 2, T])
        h0 = sb("h0", [P, NC, T])
        g1 = sb("g1", [P, NC, T])
        qT, kT = g1[:, 0:KV, :], g1[:, KV:2 * KV, :]
        pexp, pn = h0[:, 0:2, :], h0[:, 2:4, :]
        pt, ea = a1, a1
        yT = qT
        hrel = h0[:, 0:2, :]
        eh = h0.rearrange("p (e c) t -> p e c t", e=2)
        x3 = yy[:].rearrange("p (n d) -> p n d", n=TT)
        gy = nf[:].rearrange("p e (n d) -> p e n d", n=TT)
        acc = res[:].rearrange("p (n d) -> p n d", n=TT)
        gT = u
        rawh1, rawh2 = h0[:], g1[:]
        raw = stk[:].rearrange("p a b c t -> p (a b c t)").bitcast(F32)
        raw1 = raw[:, 0:512].rearrange("p (c i) -> p c i", c=NC)
        raw2 = raw[:, 512:1024].rearrange("p (c i) -> p c i", c=NC)
        raw3 = raw[:, 1024:1536]
        wo = raw[:, 1536:2560].rearrange("p (h n) -> p h n", h=HEADS)
        wq = raw[:, 2560:3584]
        wqT = xn[:, 0:2, :].rearrange("p c (h n) -> p (c h) n", h=4)
        alog = [sq[0:NU, 0:P], sq[0:NU, P:2 * P]]
        vlat = sb("vlat", [P, TT, KV * LAT])
        nmax = sb("nmax", [P, HEADS * TT])
        zsum = sb("zsum", [P, HEADS * TT])
        rz = sb("rz", [P, HEADS * TT])
        lg = sb("lg", [P, TT, E])
        lmax = sb("lmax", [P, TT])
        lsh = sb("lsh", [P, TT, E])
        lexp = sb("lexp", [P, TT, E])
        cgt = sq[:, 0:TT * E * E].rearrange("p (n e j) -> p n e j", n=TT, e=E)
        ceq = sq[:, TT * E * E:2 * TT * E * E].rearrange("p (n e j) -> p n e j", n=TT, e=E)
        rank = sb("rank", [P, TT, E])
        gsel = sb("gsel", [P, TT, E])
        gsum = sb("gsum", [P, TT])
        gates = sb("gates", [P, TT, E])
        stats = sb("stats", [P, TT, 6])
        mv = sb("mv", [P, TT, 2])
        lnv4 = sb("lnv4", [P, TT])
        rst4 = sb("rst4", [P, TT])
        otok = lnv[:].rearrange("p (n d) -> p n d", n=TT)

        sem = {n: ctx.enter_context(nc.semaphore(n)) for n in PER}
        w_in = ctx.enter_context(nc.semaphore("w_in"))
        w_tp = ctx.enter_context(nc.semaphore("w_tp"))
        w_cp = ctx.enter_context(nc.semaphore("w_cp"))
        w_set = ctx.enter_context(nc.semaphore("w_set"))
        w_exp = ctx.enter_context(nc.semaphore("w_exp"))
        block = ctx.enter_context(nc.Block())

        all_banks = list(bank.values())

        def use(name):
            return bank[(M_USE if name in M_USE else R_USE)[name][0]]

        def first(name):
            return 16 if name in ("x_in", "stacked", "stored") else 1

        def counts(b, ahead=0):
            def row(name, k):
                return b * PER[name] + (ahead * PER[name] + k + first(name))
            return row

        def x_rows(b, ahead=0):
            return a["x"][ahead:][bass.ds(b, 1)].rearrange("o (n p) d -> p (o n) d", p=P)

        def out_rows(b):
            return out[bass.ds(b, 1)].rearrange("o (n p) d -> p (o n) d", p=P)

        def turned():
            yield from (("alog", d) for d in range(2))
            yield from (("w1", 0), ("w2", 0))
            yield from (("h1", c) for c in range(NC))
            yield from (("h2", c) for c in range(NC))
            yield from (("w3", 0), ("wq", 0), ("wq", 1), ("wup", 0), ("wqk", 0), ("wvo", 0), ("wvo", 1))

        TURNED = list(turned())
        TURN = {x: i for i, x in enumerate(TURNED)}
        W_LOADS = 55

        @block.sync
        def _(sp):
            loads = [(const[:], a["const"][:, 0:C_SEL]), (raw[:, 3584:4096], a["const"][:, C_SEL:C_END])]
            for d, pre in enumerate(("fw", "bw")):
                loads += [
                    (win[d][:], a[f"{pre}_Win"]),
                    (convw[d][:], a[f"{pre}_convw"].rearrange("(h p) k -> p h k", p=P)),
                    (wx[d][:], a[f"{pre}_Wx"].rearrange("(h p) k -> p h k", p=P)),
                    (wdt[32 * d:32 * d + R, :], a[f"{pre}_Wdt"]),
                    (alog[d], a[f"{pre}_Alog"].rearrange("(g c) s -> g (c s)", c=CU)),
                    (wout[d][:], a[f"{pre}_Wout"].rearrange("(h p) n -> p h n", p=P))]
                loads += [(cols[d][:, i, :], a[f"{pre}_{v}"].rearrange("(h p) -> p h", p=P))
                          for i, v in enumerate(("convb", "bdt", "D"))]
            loads += [(raw1, a["w1_w"].rearrange("(c p) i -> p c i", p=P)),
                      (raw2, a["w2_w"].rearrange("(c p) i -> p c i", p=P)),
                      (rawh1, a["h1_w"].rearrange("(c p) i -> p c i", p=P)),
                      (rawh2, a["h2_w"].rearrange("(c p) i -> p c i", p=P)),
                      (raw3, a["w3_w"]),
                      (wq, a["wq"]), (wup[:, 0, :], a["wk_up"]), (wup[:, 1, :], a["wv_up"]),
                      (wo, a["wo"].rearrange("(h p) n -> p h n", p=P)),
                      (wkd[:], a["wk_down"].rearrange("p (k l) -> p k l", k=KV)),
                      (wvd[:], a["wv_down"]), (wgate[:], a["w_gate"])]
            loads += [(nrm[:, i:i + 1], a[v].rearrange("(p o) -> p o", o=1))
                      for i, v in enumerate(("fwn_w", "fwn_b", "fin_w", "fin_b"))]
            loads += [(fb[:, 0:2], a["ff_b1"].rearrange("(h p) -> p h", p=P)),
                      (fb[:, 2:3], a["ff_b2"].rearrange("(p o) -> p o", o=1)),
                      (ffw1[:], a["ff_W1"]),
                      (ffw2[:], a["ff_W2"].rearrange("(h p) n -> p h n", p=P))]
            loads += [(sc[:, i, :], a[v].rearrange("(c p) -> p c", p=P))
                      for i, v in enumerate(("w1_s", "w2_s", "h1_s", "h2_s"))]
            loads += [(s3[:], a["w3_s"].rearrange("(p o) -> p o", o=1)),
                      (ew1[:], a["ew1"].rearrange("e p h -> p e h")),
                      (ew3[:], a["ew3"].rearrange("e p h -> p e h"))]
            loads += [(ew2[:, e, :, :], a["ew2"][e].rearrange("(c p) n -> p c n", p=P)) for e in range(E)]
            assert len(loads) == W_LOADS, len(loads)
            for name in PER:
                sp.sem_inc(sem[name], first(name))
            with nc.allow_non_contiguous_dma(reason="per-channel vectors, once"):
                for dst, src in loads:
                    sp.dma_start(dst, src).then_inc(w_in, 16)
            with sp.Fori(0, B) as b:
                for hf in range(2 * NH):
                    cut = b * PER["lo"] + hf + 1 + first("lo")
                    spread = b * PER["du_full"] + (max(16 * (hf - 1), 0) + first("du_full"))
                    sp.compute_val(cut)
                    sp.compute_val(spread)
                    sp.wait_ge(sem["lo"], cut)
                    sp.wait_ge(sem["du_full"], spread)
                    for part in range(3):
                        for q in range(4):
                            sp.dma_start(stk[32 * part:32 * part + 32, hf % 2, :, q, :],
                                         parts[32 * q:32 * q + 32, part, :, :]
                                         ).then_inc(sem["stacked"], 16)

        @block.tensor
        def _(pe):
            pe.wait_ge(w_in, 16 * W_LOADS)
            pe.wait_ge(w_set, 3)
            for i, (kind, c) in enumerate(TURNED):
                o = all_banks[i % 8]
                if i >= 8:
                    pe.wait_ge(w_cp, i - 7)
                if kind == "alog":
                    pe.wait_ge(w_exp, c + 1)
                    ins = pe.transpose(o[:, 0:NU], alog[c], ident[0:NU, 0:NU])
                elif kind in ("w1", "w2"):
                    src = raw1 if kind == "w1" else raw2
                    for k in range(NC):
                        ins = pe.transpose(o[:, k * P:(k + 1) * P], src[:, k, :], ident)
                elif kind in ("h1", "h2"):
                    src = rawh1 if kind == "h1" else rawh2
                    for k in range(NC):
                        ins = pe.transpose(o[:, k * P:(k + 1) * P], src[:, k, c * P:(c + 1) * P], ident)
                elif kind == "w3":
                    for k in range(NC):
                        ins = pe.transpose(o[:, k * P:(k + 1) * P], raw3[:, k * P:(k + 1) * P], ident)
                elif kind == "wq":
                    for k in range(NC):
                        h = 4 * c + k
                        ins = pe.transpose(o[:, k * P:(k + 1) * P], wq[:, h * P:(h + 1) * P], ident)
                elif kind == "wup":
                    for k in range(2):
                        ins = pe.transpose(o[:, k * LAT:(k + 1) * LAT], wup[:, k, :], ident[0:LAT, 0:LAT])
                elif kind == "wqk":
                    pe.wait_ge(w_cp, TURN["wup", 0] + 1)
                    for h in range(HEADS):
                        ins = pe.matmul(o[:, h * LAT:(h + 1) * LAT], wqT[:, h, :], wupT[:, 0, :],
                                        start=True, stop=True)
                elif kind == "wvo":
                    for r in range(REP):
                        ins = pe.matmul(o[LAT * r:LAT * (r + 1), 0:D], wupT[:, 1, :], wo[:, REP * c + r, :],
                                        start=True, stop=True)
                ins.then_inc(w_tp, 1)
            pe.wait_ge(w_cp, len(TURNED))

            def mamba(row):
                def product(name, lhs, rhs, rows=slice(0, P)):
                    pe.wait_ge(sem[M_USE[name][1][0]], row(*M_USE[name][1]))
                    for i, (l, r) in enumerate(zip(lhs, rhs)):
                        ins = pe.matmul(use(name)[rows, :], l, r, start=(i == 0), stop=(i == len(lhs) - 1))
                    ins.then_inc(sem["full_m"], 1)

                def dt_in(d):
                    product(f"dtin{d}", [wx[d][:, h, 0:R] for h in range(NH)], [u[d][:, h, :] for h in range(NH)],
                            slice(32 * d, 32 * d + R))
                    product(f"B{d}", [wbc[d][:, h, 0, :] for h in range(NH)], [u[d][:, h, :] for h in range(NH)])
                    product(f"C{d}", [wbc[d][:, h, 1, :] for h in range(NH)], [u[d][:, h, :] for h in range(NH)])

                def dt_product(hf):
                    d, h = divmod(hf, NH)
                    pe.wait_ge(sem["dtin"], row("dtin", d + 1))
                    rows = slice(32 * d, 32 * d + R)
                    product(f"dtp{hf}", [wdt[rows, h * P:(h + 1) * P]], [dtin[rows, :]])

                def spread(n):
                    d, m = divmod(n, NU)
                    half, j, q = m // 16, m % 16 // 4, m % 4
                    if n % 16 == 0:
                        pe.wait_ge(sem["stacked"], row("stacked", 16 * 12 * (n // 16 + 1)))
                    if n < 2:
                        pe.wait_ge(sem[M_LAST[f"dt{n}"][0]], row(*M_LAST[f"dt{n}"]))
                    else:
                        pe.wait_ge(sem["scan"], row("scan", n - 1))
                    pe.matmul(ps_dt[n % 2][:], sel[0:96, j, :], stk[0:96, half, 0, q, :],
                              start=True, stop=True).then_inc(sem["dt_full"], 1)
                    if n == 0:
                        pe.wait_ge(sem[M_LAST["du"][0]], row(*M_LAST["du"]))
                    else:
                        pe.wait_ge(sem["dbu"], row("dbu", n))
                    pe.matmul(ps_du[:], sel[0:96, j, :], stk[0:96, half, 1, q, :],
                              start=True, stop=True).then_inc(sem["du_full"], 1)

                def reduce(k):
                    hf, j = divmod(k, 4)
                    if j == 0:
                        pe.wait_ge(sem["yskip"], row("yskip", hf))
                    pe.wait_ge(sem["hc"], row("hc", 4 * k + 4))
                    for q in range(4):
                        red = const[:, C_RED + 32 * j:C_RED + 32 * j + 32]
                        ins = pe.matmul(ps_y[32 * q:32 * q + 32, :], red, hc[:, (4 * k + q) % 6, :],
                                        start=(j == 0), stop=(j == 3))
                    ins.then_inc(sem["y_red"], 1)

                for slot in range(SLOTS):
                    if slot == 1:
                        pe.wait_ge(sem[M_USE["xT"][1][0]], row(*M_USE["xT"][1]))
                        pe.wait_ge(sem["x_in"], row("x_in", 16))
                        for n in range(TT):
                            ins = pe.transpose(use("xT")[:, n * P:(n + 1) * P], xtok[:, n, :], ident)
                        ins.then_inc(sem["full_m"], 1)
                    elif slot in (2, 4):
                        d = slot // 2 - 1
                        pe.wait_ge(sem["xT"], row("xT", 1))
                        pe.wait_ge(sem["xTr"], row("xTr", 1))
                        for h in range(NH):
                            product(f"xi{d}{h}", [win[d][:, h * P:(h + 1) * P]], [(xT, xTr)[d][:]])
                    elif slot in (3, 5):
                        d = slot // 2 - 1
                        for h in range(NH):
                            product(f"z{d}{h}", [win[d][:, DI + h * P:DI + (h + 1) * P]], [(xT, xTr)[d][:]])
                    elif slot in (6, 8):
                        d = slot // 2 - 3
                        pe.wait_ge(sem["u"], row("u", d + 1))
                        dt_in(d)
                    for hf in range(2 * NH):
                        if slot == DTP_SLOT[hf]:
                            dt_product(hf)
                    n = slot - PREP
                    if 0 <= n < UNITS:
                        spread(n)
                    if n >= 6 and (n - 6) % 4 == 0:
                        reduce((n - 6) // 4)
                    yield

            def rest(row):
                def claim(name):
                    pe.wait_ge(sem[R_USE[name][1][0]], row(*R_USE[name][1]))
                    return use(name)

                def done(ins):
                    ins.then_inc(sem["full"], 1)

                def product(name, lhs, rhs):
                    o = claim(name)
                    for i, (l, r) in enumerate(zip(lhs, rhs)):
                        ins = pe.matmul(o[:], l, r, start=(i == 0), stop=(i == len(lhs) - 1))
                    done(ins)

                pe.wait_ge(sem["gated"], row("gated", 4))
                for d in range(2):
                    product(f"mo{d}", [wout[d][:, h, :] for h in range(NH)], [gT[d][:, h, :] for h in range(NH)])
                yield
                for d in range(2):
                    pe.wait_ge(sem["resid"], row("resid", d + 1))
                    product(f"cen{d}", [center], [nf[:, d, :]])
                yield
                for d in range(2):
                    pe.wait_ge(sem["sq"], row("sq", d + 1))
                    product(f"var{d}", [mean], [sq[:]])
                    yield

                def norm(n, src_sem, k):
                    pe.wait_ge(sem[src_sem], row(src_sem, k))
                    product(f"cen{n}", [center], [res[:]])
                    yield
                    pe.wait_ge(sem["sq"], row("sq", n + 1))
                    product(f"var{n}", [mean], [sq[:]])
                    yield

                pe.wait_ge(sem["y"], row("y", 1))
                for h in range(2):
                    product(f"ff{h}", [ffw1[:, h * P:(h + 1) * P]], [yy[:]])
                yield
                pe.wait_ge(sem["relu"], row("relu", 2))
                product("ffo", [ffw2[:, h, :] for h in range(2)], [hrel[:, h, :] for h in range(2)])
                yield
                yield from norm(2, "resid", 3)
                yield from norm(3, "x1", 1)

                pe.wait_ge(sem["norm"], row("norm", 4))
                for c in range(0, NC, 2):
                    for name, w in (("a", w1T), ("b", w2T)):
                        for cc in (c, c + 1):
                            product(f"{name}{cc}", [w[:, cc * P:(cc + 1) * P]], [xn[:, 0, :]])
                        yield
                for name, src, w in (("g1", "h0", h1T), ("g2", "g1", h2T)):
                    pe.wait_ge(sem[src], row(src, 4))
                    x_in = h0 if name == "g1" else g1
                    for c in range(NC):
                        product(f"{name}_{c}", [w[:, k, c * P:(c + 1) * P] for k in range(NC)],
                                [x_in[:, k, :] for k in range(NC)])
                        yield
                pe.wait_ge(sem["g2"], row("g2", 4))
                product("fo", [w3T[:, k, :] for k in range(NC)], [h0[:, k, :] for k in range(NC)])
                yield
                yield from norm(4, "resid", 4)

                pe.wait_ge(sem["norm"], row("norm", 5))
                for k in range(KV):
                    wqk_k = wqk[:, REP * k:REP * (k + 1), :].rearrange("p r l -> p (r l)")
                    product(f"q{k}", [wqk_k], [xn[:, 1, :]])
                    product(f"k{k}", [wkrep[:, k, :, :].rearrange("p r l -> p (r l)")], [xn[:, 1, :]])
                    yield
                o = claim("v")
                for n in range(TT):
                    ins = pe.matmul(o[:, n * KV * LAT:(n + 1) * KV * LAT], xn[:, 1, n * P:(n + 1) * P],
                                    wvd[:], start=True, stop=True)
                done(ins)
                yield

                def head(i):
                    return i // (REP * TT), i // TT % REP, i % TT

                def scores(i):
                    k, r, t = head(i)
                    o = claim(f"s{i}")
                    if t == 0 and r == 0:
                        pe.wait_ge(sem["qT"], row("qT", k + 1))
                        pe.wait_ge(sem["kT"], row("kT", k + 1))
                    rows = slice(LAT * r, LAT * (r + 1))
                    pe.matmul(o[:, 0:(t + 1) * P], qT[rows, k, t * P:(t + 1) * P], kT[rows, k, 0:(t + 1) * P],
                              start=True, stop=False)
                    done(pe.matmul(o[:, t * P:(t + 1) * P], identb[:], maskb[:], start=False, stop=True))

                def turn(i):
                    t = head(i)[2]
                    o = claim(f"t{i}")
                    pe.wait_ge(sem["pn"], row("pn", i + 1))
                    for j in range(t + 1):
                        ins = pe.transpose(o[:, j * P:(j + 1) * P], pn[:, i % 2, j * P:(j + 1) * P], ident)
                    done(ins)

                def values(i):
                    k, r, t = head(i)
                    if i == REP * TT * k:
                        claim(f"att{k}")
                        pe.wait_ge(sem["vlat"], row("vlat", 1))
                    pe.wait_ge(sem["pt"], row("pt", i + 1))
                    for j in range(t + 1):
                        ins = pe.matmul(ps_att[LAT * r:LAT * (r + 1), t * P:(t + 1) * P],
                                        vlat[:, j, k * LAT:(k + 1) * LAT], pt[:, i % 2, j * P:(j + 1) * P],
                                        start=(j == 0), stop=(j == t))
                    ins.then_inc(sem["att"], 1)

                for j in range(HEADS * TT + 3):
                    if j < HEADS * TT:
                        scores(j)
                    if 2 <= j < HEADS * TT + 2:
                        turn(j - 2)
                    if j >= 3:
                        values(j - 3)
                    yield
                pe.wait_ge(sem["yT"], row("yT", 2))
                product("ao", [wvo[:, k, :] for k in range(KV)], [yT[:, k, :] for k in range(KV)])
                yield
                yield from norm(5, "resid", 5)

                pe.wait_ge(sem["norm"], row("norm", 6))
                o = claim("x3")
                for n in range(TT):
                    ins = pe.transpose(o[:, n * P:(n + 1) * P], xn[:, 0, n * P:(n + 1) * P], ident)
                done(ins)
                o = claim("lg")
                for n in range(TT):
                    ins = pe.matmul(o[:, n * E:(n + 1) * E], xn[:, 0, n * P:(n + 1) * P], wgate[:],
                                    start=True, stop=True)
                done(ins)
                yield

                def down(e):
                    o = claim(f"eo{e}")
                    pe.wait_ge(sem["eh"], row("eh", 2 * e + 2))
                    for n in range(TT):
                        for c in range(2):
                            ins = pe.matmul(o[:, n * D:(n + 1) * D], eh[:, e % 2, c, n * P:(n + 1) * P],
                                            ew2[:, e, c, :], start=(c == 0), stop=(c == 1))
                    done(ins)

                for e in range(E + 1):
                    if e < E:
                        for name, w in (("ea", ew1), ("eb", ew3)):
                            for c in range(2):
                                product(f"{name}{e}{c}", [w[:, e, c * P:(c + 1) * P]], [xn[:, 0, :]])
                            yield
                    if e >= 1:
                        down(e - 1)
                        yield
                yield
                yield

            alone(mamba(counts(0)))
            with pe.Fori(0, B - 1) as b:
                side_by_side(mamba(counts(b, 1)), rest(counts(b)))
            alone(rest(counts(B - 1)))

        @block.scalar
        def _(act):
            act.wait_ge(w_in, 16 * W_LOADS)
            for d in range(2):
                act.activation(alog[d], alog[d], ACT.Exp).then_inc(w_exp, 1)
            act.wait_ge(w_set, 3)
            def mamba(row, x_row):
                def full(name):
                    act.wait_ge(sem["full_m"], row("full_m", M_USE[name][2] + 1))
                    return use(name)

                def dt_step(hf, k):
                    d, h = divmod(hf, NH)
                    if k == 0:
                        act.wait_ge(sem["dt"], row("dt", hf))
                        act.activation(tlog[:], full(f"dtp{hf}")[:], ACT.Abs, bias=cols[d][:, 1, h:h + 1]
                                       ).then_inc(sem["absd"], 1)
                        act.wait_ge(sem["absd"], row("absd", hf + 1))
                        act.activation(texp[:], tlog[:], ACT.Exp, scale=-1.0).then_inc(sem["expd"], 1)
                        act.wait_ge(sem["expd"], row("expd", hf + 1))
                        act.activation(tser[:], texp[:], ACT.Identity, scale=1.0 / 3.0, bias=mhalf[:, 0:1]
                                       ).then_inc(sem["third"], 1)
                        act.activation(tlog[:], texp[:], ACT.Ln, bias=one[:, 0:1]).then_inc(sem["logd"], 1)
                    elif k == 2:
                        act.wait_ge(sem["du"], row("du", hf + 1))
                        act.wait_ge(sem["stacked"], row("stacked", 16 * 12 * hf))
                        act.activation(parts[:, 0, :, :], dd[:], ACT.Copy).then_inc(sem["hi"], 1)
                    elif k == 3:
                        act.wait_ge(sem["res"], row("res", hf + 1))
                        act.activation(parts[:, 1, :, :], dd[:], ACT.Copy).then_inc(sem["mid"], 1)

                for slot in range(SLOTS):
                    if slot == 0:
                        act.wait_ge(sem["xT"], row("xT", 0))
                        act.dma_start(xtok[:], x_row).then_inc(sem["x_in"], 16)
                    elif slot == 1:
                        act.activation(xT[:], full("xT")[:], ACT.Copy).then_inc(sem["xT"], 1)
                    elif slot in (2, 4):
                        d = slot // 2 - 1
                        act.wait_ge(sem["conv"], row("conv", d))
                        for h in range(NH):
                            act.activation(xpad[:, h, KC - 1:], full(f"xi{d}{h}")[:], ACT.Copy
                                           ).then_inc(sem["xi"], 1)
                    elif slot in (3, 5):
                        d = slot // 2 - 1
                        act.wait_ge(sem["gated"], row("gated", 0))
                        for h in range(NH):
                            act.activation(sz[d][:, h, :], full(f"z{d}{h}")[:], ACT.Silu).then_inc(sem["z"], 1)
                        act.wait_ge(sem["conv"], row("conv", d + 1))
                        act.activation(u[d][:], u[d][:], ACT.Silu).then_inc(sem["u"], 1)
                    elif slot in (6, 8):
                        d = slot // 2 - 3
                        act.wait_ge(sem["hc"], row("hc", 0))
                        act.activation(brep[d][:], full(f"B{d}")[:], ACT.Copy).then_inc(sem["brep"], 1)
                        act.activation(crep[d][:], full(f"C{d}")[:], ACT.Copy).then_inc(sem["crep"], 1)
                    for hf in range(2 * NH):
                        if slot in DT_SLOTS[hf]:
                            dt_step(hf, DT_SLOTS[hf].index(slot))
                    n = slot - PREP
                    if 0 <= n < UNITS:
                        d, m = divmod(n, NU)
                        half, j, q = m // 16, m % 16 // 4, m % 4
                        g = (4 * half + q) * NJ + j
                        act.wait_ge(sem["dt_full"], row("dt_full", n + 1))
                        act.activation(ps_dt[n % 2][:], ps_dt[n % 2][:], ACT.Exp, scale=A[d][:, g:g + 1]
                                       ).then_inc(sem["dA"], 1)
                    if slot == XKEEP_SLOT:
                        act.wait_ge(sem["x1"], row("x1", 0))
                        act.activation(xkept[:], xT[:], ACT.Copy).then_inc(sem["xkeep"], 1)
                    yield

            def rest(row, out_row):
                def full(name):
                    act.wait_ge(sem["full"], row("full", R_USE[name][2] + 1))
                    return use(name)

                def square(n):
                    act.activation(sq[:], full(f"cen{n}")[:], ACT.Square).then_inc(sem["sq"], 1)

                def root(n):
                    act.activation(lnv[:], full(f"var{n}")[:], ACT.Ln, bias=eps[:, 0:1]).then_inc(sem["logv"], 1)
                    act.wait_ge(sem["norm"], row("norm", n))
                    act.wait_ge(sem["logv"], row("logv", n + 1))
                    act.activation(rstd[:], lnv[:], ACT.Exp, scale=-0.5).then_inc(sem["rstd"], 1)

                yield
                act.wait_ge(sem["stored"], row("stored", 0))
                square(0)
                yield
                root(0)
                square(1)
                yield
                root(1)
                yield
                for h in range(2):
                    act.activation(hrel[:, h, :], full(f"ff{h}")[:], ACT.Relu, bias=fb[:, h:h + 1]
                                   ).then_inc(sem["relu"], 1)
                yield
                yield
                for n in (2, 3):
                    square(n)
                    yield
                    root(n)
                    yield
                for c in range(0, NC, 2):
                    for cc in (c, c + 1):
                        act.wait_ge(sem["h0"], row("h0", max(cc - 1, 0)))
                        act.activation(a1[:, cc % 2, :], full(f"a{cc}")[:], ACT.Silu, scale=sc[:, 0, cc:cc + 1]
                                       ).then_inc(sem["a1"], 1)
                    yield
                    yield
                for name, dst, i in (("g1", g1, 2), ("g2", h0, 3)):
                    for c in range(0, NC, 2):
                        yield
                        for cc in (c, c + 1):
                            act.activation(dst[:, cc, :], full(f"{name}_{cc}")[:], ACT.Gelu, scale=sc[:, i, cc:cc + 1]
                                           ).then_inc(sem[name], 1)
                        yield
                yield
                square(4)
                yield
                root(4)
                yield
                for k in range(KV):
                    act.activation(qT[:, k, :], full(f"q{k}")[:], ACT.Copy, scale=float(D) ** -0.5
                                   ).then_inc(sem["qT"], 1)
                    yield
                act.activation(vlat[:].rearrange("p n l -> p (n l)"), full("v")[:, 0:TT * KV * LAT], ACT.Copy
                               ).then_inc(sem["vlat"], 1)
                yield
                for j in range(HEADS * TT + 3):
                    if j < HEADS * TT:
                        w = (j % TT + 1) * P
                        act.wait_ge(sem["smax"], row("smax", j + 1))
                        if j >= 2:
                            act.wait_ge(sem["pn"], row("pn", j - 1))
                        act.activation(pexp[:, j % 2, 0:w], use(f"s{j}")[:, 0:w], ACT.Exp,
                                       bias=nmax[:, j:j + 1], accum_out=zsum[:, j:j + 1]
                                       ).then_inc(sem["pexp"], 1)
                    if 2 <= j < HEADS * TT + 2:
                        k = j - 2
                        w = (k % TT + 1) * P
                        if k >= 2:
                            act.wait_ge(sem["att"], row("att", k - 1))
                        act.activation(pt[:, k % 2, 0:w], full(f"t{k}")[:, 0:w], ACT.Copy).then_inc(sem["pt"], 1)
                    yield
                yield
                square(5)
                yield
                root(5)
                yield
                act.activation(x3.rearrange("p n d -> p (n d)"), full("x3")[:], ACT.Copy).then_inc(sem["x3"], 1)
                act.wait_ge(sem["gmax"], row("gmax", 1))
                act.activation(lexp[:], lsh[:], ACT.Exp).then_inc(sem["gexp"], 1)
                yield
                for e in range(E + 1):
                    if e < E:
                        for i in (2 * e, 2 * e + 1):
                            if i >= 2:
                                act.wait_ge(sem["eh"], row("eh", i - 1))
                            act.activation(ea[:, i % 2, :], full(f"ea{e}{i % 2}")[:], ACT.Silu).then_inc(sem["ea"], 1)
                        yield
                        yield
                    if e >= 1:
                        yield
                act.wait_ge(sem["mv"], row("mv", 1))
                act.activation(lnv4[:], mv[:, :, 1], ACT.Ln, bias=eps[:, 0:1]).then_inc(sem["logv"], 1)
                act.wait_ge(sem["logv"], row("logv", 7))
                act.activation(rst4[:], lnv4[:], ACT.Exp, scale=-0.5).then_inc(sem["trs"], 1)
                yield
                act.wait_ge(sem["outn"], row("outn", 1))
                act.dma_start(out_row, otok).then_inc(sem["stored"], 16)
                yield

            alone(mamba(counts(0), x_rows(0)))
            with act.Fori(0, B - 1) as b:
                side_by_side(mamba(counts(b, 1), x_rows(b, 1)), rest(counts(b), out_rows(b)))
            alone(rest(counts(B - 1), out_rows(B - 1)))
            act.wait_ge(sem["stored"], 16 * B + first("stored"))


        @block.vector
        def _(dve):
            dve.memset(eps[:], EPS)
            dve.memset(mhalf[:], -0.5)
            dve.memset(one[:], 1.0).then_inc(w_set, 1)
            dve.wait_ge(w_in, 16 * W_LOADS)
            dve.tensor_copy(sel[:], raw[:, 3584:4096].rearrange("p (j m) -> p j m", j=NJ))
            dve.tensor_copy(identb[:], ident)
            dve.tensor_copy(maskb[:], const[:, C_MASK:C_MASK + P])
            for d in range(2):
                for w in range(2):
                    cut = wx[d][:, :, R + S * w:R + S * (w + 1)]
                    for h in range(NH):
                        dve.tensor_copy(wbc[d][:, h, w, :].rearrange("p (c s) -> p c s", c=CU),
                                        cut[:, h, :].unsqueeze(1).broadcast_to([P, CU, S]))
            for k in range(KV):
                dve.tensor_copy(wkrep[:, k, :, :], wkd[:, k, :].unsqueeze(1).broadcast_to([P, REP, LAT]))
            dve.tensor_scalar(fwb2[:], nrm[:, 1:2], 2.0, None, ALU.mult).then_inc(w_set, 1)
            for i, (kind, c) in enumerate(TURNED):
                o = all_banks[i % 8]
                dve.wait_ge(w_tp, i + 1)
                if kind == "alog":
                    ins = dve.tensor_scalar(A[c][:], o[:, 0:NU], -1.0, None, ALU.mult)
                else:
                    dst, n = {"w1": (w1T[:], HID), "w2": (w2T[:], HID), "h1": (h1T[:, c, :], HID),
                              "h2": (h2T[:, c, :], HID), "w3": (w3T[:].rearrange("p c n -> p (c n)"), HID),
                              "wq": (wqT[:, 4 * (c % 2):4 * (c % 2) + 4, :].rearrange("p h n -> p (h n)"), HID),
                              "wup": (wupT[:].rearrange("p a n -> p (a n)"), 2 * LAT),
                              "wqk": (wqk[:].rearrange("p h l -> p (h l)"), HEADS * LAT),
                              "wvo": (wvo[:, c % KV, :], D)}[kind]
                    ins = dve.tensor_copy(dst, o[:, 0:n])
                ins.then_inc(w_cp, 1)

            def mamba(row, before=None):
                def full(name):
                    dve.wait_ge(sem["full_m"], row("full_m", M_USE[name][2] + 1))
                    return use(name)

                links = [0]

                def link(ins):
                    links[0] += 1
                    ins.then_inc(sem["dve_m"], 1)
                    dve.wait_ge(sem["dve_m"], row("dve_m", links[0]))

                def dt_step(hf, k):
                    d, h = divmod(hf, NH)
                    if k == 0:
                        dve.wait_ge(sem["absd"], row("absd", hf + 1))
                        dve.tensor_scalar(tpos[:], use(f"dtp{hf}")[:], cols[d][:, 1, h:h + 1], 0.0,
                                          ALU.add, ALU.max).then_inc(sem["rpos"], 1)
                        dve.wait_ge(sem["expd"], row("expd", hf + 1))
                        dve.tensor_scalar(tsel[:], texp[:], SMALL, None, ALU.is_gt)
                    elif k == 1:
                        dve.wait_ge(sem["series"], row("series", hf + 1))
                        link(dve.scalar_tensor_tensor(tser[:], tser[:], 1.0, texp[:], ALU.add, ALU.mult))
                        dve.wait_ge(sem["logd"], row("logd", hf + 1))
                        dve.memset(tick[:], 0.0)
                        link(dve.copy_predicated(tser[:], tsel[:], tlog[:]))
                        dve.wait_ge(sem["lo"], row("lo", hf))
                        dve.tensor_tensor(dd[:, 0, :], tser[:], tpos[:], ALU.add).then_inc(sem["dt"], 1)
                        dve.wait_ge(sem["dt"], row("dt", hf + 1))
                        dve.tensor_tensor(dd[:, 1, :], dd[:, 0, :], u[d][:, h, :], ALU.mult
                                          ).then_inc(sem["du"], 1)

                def drive(n):
                    dve.wait_ge(sem["du_full"], row("du_full", n + 1))
                    dve.tensor_tensor(dbu[:, n % 2, :], ps_du[:], brep[n // NU][:], ALU.mult
                                      ).then_inc(sem["dbu"], 1)

                def scan(n):
                    dve.wait_ge(sem["dbu"], row("dbu", n + 1))
                    dve.wait_ge(sem["dA"], row("dA", n + 1))
                    dve.wait_ge(sem["hc"], row("hc", max(n - 2, 0)))
                    dve.tensor_tensor_scan(hst[:, n % 3, :], ps_dt[n % 2][:], dbu[:, n % 2, :], 0.0,
                                           ALU.mult, ALU.add).then_inc(sem["scan"], 1)

                def gate(hf):
                    d, h = divmod(hf, NH)
                    dve.wait_ge(sem["y_red"], row("y_red", 4 * hf + 4))
                    dve.scalar_tensor_tensor(yg[:], u[d][:, h, :], cols[d][:, 2, h:h + 1], ps_y[:],
                                             ALU.mult, ALU.add).then_inc(sem["yskip"], 1)
                    dve.wait_ge(sem["yskip"], row("yskip", hf + 1))
                    o = gT[d][:, h, :] if d == 0 else gT[d][:, h, ::-1]
                    dve.tensor_tensor(o, yg[:], sz[d][:, h, :], ALU.mult).then_inc(sem["gated"], 1)

                for slot in range(SLOTS):
                    if slot == 1:
                        dve.wait_ge(sem["xT"], row("xT", 1))
                        dve.tensor_copy(xTr[:, ::-1], xT[:]).then_inc(sem["xTr"], 1)
                    elif slot in (3, 5):
                        d = slot // 2 - 1
                        dve.wait_ge(sem["xi"], row("xi", 2 * d + 2))
                        if before is not None:
                            dve.wait_ge(sem["full"], before("full", R_USE[f"mo{d}"][2] + 1))
                        for k in range(KC):
                            for h in range(NH):
                                x_k = xpad[:, h, k:k + T]
                                if k == 0:
                                    ins = dve.tensor_scalar(u[d][:, h, :], x_k, convw[d][:, h, 0:1],
                                                            cols[d][:, 0, h:h + 1], ALU.mult, ALU.add)
                                else:
                                    ins = dve.scalar_tensor_tensor(u[d][:, h, :], x_k, convw[d][:, h, k:k + 1],
                                                                   u[d][:, h, :], ALU.mult, ALU.add)
                            if k < KC - 1:
                                link(ins)
                        ins.then_inc(sem["conv"], 1)
                    elif slot in (6, 8):
                        d = slot // 2 - 3
                        dve.tensor_copy(dtin[32 * d:32 * d + R, :], full(f"dtin{d}")[32 * d:32 * d + R, :]
                                        ).then_inc(sem["dtin"], 1)
                    for hf in range(2 * NH):
                        if slot in DT_SLOTS[hf]:
                            dt_step(hf, DT_SLOTS[hf].index(slot))
                    n = slot - PREP
                    if 0 <= n < UNITS:
                        drive(n)
                    if 1 <= n <= UNITS:
                        scan(n - 1)
                    if n > 16 and n % 16 == 6 or n == UNITS + 2:
                        gate((n - 4) // 16 - 1 if n < UNITS else 3)
                    yield
                assert links[0] == PER["dve_m"], links

            def rest(row):
                def full(name):
                    dve.wait_ge(sem["full"], row("full", R_USE[name][2] + 1))
                    return use(name)

                links = [0]

                def link(ins):
                    links[0] += 1
                    ins.then_inc(sem["dve_r"], 1)
                    dve.wait_ge(sem["dve_r"], row("dve_r", links[0]))

                def scaled(n, dst):
                    dve.wait_ge(sem["rstd"], row("rstd", n + 1))
                    return dve.tensor_tensor(dst, use(f"cen{n}")[:], rstd[:], ALU.mult).then_inc(sem["norm"], 1)

                dve.wait_ge(sem["xkeep"], row("xkeep", 1))
                for d in range(2):
                    dve.tensor_tensor(nf[:, d, :], full(f"mo{d}")[:], xkept[:], ALU.add).then_inc(sem["resid"], 1)
                yield
                yield
                scaled(0, nf[:, 0, :])
                yield
                scaled(1, nf[:, 1, :])
                dve.wait_ge(sem["norm"], row("norm", 2))
                link(dve.tensor_tensor(nf[:, 0, :], nf[:, 0, :], nf[:, 1, :], ALU.add))
                dve.tensor_scalar(yy[:], nf[:, 0, :], nrm[:, 0:1], fwb2[:, 0:1], ALU.mult, ALU.add
                                  ).then_inc(sem["y"], 1)
                yield
                yield
                dve.wait_ge(sem["y"], row("y", 1))
                dve.scalar_tensor_tensor(res[:], full("ffo")[:], fb[:, 2:3], yy[:], ALU.add, ALU.add
                                         ).then_inc(sem["resid"], 1)
                yield
                yield
                scaled(2, nf[:, 0, :])
                dve.wait_ge(sem["norm"], row("norm", 3))
                link(dve.tensor_scalar(nf[:, 1, :], nf[:, 0, :], nrm[:, 2:3], nrm[:, 3:4], ALU.mult, ALU.add))
                dve.tensor_tensor(res[:], nf[:, 1, :], xkept[:], ALU.add).then_inc(sem["x1"], 1)
                yield
                yield
                scaled(3, xn[:, 0, :])
                yield
                for c in range(0, NC, 2):
                    yield
                    for cc in (c, c + 1):
                        dve.wait_ge(sem["a1"], row("a1", cc + 1))
                        dve.scalar_tensor_tensor(h0[:, cc, :], full(f"b{cc}")[:], sc[:, 1, cc:cc + 1], a1[:, cc % 2, :],
                                                 ALU.mult, ALU.mult).then_inc(sem["h0"], 1)
                    yield
                for _ in range(2 * NC):
                    yield
                dve.wait_ge(sem["norm"], row("norm", 4))
                dve.scalar_tensor_tensor(res[:], full("fo")[:], s3[:, 0:1], xn[:, 0, :], ALU.mult, ALU.add
                                         ).then_inc(sem["resid"], 1)
                yield
                yield
                scaled(4, xn[:, 1, :])
                yield
                for k in range(KV):
                    dve.tensor_copy(kT[:, k, :], full(f"k{k}")[:]).then_inc(sem["kT"], 1)
                    yield
                yield
                for j in range(HEADS * TT + 3):
                    if j < HEADS * TT:
                        w = (j % TT + 1) * P
                        dve.tensor_reduce(nmax[:, j:j + 1], full(f"s{j}")[:, 0:w], AX.X, ALU.max, negate=True
                                          ).then_inc(sem["smax"], 1)
                    if 1 <= j <= HEADS * TT:
                        dve.wait_ge(sem["pexp"], row("pexp", j))
                        dve.reciprocal(rz[:, j - 1:j], zsum[:, j - 1:j]).then_inc(sem["rz"], 1)
                    if j in (REP * TT + 2, HEADS * TT + 2):
                        k = j // (REP * TT) - 1
                        dve.wait_ge(sem["att"], row("att", REP * TT * (k + 1)))
                        dve.tensor_copy(yT[:, k, :], ps_att[:]).then_inc(sem["yT"], 1)
                    yield
                dve.wait_ge(sem["norm"], row("norm", 5))
                dve.tensor_tensor(res[:], full("ao")[:], xn[:, 1, :], ALU.add).then_inc(sem["resid"], 1)
                yield
                yield
                scaled(5, xn[:, 0, :])
                yield

                dve.tensor_copy(lg[:].rearrange("p n e -> p (n e)"), full("lg")[:, 0:TT * E]).then_inc(sem["lg"], 1)
                dve.wait_ge(sem["lg"], row("lg", 1))
                l_e = lg[:].unsqueeze(3).broadcast_to([P, TT, E, E])
                l_j = lg[:].unsqueeze(2).broadcast_to([P, TT, E, E])
                link(dve.tensor_reduce(lmax[:], lg[:], AX.X, ALU.max))
                dve.tensor_tensor(lsh[:], lg[:], lmax[:].unsqueeze(2).broadcast_to([P, TT, E]), ALU.subtract
                                  ).then_inc(sem["gmax"], 1)
                dve.tensor_tensor(cgt, l_j, l_e, ALU.is_gt)
                link(dve.tensor_tensor(ceq, l_j, l_e, ALU.is_equal))
                for n in range(TT):
                    ins = dve.tensor_tensor(ceq[:, n, :, :], ceq[:, n, :, :], lower, ALU.mult)
                link(ins)
                yield

                def more_gates():
                    link(dve.tensor_tensor(cgt, cgt, ceq, ALU.add))
                    link(dve.tensor_reduce(rank[:], cgt, AX.X, ALU.add))
                    dve.wait_ge(sem["gexp"], row("gexp", 1))
                    link(dve.scalar_tensor_tensor(gsel[:], rank[:], 2.0, lexp[:], ALU.is_lt, ALU.mult))
                    link(dve.tensor_reduce(gsum[:], gsel[:], AX.X, ALU.add))
                    link(dve.reciprocal(gsum[:], gsum[:]))
                    dve.tensor_tensor(gates[:], gsel[:], gsum[:].unsqueeze(2).broadcast_to([P, TT, E]), ALU.mult
                                      ).then_inc(sem["gates"], 1)

                for e in range(E + 1):
                    if e < E:
                        if e == 0:
                            more_gates()
                        yield
                        if e >= 2:
                            dve.wait_ge(sem["full"], row("full", R_USE[f"eo{e - 2}"][2] + 1))
                        for c in range(2):
                            i = 2 * e + c
                            dve.wait_ge(sem["ea"], row("ea", i + 1))
                            dve.tensor_tensor(eh[:, e % 2, c, :], full(f"eb{e}{c}")[:], ea[:, i % 2, :], ALU.mult
                                              ).then_inc(sem["eh"], 1)
                        yield
                    if e >= 1:
                        i = e - 1
                        if i == 0:
                            dve.wait_ge(sem["gates"], row("gates", 1))
                        if i >= 2:
                            dve.wait_ge(sem["acc"], row("acc", i - 1))
                        gate_e = gates[:, :, i:i + 1].broadcast_to([P, TT, D])
                        dve.tensor_tensor(gy[:, i % 2, :, :], full(f"eo{i}")[:].rearrange("p (n d) -> p n d", n=TT),
                                          gate_e, ALU.mult).then_inc(sem["eo"], 1)
                        yield
                dve.wait_ge(sem["acc"], row("acc", E))
                for n in range(TT):
                    ins = dve.bn_stats(stats[:, n, :], acc[:, n, :])
                link(ins)
                dve.memset(tick[:], 0.0)
                for n in range(TT):
                    ins = dve.bn_aggr(mv[:, n, :], stats[:, n, :])
                ins.then_inc(sem["mv"], 1)
                yield
                dve.wait_ge(sem["stored"], row("stored", 0))
                dve.wait_ge(sem["trs"], row("trs", 1))
                for n in range(TT):
                    ins = dve.tensor_scalar(otok[:, n, :], acc[:, n, :], mv[:, n, 0:1], rst4[:, n:n + 1],
                                            ALU.subtract, ALU.mult)
                ins.then_inc(sem["outn"], 1)
                yield
                assert links[0] == PER["dve_r"], links

            alone(mamba(counts(0)))
            with dve.Fori(0, B - 1) as b:
                side_by_side(mamba(counts(b, 1), counts(b)), rest(counts(b)))
            alone(rest(counts(B - 1)))


        @block.gpsimd
        def _(pool):
            pool.memset(xpad[:, :, 0:KC - 1], 0.0).then_inc(w_set, 1)
            def mamba(row):
                def dt_step(hf, k):
                    if k == 0:
                        pool.wait_ge(sem["third"], row("third", hf + 1))
                        pool.tensor_tensor(tser[:], tser[:], texp[:], ALU.mult).then_inc(sem["series"], 1)
                    elif k == 2:
                        pool.wait_ge(sem["hi"], row("hi", hf + 1))
                        pool.tensor_tensor(dd[:], dd[:], parts[:, 0, :, :], ALU.subtract
                                           ).then_inc(sem["res"], 1)
                    elif k == 3:
                        pool.wait_ge(sem["mid"], row("mid", hf + 1))
                        pool.tensor_tensor(parts[:, 2, :, :], dd[:], parts[:, 1, :, :], ALU.subtract
                                           ).then_inc(sem["lo"], 1)

                for slot in range(SLOTS):
                    for hf in range(2 * NH):
                        if slot in DT_SLOTS[hf]:
                            dt_step(hf, DT_SLOTS[hf].index(slot))
                    n = slot - PREP - 1
                    if 0 <= n < UNITS:
                        pool.wait_ge(sem["scan"], row("scan", n + 1))
                        pool.wait_ge(sem["y_red"], row("y_red", max((n - 6) // 4 + 1, 0)))
                        pool.tensor_tensor(hc[:, n % 6, :], hst[:, n % 3, :], crep[n // NU][:], ALU.mult
                                           ).then_inc(sem["hc"], 1)
                    yield

            def rest(row):
                for _ in range(28):
                    yield
                for j in range(HEADS * TT + 3):
                    if 1 <= j <= HEADS * TT:
                        i = j - 1
                        w = (i % TT + 1) * P
                        pool.wait_ge(sem["rz"], row("rz", i + 1))
                        if i >= 2:
                            pool.wait_ge(sem["full"], row("full", R_USE[f"t{i - 2}"][2] + 1))
                        pool.tensor_tensor(pn[:, i % 2, 0:w], pexp[:, i % 2, 0:w],
                                           rz[:, i:i + 1].broadcast_to([P, w]), ALU.mult).then_inc(sem["pn"], 1)
                    yield
                for _ in range(4):
                    yield
                for e in range(E + 1):
                    if e < E:
                        yield
                        yield
                    if e >= 1:
                        if e == 1:
                            pool.wait_ge(sem["x3"], row("x3", 1))
                        else:
                            pool.wait_ge(sem["acc"], row("acc", e - 1))
                        pool.wait_ge(sem["eo"], row("eo", e))
                        pool.tensor_tensor(acc, gy[:, (e - 1) % 2, :, :], x3 if e == 1 else acc, ALU.add
                                           ).then_inc(sem["acc"], 1)
                        yield
                yield
                yield

            alone(mamba(counts(0)))
            with pool.Fori(0, B - 1) as b:
                side_by_side(mamba(counts(b, 1)), rest(counts(b)))
            alone(rest(counts(B - 1)))


_PRE = {"L0_attn_": "", "L0_ffn_": "", "L1_attn_": "", "L1_ffn_": ""}


def _short(name):
    for pre in _PRE:
        if name.startswith(pre):
            short = name[len(pre):]
            return "e" + short if pre == "L1_ffn_" and short in ("w1", "w2", "w3") else short
    return name


def kernel(**inputs):
    import numpy as _np
    import concourse.bacc as _bacc
    from concourse import mybir as _mybir
    from concourse.bass_utils import run_bass_kernel_spmd as _run

    nc = _bacc.Bacc("TRN2", target_bir_lowering=False, num_devices=1)
    arrays, args = {}, {}
    for name, value in list(inputs.items()) + [("const", constants())]:
        v = _np.ascontiguousarray(value)
        key = f"in_{name}_dram"
        arrays[key] = v
        args[_short(name)] = nc.dram_tensor(key, v.shape, _mybir.dt.from_np(v.dtype), kind="ExternalInput").ap()
    shape = inputs["L0_attn_x"].shape
    out = nc.dram_tensor("out_dram", shape, F32, kind="ExternalOutput").ap()
    two_layer_kernel(nc, args, out)
    r = _run(nc, [arrays], core_ids=[0])
    return r.results[0]["out_dram"]
```

```python
from contextlib import ExitStack

import numpy as np

import concourse.bass as bass
from concourse import mybir

F32 = mybir.dt.float32
BF16 = mybir.dt.bfloat16
U32 = mybir.dt.uint32
ALU = mybir.AluOpType
ACT = mybir.ActivationFunctionType
AX = mybir.AxisListType

P = 128
T = 512
TT = T // P
D = 128
DI = 256
NH = DI // P
S = 16
R = 8
CU = P // S
NJ = 32 // CU
KC = 4
NU = NH * 16
HID = 512
NC = HID // P
HEADS, KV, LAT = 8, 2, 32
REP = HEADS // KV
E, EH = 8, 256
EPS = 1e-5
SMALL = 0.008
MASKED = -3.0e38

C_ID, C_CEN, C_MEAN, C_RED, C_MASK, C_LT, C_SEL = 0, 128, 256, 384, 512, 640, 704
C_END = C_SEL + NJ * P


def constants():
    c = np.zeros((P, C_END), np.float32)
    p = np.arange(P)
    c[:, C_ID:C_ID + P] = np.eye(P)
    c[:, C_CEN:C_CEN + P] = np.eye(P) - 1.0 / P
    c[:, C_MEAN:C_MEAN + P] = 1.0 / P
    for j in range(NJ):
        for part in range(3):
            c[part * 32 + CU * j + p // S, C_SEL + j * P + p] = 1.0
        c[p, C_RED + j * 32 + CU * j + p // S] = 1.0
    c[:, C_MASK:C_MASK + P] = np.where(p[None, :] > p[:, None], MASKED, 0.0)
    c[:, C_LT:C_LT + E * E] = np.tril(np.ones((E, E)), -1).reshape(-1)
    return c


PER = dict(
    x_in=16, stacked=16 * 48, stored=16,
    full_m=0, full=0, dt_full=64, du_full=64, y_red=16, att=8,
    xT=1, xkeep=1, z=4, u=4, dtin=2, brep=2, crep=2, absd=4, rpos=4, expd=4, third=4,
    logd=4, series=4, dt=4, du=4, hi=4, res=4, mid=4, lo=4,
    dA=64, dbu=64, scan=64, hc=64, yskip=4, gated=4, resid=5, sq=6, rstd=6, norm=6,
    y=1, relu=2, x1=1, a1=4, h0=4, g1=4, g2=4,
    qT=2, kT=2, qz=32, vlat=1, smax=32, pexp=32, rz=32, pn=32, pt=32, yT=2,
    x3=1, lg=1, gmax=1, gexp=1, gates=1, ea=16, eh=16, eo=8, acc=8, mv=1, trs=1, outn=1,
    logv=7, dve_m=8, dve_r=11,
)

PREP, UNITS = 10, 2 * NU
SLOTS = PREP + UNITS + 3
DTP_SLOT = (5, 7, PREP + 21, PREP + 37)
DT_SLOTS = ((5, 6, 7, 8), (PREP + 1, PREP + 2, PREP + 4, PREP + 5), (PREP + 21, PREP + 22, PREP + 23, PREP + 24),
            (PREP + 37, PREP + 38, PREP + 39, PREP + 40))
GATES = (20, 36, 52, UNITS + 2)
XKEEP_SLOT = PREP + 44


def head(i):
    return i // (REP * TT), i // REP % TT, i % REP


def expert_steps():
    for pair in range(0, E + 2, 2):
        yield from (("gate", e) for e in (pair, pair + 1) if e < E)
        yield from (("down", e - 2) for e in (pair, pair + 1) if e >= 2)
        yield from (("up", e) for e in (pair, pair + 1) if e < E)


def mamba_uses():
    uses = [("xT", "xT", 1)]
    for d in range(2):
        uses += [(f"xi{d}{h}", "u", 2 * d + h + 1) for h in range(NH)]
        uses += [(f"z{d}{h}", "z", 2 * d + h + 1) for h in range(NH)]
        uses += [(f"dtin{d}", "dtin", d + 1), (f"B{d}", "brep", d + 1), (f"C{d}", "crep", d + 1)]
        uses += [(f"dtp{d}", "rpos", d + 1)]
    uses += [(f"sums{hf - 2}", "yskip", hf - 1) if part == 0 else (f"dtp{hf}", "rpos", hf + 1)
             for hf in (2, 3) for part in range(2)]
    return uses


def rest_uses():
    def norm(n):
        return [(f"cen{n}", "norm", n + 1), (f"var{n}", "rstd", n + 1)]

    uses = [("mo0", "resid", 1), ("mo1", "resid", 2), ("cen0", "norm", 1), ("cen1", "norm", 2),
            ("var0", "rstd", 1), ("var1", "rstd", 2)]
    uses += [("ff0", "relu", 1), ("ff1", "relu", 2), ("ffo", "resid", 3)] + norm(2) + norm(3)
    for c in range(0, NC, 2):
        uses += [(f"a{c}", "a1", c + 1), (f"a{c + 1}", "a1", c + 2), (f"b{c}", "h0", c + 1), (f"b{c + 1}", "h0", c + 2)]
    uses += [(f"g1_{c}", "g1", c + 1) for c in range(NC)]
    uses += [(f"g2_{c}", "g2", c + 1) for c in range(NC)]
    uses += [("fo", "resid", 4), ("var4", "rstd", 5)]
    for k in range(KV):
        uses += [(f"q{k}", "qT", k + 1), (f"k{k}", "kT", k + 1)]
    uses += [("v", "vlat", 1)]
    for j in range(HEADS * TT + 3):
        if j < HEADS * TT:
            uses += [(f"s{j}", "pexp", j + 1)]
        if j in (6, REP * TT + 6):
            uses += [(f"att{j // (REP * TT)}", "yT", j // (REP * TT) + 1)]
        if 2 <= j < HEADS * TT + 2:
            uses += [(f"t{j - 2}", "pt", j - 1)]
    uses += [("ao", "resid", 5), ("var5", "rstd", 6)]
    uses += [("x3", "x3", 1), ("lg", "lg", 1)]
    for step, e in expert_steps():
        if step == "gate":
            uses += [(f"ea{e}{c}", "ea", 2 * e + c + 1) for c in range(2)]
        elif step == "up":
            uses += [(f"eb{e}{c}", "eh", 2 * e + c + 1) for c in range(2)]
        else:
            uses += [(f"eo{e}", "eo", e + 1)]
    return uses


def place(uses, bank_of, before):
    placed, last, i = {}, dict(before), 0
    for name, semaphore, count in uses:
        bank = bank_of(i, name)
        placed[name] = (bank, last[bank], i)
        last[bank] = (semaphore, count)
        i += name[:3] not in ("att", "sum")
    return placed, last


def mamba_bank(i, name):
    return "y" if name[:3] in ("dtp", "sum") else ("dt0", "dt1", "du")[i % 3]


def rest_bank(i, name):
    if name[:3] == "att":
        return "att"
    if name[0] == "s":
        return ("g0", "g2")[int(name[1:]) % 2]
    return "g1" if name[0] == "t" else ("g0", "g1", "g2", "att")[i % 4]


M_USE, M_LAST = place(mamba_uses(), mamba_bank, dict(y=("yskip", 0), dt0=("scan", 0), dt1=("scan", 0), du=("dbu", 0)))
_, R_LAST = place(rest_uses(), rest_bank, dict(g0=None, g1=None, g2=None, att=None))
R_USE, _ = place(rest_uses(), rest_bank, {bank: (semaphore, 0) for bank, (semaphore, _) in R_LAST.items()})
PER["full_m"], PER["full"] = len(M_USE) - 2, len(R_USE) - 2


PREP_FOLLOW = [1, 1, 1, 1, 1, 1, 1, 1, 2, 2]
COST = dict(ln=1.44, ff=1.28, ab=2.2, g=4, q=2.5, att0=0.9, att1=0.62, lg=2, moe=2.75, end=1.21, unit=1.28)


def follow():
    w = COST
    rest = [0, 0, 0] + [w["ff"]] * 2 + [w["ln"]] * 4 + [w["ab"]] * 4 + [w["g"]] * 9 + [w["ln"]] + [w["q"]] * 3
    rest += [w["att0"] + w["att1"] * head(min(j, HEADS * TT - 1))[1] for j in range(HEADS * TT + 3)]
    rest += [w["ff"]] + [w["ln"]] + [w["lg"]] + [w["moe"]] * (3 * E) + [w["end"]] * 2
    steps, k = list(PREP_FOLLOW), sum(PREP_FOLLOW)
    each = sum(rest[k:]) / (SLOTS - PREP) + w["unit"]
    done = 0.0
    for n in range(SLOTS - PREP):
        done += w["unit"]
        steps.append(0)
        while k < len(rest) and (done + rest[k] / 2 <= each * (n + 1) or n == SLOTS - PREP - 1):
            done += rest[k]
            k += 1
            steps[-1] += 1
    return steps


FOLLOW = follow()
TURN_STEPS = [2] + [0] * (PREP + 3) + [1] * 18 + [0] * (SLOTS - PREP - 22)


def side_by_side(mamba, rest, steps_of_slot):
    for steps in steps_of_slot:
        next(mamba)
        for _ in range(steps):
            next(rest)


def alone(steps):
    for _ in steps:
        pass


def two_layer_kernel(nc, a, out):
    B = a["x"].shape[0]
    with ExitStack() as ctx:
        def sb(name, shape, dt=F32):
            return ctx.enter_context(nc.sbuf_tensor("sb_" + name, shape, dt))

        def psum(name):
            return ctx.enter_context(nc.psum_tensor("ps_" + name, [P, T], F32))

        bank = {name: psum(name) for name in ("dt0", "dt1", "du", "y", "g0", "g1", "g2", "att")}
        ps_dt, ps_du, ps_y, ps_att = [bank["dt0"], bank["dt1"]], bank["du"], bank["y"], bank["att"]

        const = sb("const", [P, C_SEL])
        ident = const[:, C_ID:C_ID + P]
        center = const[:, C_CEN:C_CEN + P]
        mean = const[:, C_MEAN:C_MEAN + P]
        sel = sb("sel", [P, NJ, P], BF16)
        identb = sb("identb", [P, P], BF16)
        maskb = sb("maskb", [P, P], BF16)
        lower = const[:, C_LT:C_LT + E * E].rearrange("p (e j) -> p e j", e=E)
        eps = sb("eps", [P, 1])
        one = sb("one", [P, 1])
        mhalf = sb("mhalf", [P, 1])
        tick = sb("tick", [P, 1])

        winx = [sb(f"winx{d}", [P, KC, DI]) for d in range(2)]
        winz = [sb(f"winz{d}", [P, DI]) for d in range(2)]
        cols = [sb(f"cols{d}", [P, 3, NH]) for d in range(2)]
        wx = [sb(f"wx{d}", [P, NH, R + 2 * S]) for d in range(2)]
        wbc = [sb(f"wbc{d}", [P, NH, 2, P]) for d in range(2)]
        wdt = sb("wdt", [32 + R, DI])
        A = [sb(f"A{d}", [P, NU]) for d in range(2)]
        wout = [sb(f"wout{d}", [P, NH, D]) for d in range(2)]
        nrm = sb("nrm", [P, 4])
        fb = sb("fb", [P, 3])
        fwb2 = sb("fwb2", [P, 1])
        ffw1 = sb("ffw1", [P, 2 * D])
        ffw2 = sb("ffw2", [P, 2, D])
        w1T = sb("w1T", [P, HID])
        w2T = sb("w2T", [P, HID])
        h1T = sb("h1T", [P, NC, HID])
        h2T = sb("h2T", [P, NC, HID])
        w3T = sb("w3T", [P, NC, D])
        sc = sb("sc", [P, 4, NC])
        wkd = sb("wkd", [P, KV, LAT])
        wkrep = sb("wkrep", [P, KV, REP, LAT])
        wvd = sb("wvd", [P, KV * LAT])
        wup = sb("wup", [LAT, 2, P])
        wupT = sb("wupT", [P, 2, LAT])
        wqk = sb("wqk", [P, HEADS, LAT])
        wvo = sb("wvo", [P, KV, D])
        wgate = sb("wgate", [P, E])
        ew1 = sb("ew1", [P, E, EH])
        ew3 = sb("ew3", [P, E, EH])
        ew2 = sb("ew2", [P, E, 2, D])

        xtok = sb("xtok", [P, TT, D])
        xpad = sb("xpad", [P, T + 2 * (KC - 1)])
        xT = xpad[:, KC - 1:KC - 1 + T]
        xkept = sb("xkept", [P, T])
        u = [sb(f"u{d}", [P, NH, T]) for d in range(2)]
        sz = [sb(f"sz{d}", [P, NH, T]) for d in range(2)]
        dtin = sb("dtin", [32 + R, T])
        brep = [sb(f"brep{d}", [P, T]) for d in range(2)]
        crep = [sb(f"crep{d}", [P, T]) for d in range(2)]
        texp = sb("texp", [P, T])
        tlog = sb("tlog", [P, T])
        tpos = sb("tpos", [P, T])
        tser = sb("tser", [P, T])
        tsel = sb("tsel", [P, T], U32)
        dd = sb("dd", [P, 2, T])
        parts = sb("parts", [P, 3, 2, T], BF16)
        stk = sb("stk", [P, 2, 2, 4, T], BF16)
        dbu = sb("dbu", [P, 2, T])
        hst = sb("hst", [P, 3, T])
        hc = sb("hc", [P, 6, T])
        before_loop = hc[:].rearrange("p c t -> p (c t)")
        rawin = [before_loop[:, DI * d:DI * (d + 1)] for d in range(2)]
        rawconv = [before_loop[:, 2 * DI + DI * KC * d:2 * DI + DI * KC * (d + 1)] for d in range(2)]
        yg = tpos
        res = sb("res", [P, T])
        sq = sb("sq", [P, T])
        lnv = sb("lnv", [P, T])
        rstd = sb("rstd", [P, T])
        mix = sb("mix", [P, 4, T])
        nf, a1 = mix[:, 0:2, :], mix[:, 2:4, :]
        yy = sb("yy", [P, T])
        xn = sb("xn", [P, 2, T])
        qz = sb("qz", [P, REP, P])
        h0 = sb("h0", [P, NC, T])
        g1 = sb("g1", [P, NC, T])
        qT, kT = g1[:, 0:KV, :], g1[:, KV:2 * KV, :]
        pexp, pn = h0[:, 0:2, :], h0[:, 2:4, :]
        pt, ea = mix, g1
        yT = qT
        hrel = h0[:, 0:2, :]
        eh = h0.rearrange("p (e c) t -> p e c t", e=2)
        x3 = yy[:].rearrange("p (n d) -> p n d", n=TT)
        gy = nf.rearrange("p e (n d) -> p e n d", n=TT)
        acc = res[:].rearrange("p (n d) -> p n d", n=TT)
        gT = u
        rawh1, rawh2 = h0[:], g1[:]
        raw1 = res[:].rearrange("p (c i) -> p c i", c=NC)
        raw2 = lnv[:].rearrange("p (c i) -> p c i", c=NC)
        raw3 = yy[:]
        rawsel = rstd[:]
        wo = mix[:, 0:2, :].rearrange("p c (h n) -> p (c h) n", h=4)
        wq = mix[:, 2:4, :].rearrange("p c n -> p (c n)")
        wqT = xn[:].rearrange("p c (h n) -> p (c h) n", h=4)
        s3 = sq[:, 2 * P:3 * P]
        alog = [sq[0:NU, 0:P], sq[0:NU, P:2 * P]]
        vlat = sb("vlat", [P, TT, KV * LAT])
        nmax = sb("nmax", [P, HEADS * TT])
        zsum = sb("zsum", [P, HEADS * TT])
        rz = sb("rz", [P, HEADS * TT])
        lg = sb("lg", [P, TT, E])
        lmax = sb("lmax", [P, TT])
        lsh = sb("lsh", [P, TT, E])
        lexp = sb("lexp", [P, TT, E])
        cgt = sq[:, 0:TT * E * E].rearrange("p (n e j) -> p n e j", n=TT, e=E)
        ceq = sq[:, TT * E * E:2 * TT * E * E].rearrange("p (n e j) -> p n e j", n=TT, e=E)
        rank = sb("rank", [P, TT, E])
        gsel = sb("gsel", [P, TT, E])
        gsum = sb("gsum", [P, TT])
        gates = sb("gates", [P, TT, E])
        stats = sb("stats", [P, TT, 6])
        mv = sb("mv", [P, TT, 2])
        lnv4 = sb("lnv4", [P, TT])
        rst4 = sb("rst4", [P, TT])
        otok = lnv[:].rearrange("p (n d) -> p n d", n=TT)

        sem = {n: ctx.enter_context(nc.semaphore(n)) for n in PER}
        w_in = ctx.enter_context(nc.semaphore("w_in"))
        w_later = ctx.enter_context(nc.semaphore("w_later"))
        w_tp = ctx.enter_context(nc.semaphore("w_tp"))
        w_cp = ctx.enter_context(nc.semaphore("w_cp"))
        w_set = ctx.enter_context(nc.semaphore("w_set"))
        w_fold = ctx.enter_context(nc.semaphore("w_fold"))
        w_exp = ctx.enter_context(nc.semaphore("w_exp"))
        block = ctx.enter_context(nc.Block())

        turn_banks = [bank[name] for name in ("g0", "g1", "g2", "att")]

        def use(name):
            return bank[(M_USE if name in M_USE else R_USE)[name][0]]

        def first(name):
            return 16 if name in ("x_in", "stacked", "stored") else 1

        def counts(b, ahead=0):
            def row(name, k):
                return b * PER[name] + (ahead * PER[name] + k + first(name))
            return row

        def out_rows(b):
            return out[bass.ds(b, 1)].rearrange("o (n p) d -> p (o n) d", p=P)

        def turned():
            yield from (("alog", d) for d in range(2))
            yield from (("w1", 0), ("w2", 0))
            yield from (("h1", c) for c in range(NC))
            yield from (("h2", c) for c in range(NC))
            yield from (("w3", 0), ("wq", 0), ("wq", 1), ("wup", 0), ("wqk", 0), ("wvo", 0), ("wvo", 1))

        TURNED = list(turned())
        TURN = {x: i for i, x in enumerate(TURNED)}
        M_LOADS, R_LOADS = 20, 37

        @block.sync
        def _(sp):
            loads = [(const[:], a["const"][:, 0:C_SEL]), (rawsel, a["const"][:, C_SEL:C_END])]
            for d, pre in enumerate(("fw", "bw")):
                loads += [
                    (rawin[d], a[f"{pre}_Win"][:, 0:DI]),
                    (rawconv[d], a[f"{pre}_convw"].rearrange("c k -> (c k)").partition_broadcast(P)),
                    (winz[d][:], a[f"{pre}_Win"][:, DI:2 * DI]),
                    (wx[d][:], a[f"{pre}_Wx"].rearrange("(h p) k -> p h k", p=P)),
                    (wdt[32 * d:32 * d + R, :], a[f"{pre}_Wdt"]),
                    (alog[d], a[f"{pre}_Alog"].rearrange("(g c) s -> g (c s)", c=CU))]
                loads += [(cols[d][:, i, :], a[f"{pre}_{v}"].rearrange("(h p) -> p h", p=P))
                          for i, v in enumerate(("convb", "bdt", "D"))]
            assert len(loads) == M_LOADS, len(loads)
            later = [(wout[d][:], a[f"{pre}_Wout"].rearrange("(h p) n -> p h n", p=P))
                     for d, pre in enumerate(("fw", "bw"))]
            later += [(raw1, a["w1_w"].rearrange("(c p) i -> p c i", p=P)),
                      (raw2, a["w2_w"].rearrange("(c p) i -> p c i", p=P)),
                      (rawh1, a["h1_w"].rearrange("(c p) i -> p c i", p=P)),
                      (rawh2, a["h2_w"].rearrange("(c p) i -> p c i", p=P)),
                      (raw3, a["w3_w"]),
                      (wq, a["wq"]), (wup[:, 0, :], a["wk_up"]), (wup[:, 1, :], a["wv_up"]),
                      (wo, a["wo"].rearrange("(h p) n -> p h n", p=P)),
                      (wkd[:], a["wk_down"].rearrange("p (k l) -> p k l", k=KV)),
                      (wvd[:], a["wv_down"]), (wgate[:], a["w_gate"])]
            later += [(nrm[:, i:i + 1], a[v].rearrange("(p o) -> p o", o=1))
                      for i, v in enumerate(("fwn_w", "fwn_b", "fin_w", "fin_b"))]
            later += [(fb[:, 0:2], a["ff_b1"].rearrange("(h p) -> p h", p=P)),
                      (fb[:, 2:3], a["ff_b2"].rearrange("(p o) -> p o", o=1)),
                      (ffw1[:], a["ff_W1"]),
                      (ffw2[:], a["ff_W2"].rearrange("(h p) n -> p h n", p=P))]
            later += [(sc[:, i, :], a[v].rearrange("(c p) -> p c", p=P))
                      for i, v in enumerate(("w1_s", "w2_s", "h1_s", "h2_s"))]
            later += [(s3, a["w3_s"].partition_broadcast(P)),
                      (ew1[:], a["ew1"].rearrange("e p h -> p e h")),
                      (ew3[:], a["ew3"].rearrange("e p h -> p e h"))]
            later += [(ew2[:, e, :, :], a["ew2"][e].rearrange("(c p) n -> p c n", p=P)) for e in range(E)]
            assert len(later) == R_LOADS, len(later)
            for name in PER:
                sp.sem_inc(sem[name], first(name))
            with nc.allow_non_contiguous_dma(reason="per-channel vectors, once"):
                for dst, src in loads:
                    sp.dma_start(dst, src).then_inc(w_in, 16)
                sp.dma_start(xtok[:], a["x"][0:1].rearrange("o (n p) d -> p (o n) d", p=P)).then_inc(sem["x_in"], 16)
                for dst, src in later:
                    sp.dma_start(dst, src).then_inc(w_later, 16)

            def stacks(b):
                for hf in range(2 * NH):
                    cut = b * PER["lo"] + (hf + 1 + first("lo"))
                    spread = b * PER["dt_full"] + (max(16 * (hf - 1), 0) + first("dt_full"))
                    for value in (cut, spread):
                        if not isinstance(value, int):
                            sp.compute_val(value)
                    sp.wait_ge(sem["lo"], cut)
                    sp.wait_ge(sem["dt_full"], spread)
                    for part in range(3):
                        for q in range(4):
                            sp.dma_start(stk[32 * part:32 * part + 32, hf % 2, :, q, :],
                                         parts[32 * q:32 * q + 32, part, :, :]
                                         ).then_inc(sem["stacked"], 16)

            with sp.Fori(0, B - 1) as b:
                stacks(b)
                sp.dma_start(xtok[:], a["x"][1:][bass.ds(b, 1)].rearrange("o (n p) d -> p (o n) d", p=P)
                             ).then_inc(sem["x_in"], 16)
            stacks(B - 1)

        @block.tensor
        def _(pe):
            def turn_weights():
                for i, (kind, c) in enumerate(TURNED):
                  o = turn_banks[i % 4]
                  if i == 2:
                      pe.wait_ge(w_later, 16 * R_LOADS)
                  if i >= 4:
                      pe.wait_ge(w_cp, i - 3)
                  if kind == "alog":
                      pe.wait_ge(w_exp, c + 1)
                      ins = pe.transpose(o[:, 0:NU], alog[c], ident[0:NU, 0:NU])
                  elif kind in ("w1", "w2"):
                      src = raw1 if kind == "w1" else raw2
                      for k in range(NC):
                          ins = pe.transpose(o[:, k * P:(k + 1) * P], src[:, k, :], ident)
                  elif kind in ("h1", "h2"):
                      src = rawh1 if kind == "h1" else rawh2
                      for k in range(NC):
                          ins = pe.transpose(o[:, k * P:(k + 1) * P], src[:, k, c * P:(c + 1) * P], ident)
                  elif kind == "w3":
                      for k in range(NC):
                          ins = pe.transpose(o[:, k * P:(k + 1) * P], raw3[:, k * P:(k + 1) * P], ident)
                  elif kind == "wq":
                      for k in range(NC):
                          h = 4 * c + k
                          ins = pe.transpose(o[:, k * P:(k + 1) * P], wq[:, h * P:(h + 1) * P], ident)
                  elif kind == "wup":
                      for k in range(2):
                          ins = pe.transpose(o[:, k * LAT:(k + 1) * LAT], wup[:, k, :], ident[0:LAT, 0:LAT])
                  elif kind == "wqk":
                      pe.wait_ge(w_cp, TURN["wup", 0] + 1)
                      for h in range(HEADS):
                          ins = pe.matmul(o[:, h * LAT:(h + 1) * LAT], wqT[:, h, :], wupT[:, 0, :],
                                          start=True, stop=True)
                  elif kind == "wvo":
                      for r in range(REP):
                          ins = pe.matmul(o[LAT * r:LAT * (r + 1), 0:D], wupT[:, 1, :], wo[:, REP * c + r, :],
                                          start=True, stop=True)
                  ins.then_inc(w_tp, 1)
                  yield
                pe.wait_ge(w_cp, len(TURNED))
                yield

            pe.wait_ge(w_in, 16 * M_LOADS)

            def mamba(row):
                def product(name, lhs, rhs, rows=slice(0, P)):
                    pe.wait_ge(sem[M_USE[name][1][0]], row(*M_USE[name][1]))
                    for i, (l, r) in enumerate(zip(lhs, rhs)):
                        ins = pe.matmul(use(name)[rows, :], l, r, start=(i == 0), stop=(i == len(lhs) - 1))
                    ins.then_inc(sem["full_m"], 1)

                def shifted(d, k):
                    return xpad[:, k:k + T] if d == 0 else xpad[:, T + 2 * (KC - 1) - 1 - k:KC - 2 - k if k < KC - 1 else None:-1][:, 0:T]

                def dt_in(d):
                    product(f"dtin{d}", [wx[d][:, h, 0:R] for h in range(NH)], [u[d][:, h, :] for h in range(NH)],
                            slice(32 * d, 32 * d + R))
                    product(f"B{d}", [wbc[d][:, h, 0, :] for h in range(NH)], [u[d][:, h, :] for h in range(NH)])
                    product(f"C{d}", [wbc[d][:, h, 1, :] for h in range(NH)], [u[d][:, h, :] for h in range(NH)])

                def dt_product(hf):
                    d, h = divmod(hf, NH)
                    pe.wait_ge(sem["dtin"], row("dtin", d + 1))
                    rows = slice(32 * d, 32 * d + R)
                    product(f"dtp{hf}", [wdt[rows, h * P:(h + 1) * P]], [dtin[rows, :]])

                def spread(n):
                    d, m = divmod(n, NU)
                    half, j, q = m // 16, m % 16 // 4, m % 4
                    if n % 16 == 0:
                        pe.wait_ge(sem["stacked"], row("stacked", 16 * 12 * (n // 16 + 1)))
                    if n == 0:
                        pe.wait_ge(sem[M_LAST["du"][0]], row(*M_LAST["du"]))
                    else:
                        pe.wait_ge(sem["dbu"], row("dbu", n))
                    pe.matmul(ps_du[:], sel[0:96, j, :], stk[0:96, half, 1, q, :],
                              start=True, stop=True).then_inc(sem["du_full"], 1)
                    if n < 2:
                        pe.wait_ge(sem[M_LAST[f"dt{n}"][0]], row(*M_LAST[f"dt{n}"]))
                    else:
                        pe.wait_ge(sem["scan"], row("scan", n - 1))
                    pe.matmul(ps_dt[n % 2][:], sel[0:96, j, :], stk[0:96, half, 0, q, :],
                              start=True, stop=True).then_inc(sem["dt_full"], 1)

                def reduce(k):
                    hf, j = divmod(k, 4)
                    if j == 0 and hf < 3:
                        pe.wait_ge(sem["rpos"], row("rpos", hf + 2))
                    elif j == 0:
                        pe.wait_ge(sem["yskip"], row("yskip", hf))
                    pe.wait_ge(sem["hc"], row("hc", 4 * k + 4))
                    for q in range(4):
                        red = const[:, C_RED + 32 * j:C_RED + 32 * j + 32]
                        ins = pe.matmul(ps_y[32 * q:32 * q + 32, :], red, hc[:, (4 * k + q) % 6, :],
                                        start=(j == 0), stop=(j == 3))
                    ins.then_inc(sem["y_red"], 1)

                for slot in range(SLOTS):
                    if slot == DTP_SLOT[0]:
                        dt_product(0)
                    if slot == 1:
                        pe.wait_ge(sem[M_USE["xT"][1][0]], row(*M_USE["xT"][1]))
                        pe.wait_ge(sem["x_in"], row("x_in", 16))
                        for n in range(TT):
                            ins = pe.transpose(use("xT")[:, n * P:(n + 1) * P], xtok[:, n, :], ident)
                        ins.then_inc(sem["full_m"], 1)
                    elif slot in (2, 5):
                        d = slot // 3
                        pe.wait_ge(sem["xT"], row("xT", 1))
                        for h in range(NH):
                            product(f"xi{d}{h}", [winx[d][:, k, h * P:(h + 1) * P] for k in range(KC)],
                                    [shifted(d, k) for k in range(KC)])
                    elif slot in (3, 6):
                        d = slot // 3 - 1
                        for h in range(NH):
                            product(f"z{d}{h}", [winz[d][:, h * P:(h + 1) * P]], [shifted(d, KC - 1)])
                    elif slot in (4, 7):
                        d = slot // 3 - 1
                        pe.wait_ge(sem["u"], row("u", 2 * d + 2))
                        dt_in(d)
                    if slot in DTP_SLOT[1:]:
                        dt_product(DTP_SLOT.index(slot))
                    n = slot - PREP
                    if 0 <= n < UNITS:
                        spread(n)
                    if n >= 6 and (n - 6) % 4 == 0:
                        reduce((n - 6) // 4)
                    yield

            def rest(row):
                def claim(name):
                    pe.wait_ge(sem[R_USE[name][1][0]], row(*R_USE[name][1]))
                    return use(name)

                def done(ins):
                    ins.then_inc(sem["full"], 1)

                def product(name, lhs, rhs):
                    o = claim(name)
                    for i, (l, r) in enumerate(zip(lhs, rhs)):
                        ins = pe.matmul(o[:], l, r, start=(i == 0), stop=(i == len(lhs) - 1))
                    done(ins)

                pe.wait_ge(sem["gated"], row("gated", 4))
                for d in range(2):
                    product(f"mo{d}", [wout[d][:, h, :] for h in range(NH)], [gT[d][:, h, :] for h in range(NH)])
                yield
                for d in range(2):
                    pe.wait_ge(sem["resid"], row("resid", d + 1))
                    product(f"cen{d}", [center], [nf[:, d, :]])
                yield
                for d in range(2):
                    pe.wait_ge(sem["sq"], row("sq", d + 1))
                    product(f"var{d}", [mean], [(sq, yy)[d][:]])
                yield

                def norm(n, src_sem, k):
                    pe.wait_ge(sem[src_sem], row(src_sem, k))
                    product(f"cen{n}", [center], [res[:]])
                    yield
                    pe.wait_ge(sem["sq"], row("sq", n + 1))
                    product(f"var{n}", [mean], [sq[:]])
                    yield

                pe.wait_ge(sem["y"], row("y", 1))
                for h in range(2):
                    product(f"ff{h}", [ffw1[:, h * P:(h + 1) * P]], [yy[:]])
                yield
                pe.wait_ge(sem["relu"], row("relu", 2))
                product("ffo", [ffw2[:, h, :] for h in range(2)], [hrel[:, h, :] for h in range(2)])
                yield
                yield from norm(2, "resid", 3)
                yield from norm(3, "x1", 1)

                pe.wait_ge(sem["norm"], row("norm", 4))
                for c in range(0, NC, 2):
                    for name, w in (("a", w1T), ("b", w2T)):
                        for cc in (c, c + 1):
                            product(f"{name}{cc}", [w[:, cc * P:(cc + 1) * P]], [xn[:, 0, :]])
                        yield
                for name, src, w in (("g1", "h0", h1T), ("g2", "g1", h2T)):
                    pe.wait_ge(sem[src], row(src, 4))
                    x_in = h0 if name == "g1" else g1
                    for c in range(NC):
                        product(f"{name}_{c}", [w[:, k, c * P:(c + 1) * P] for k in range(NC)],
                                [x_in[:, k, :] for k in range(NC)])
                        yield
                pe.wait_ge(sem["g2"], row("g2", 4))
                product("fo", [w3T[:, k, :] for k in range(NC)], [h0[:, k, :] for k in range(NC)])
                yield
                pe.wait_ge(sem["sq"], row("sq", 5))
                product("var4", [mean], [sq[:]])
                yield

                pe.wait_ge(sem["norm"], row("norm", 5))
                for k in range(KV):
                    wqk_k = wqk[:, REP * k:REP * (k + 1), :].rearrange("p r l -> p (r l)")
                    product(f"q{k}", [wqk_k], [xn[:, 1, :]])
                    product(f"k{k}", [wkrep[:, k, :, :].rearrange("p r l -> p (r l)")], [xn[:, 1, :]])
                    yield
                o = claim("v")
                for n in range(TT):
                    ins = pe.matmul(o[:, n * KV * LAT:(n + 1) * KV * LAT], xn[:, 1, n * P:(n + 1) * P],
                                    wvd[:], start=True, stop=True)
                done(ins)
                yield

                def scores(i):
                    k, t, r = head(i)
                    o = claim(f"s{i}")
                    if t == 0 and r == 0:
                        pe.wait_ge(sem["kT"], row("kT", k + 1))
                    pe.wait_ge(sem["qz"], row("qz", i + 1))
                    pe.matmul(o[:, 0:(t + 1) * P], qz[:, r, :], kT[:, k, 0:(t + 1) * P], start=True, stop=False)
                    done(pe.matmul(o[:, t * P:(t + 1) * P], identb[:], maskb[:], start=False, stop=True))

                def turn(i):
                    t = head(i)[1]
                    o = claim(f"t{i}")
                    pe.wait_ge(sem["pn"], row("pn", i + 1))
                    for j in range(t + 1):
                        ins = pe.transpose(o[:, j * P:(j + 1) * P], pn[:, i % 2, j * P:(j + 1) * P], ident)
                    done(ins)

                def values(g):
                    k, t = divmod(g, TT)
                    if t == 0:
                        claim(f"att{k}")
                        pe.wait_ge(sem["vlat"], row("vlat", 1))
                    pe.wait_ge(sem["pt"], row("pt", REP * (g + 1)))
                    for j in range(t + 1):
                        for r in range(REP):
                            ins = pe.matmul(ps_att[LAT * r:LAT * (r + 1), t * P:(t + 1) * P],
                                            vlat[:, j, k * LAT:(k + 1) * LAT], pt[:, r, j * P:(j + 1) * P],
                                            start=(j == 0), stop=(j == t))
                    ins.then_inc(sem["att"], 1)

                for j in range(HEADS * TT + 3):
                    if j < HEADS * TT:
                        scores(j)
                    if j >= 6 and (j - 6) % REP == 0:
                        values((j - 6) // REP)
                    if 2 <= j < HEADS * TT + 2:
                        turn(j - 2)
                    yield
                pe.wait_ge(sem["yT"], row("yT", 2))
                product("ao", [wvo[:, k, :] for k in range(KV)], [yT[:, k, :] for k in range(KV)])
                yield
                pe.wait_ge(sem["sq"], row("sq", 6))
                product("var5", [mean], [sq[:]])
                yield

                pe.wait_ge(sem["norm"], row("norm", 6))
                o = claim("x3")
                for n in range(TT):
                    ins = pe.transpose(o[:, n * P:(n + 1) * P], xn[:, 0, n * P:(n + 1) * P], ident)
                done(ins)
                o = claim("lg")
                for n in range(TT):
                    ins = pe.matmul(o[:, n * E:(n + 1) * E], xn[:, 0, n * P:(n + 1) * P], wgate[:],
                                    start=True, stop=True)
                done(ins)
                yield

                def down(e):
                    o = claim(f"eo{e}")
                    pe.wait_ge(sem["eh"], row("eh", 2 * e + 2))
                    for n in range(TT):
                        for c in range(2):
                            ins = pe.matmul(o[:, n * D:(n + 1) * D], eh[:, e % 2, c, n * P:(n + 1) * P],
                                            ew2[:, e, c, :], start=(c == 0), stop=(c == 1))
                    done(ins)

                for step, e in expert_steps():
                    if step == "down":
                        down(e)
                    else:
                        name, w = ("ea", ew1) if step == "gate" else ("eb", ew3)
                        for c in range(2):
                            product(f"{name}{e}{c}", [w[:, e, c * P:(c + 1) * P]], [xn[:, 0, :]])
                    yield
                yield
                yield

            pe.wait_ge(w_set, 2)
            side_by_side(mamba(counts(0)), turn_weights(), TURN_STEPS)
            with pe.Fori(0, B - 1) as b:
                side_by_side(mamba(counts(b, 1)), rest(counts(b)), FOLLOW)
            alone(rest(counts(B - 1)))

        @block.scalar
        def _(act):
            act.wait_ge(w_in, 16 * M_LOADS)
            for d in range(2):
                act.activation(alog[d], alog[d], ACT.Exp).then_inc(w_exp, 1)
            act.wait_ge(w_set, 2)
            def mamba(row, before=None):
                def full(name):
                    act.wait_ge(sem["full_m"], row("full_m", M_USE[name][2] + 1))
                    return use(name)

                def dt_step(hf, k):
                    d, h = divmod(hf, NH)
                    if k == 0:
                        act.wait_ge(sem["dt"], row("dt", hf))
                        act.activation(tlog[:], full(f"dtp{hf}")[:], ACT.Abs, bias=cols[d][:, 1, h:h + 1]
                                       ).then_inc(sem["absd"], 1)
                        act.wait_ge(sem["absd"], row("absd", hf + 1))
                        act.activation(texp[:], tlog[:], ACT.Exp, scale=-1.0).then_inc(sem["expd"], 1)
                        act.wait_ge(sem["expd"], row("expd", hf + 1))
                        act.activation(tser[:], texp[:], ACT.Identity, scale=1.0 / 3.0, bias=mhalf[:, 0:1]
                                       ).then_inc(sem["third"], 1)
                        act.activation(tlog[:], texp[:], ACT.Ln, bias=one[:, 0:1]).then_inc(sem["logd"], 1)
                    elif k == 2:
                        act.wait_ge(sem["du"], row("du", hf + 1))
                        act.wait_ge(sem["stacked"], row("stacked", 16 * 12 * hf))
                        act.activation(parts[:, 0, :, :], dd[:], ACT.Copy).then_inc(sem["hi"], 1)
                    elif k == 3:
                        act.wait_ge(sem["res"], row("res", hf + 1))
                        act.activation(parts[:, 1, :, :], dd[:], ACT.Copy).then_inc(sem["mid"], 1)

                for slot in range(SLOTS):
                    for hf in range(2 * NH):
                        if slot in DT_SLOTS[hf]:
                            dt_step(hf, DT_SLOTS[hf].index(slot))
                    if slot == 1:
                        act.activation(xT, full("xT")[:], ACT.Copy).then_inc(sem["xT"], 1)
                    elif slot in (2, 5):
                        d = slot // 3
                        if before is not None:
                            act.wait_ge(sem["full"], before("full", R_USE[f"mo{d}"][2] + 1))
                        for h in range(NH):
                            act.activation(u[d][:, h, :], full(f"xi{d}{h}")[:], ACT.Silu, bias=cols[d][:, 0, h:h + 1]
                                           ).then_inc(sem["u"], 1)
                    elif slot in (3, 6):
                        d = slot // 3 - 1
                        act.wait_ge(sem["gated"], row("gated", 0))
                        for h in range(NH):
                            act.activation(sz[d][:, h, :], full(f"z{d}{h}")[:], ACT.Silu).then_inc(sem["z"], 1)
                    elif slot in (4, 7):
                        d = slot // 3 - 1
                        act.wait_ge(sem["hc"], row("hc", 0))
                        act.activation(brep[d][:], full(f"B{d}")[:], ACT.Copy).then_inc(sem["brep"], 1)
                        act.activation(crep[d][:], full(f"C{d}")[:], ACT.Copy).then_inc(sem["crep"], 1)
                    n = slot - PREP
                    if 0 <= n < UNITS:
                        d, m = divmod(n, NU)
                        half, j, q = m // 16, m % 16 // 4, m % 4
                        g = (4 * half + q) * NJ + j
                        act.wait_ge(sem["dt_full"], row("dt_full", n + 1))
                        act.activation(ps_dt[n % 2][:], ps_dt[n % 2][:], ACT.Exp, scale=A[d][:, g:g + 1]
                                       ).then_inc(sem["dA"], 1)
                    if slot == XKEEP_SLOT:
                        act.wait_ge(sem["x1"], row("x1", 0))
                        act.activation(xkept[:], xT, ACT.Copy).then_inc(sem["xkeep"], 1)
                    yield

            def rest(row, out_row):
                def full(name):
                    act.wait_ge(sem["full"], row("full", R_USE[name][2] + 1))
                    return use(name)

                def square(n):
                    act.activation(sq[:], full(f"cen{n}")[:], ACT.Square).then_inc(sem["sq"], 1)

                def root(n):
                    act.activation(lnv[:], full(f"var{n}")[:], ACT.Ln, bias=eps[:, 0:1]).then_inc(sem["logv"], 1)
                    act.wait_ge(sem["norm"], row("norm", n))
                    act.wait_ge(sem["logv"], row("logv", n + 1))
                    act.activation(rstd[:], lnv[:], ACT.Exp, scale=-0.5).then_inc(sem["rstd"], 1)

                yield
                act.wait_ge(sem["stored"], row("stored", 0))
                act.activation(sq[:], full("cen0")[:], ACT.Square).then_inc(sem["sq"], 1)
                act.activation(yy[:], full("cen1")[:], ACT.Square).then_inc(sem["sq"], 1)
                yield
                act.activation(lnv[:], full("var0")[:], ACT.Ln, bias=eps[:, 0:1]).then_inc(sem["logv"], 1)
                act.activation(res[:], full("var1")[:], ACT.Ln, bias=eps[:, 0:1]).then_inc(sem["logv"], 1)
                act.wait_ge(sem["norm"], row("norm", 0))
                act.wait_ge(sem["logv"], row("logv", 1))
                act.activation(rstd[:], lnv[:], ACT.Exp, scale=-0.5).then_inc(sem["rstd"], 1)
                act.wait_ge(sem["logv"], row("logv", 2))
                act.activation(res[:], res[:], ACT.Exp, scale=-0.5).then_inc(sem["rstd"], 1)
                yield
                for h in range(2):
                    act.activation(hrel[:, h, :], full(f"ff{h}")[:], ACT.Relu, bias=fb[:, h:h + 1]
                                   ).then_inc(sem["relu"], 1)
                yield
                yield
                for n in (2, 3):
                    square(n)
                    yield
                    root(n)
                    yield
                for c in range(0, NC, 2):
                    for cc in (c, c + 1):
                        act.wait_ge(sem["h0"], row("h0", max(cc - 1, 0)))
                        act.activation(a1[:, cc % 2, :], full(f"a{cc}")[:], ACT.Silu, scale=sc[:, 0, cc:cc + 1]
                                       ).then_inc(sem["a1"], 1)
                    yield
                    yield
                for name, dst, i in (("g1", g1, 2), ("g2", h0, 3)):
                    for c in range(0, NC, 2):
                        yield
                        for cc in (c, c + 1):
                            act.activation(dst[:, cc, :], full(f"{name}_{cc}")[:], ACT.Gelu, scale=sc[:, i, cc:cc + 1]
                                           ).then_inc(sem[name], 1)
                        yield
                act.wait_ge(sem["resid"], row("resid", 4))
                act.activation(sq[:], res[:], ACT.Square).then_inc(sem["sq"], 1)
                yield
                root(4)
                yield
                for k in range(KV):
                    act.activation(qT[:, k, :], full(f"q{k}")[:], ACT.Copy, scale=float(D) ** -0.5
                                   ).then_inc(sem["qT"], 1)
                    yield
                act.activation(vlat[:].rearrange("p n l -> p (n l)"), full("v")[:, 0:TT * KV * LAT], ACT.Copy
                               ).then_inc(sem["vlat"], 1)
                yield
                for j in range(HEADS * TT + 3):
                    if j < HEADS * TT:
                        w = (head(j)[1] + 1) * P
                        act.wait_ge(sem["smax"], row("smax", j + 1))
                        if j >= 2:
                            act.wait_ge(sem["pn"], row("pn", j - 1))
                        act.activation(pexp[:, j % 2, 0:w], use(f"s{j}")[:, 0:w], ACT.Exp,
                                       bias=nmax[:, j:j + 1], accum_out=zsum[:, j:j + 1]
                                       ).then_inc(sem["pexp"], 1)
                    if 2 <= j < HEADS * TT + 2:
                        k = j - 2
                        w = (head(k)[1] + 1) * P
                        if k >= REP:
                            act.wait_ge(sem["att"], row("att", k // REP))
                        act.activation(pt[:, k % REP, 0:w], full(f"t{k}")[:, 0:w], ACT.Copy).then_inc(sem["pt"], 1)
                    yield
                act.wait_ge(sem["resid"], row("resid", 5))
                act.activation(sq[:], res[:], ACT.Square).then_inc(sem["sq"], 1)
                yield
                root(5)
                yield
                act.activation(x3.rearrange("p n d -> p (n d)"), full("x3")[:], ACT.Copy).then_inc(sem["x3"], 1)
                act.wait_ge(sem["gmax"], row("gmax", 1))
                act.activation(lexp[:], lsh[:], ACT.Exp).then_inc(sem["gexp"], 1)
                yield
                for step, e in expert_steps():
                    if step == "gate" and e % 2 == 1:
                        for i in range(2 * e - 2, 2 * e + 2):
                            if i >= 4:
                                act.wait_ge(sem["eh"], row("eh", i - 3))
                            act.activation(ea[:, i % 4, :], full(f"ea{i // 2}{i % 2}")[:], ACT.Silu
                                           ).then_inc(sem["ea"], 1)
                    yield
                act.wait_ge(sem["mv"], row("mv", 1))
                act.activation(lnv4[:], mv[:, :, 1], ACT.Ln, bias=eps[:, 0:1]).then_inc(sem["logv"], 1)
                act.wait_ge(sem["logv"], row("logv", 7))
                act.activation(rst4[:], lnv4[:], ACT.Exp, scale=-0.5).then_inc(sem["trs"], 1)
                yield
                act.wait_ge(sem["outn"], row("outn", 1))
                act.dma_start(out_row, otok).then_inc(sem["stored"], 16)
                yield

            act.wait_ge(w_cp, 2)
            alone(mamba(counts(0)))
            act.wait_ge(w_later, 16 * R_LOADS)
            with act.Fori(0, B - 1) as b:
                side_by_side(mamba(counts(b, 1), counts(b)), rest(counts(b), out_rows(b)), FOLLOW)
            alone(rest(counts(B - 1), out_rows(B - 1)))
            act.wait_ge(sem["stored"], 16 * B + first("stored"))


        @block.vector
        def _(dve):
            dve.memset(eps[:], EPS)
            dve.memset(mhalf[:], -0.5)
            dve.memset(one[:], 1.0)
            dve.wait_ge(w_in, 16 * M_LOADS)
            dve.tensor_copy(sel[:], rawsel.rearrange("p (j m) -> p j m", j=NJ))
            dve.tensor_copy(identb[:], ident)
            dve.tensor_copy(maskb[:], const[:, C_MASK:C_MASK + P])
            for d in range(2):
                for w in range(2):
                    cut = wx[d][:, :, R + S * w:R + S * (w + 1)]
                    for h in range(NH):
                        dve.tensor_copy(wbc[d][:, h, w, :].rearrange("p (c s) -> p c s", c=CU),
                                        cut[:, h, :].unsqueeze(1).broadcast_to([P, CU, S]))
            for d in range(2):
                taps = rawconv[d].rearrange("p (c k) -> p c k", k=KC)
                for k in range(KC):
                    ins = dve.tensor_tensor(winx[d][:, k, :], rawin[d], taps[:, :, k], ALU.mult)
            ins.then_inc(w_set, 1)

            def turned_out():
                links = [0]

                def link(ins):
                    links[0] += 1
                    ins.then_inc(w_fold, 1)
                    dve.wait_ge(w_fold, links[0])

                for i, (kind, c) in enumerate(TURNED):
                    o = turn_banks[i % 4]
                    if i == 2:
                        dve.wait_ge(w_later, 16 * R_LOADS)
                        for k in range(KV):
                            dve.tensor_copy(wkrep[:, k, :, :], wkd[:, k, :].unsqueeze(1).broadcast_to([P, REP, LAT]))
                        dve.tensor_scalar(fwb2[:], nrm[:, 1:2], 2.0, None, ALU.mult)
                    dve.wait_ge(w_tp, i + 1)
                    if kind == "alog":
                        ins = dve.tensor_scalar(A[c][:], o[:, 0:NU], -1.0, None, ALU.mult)
                    else:
                        dst, n = {"w1": (w1T[:], HID), "w2": (w2T[:], HID), "h1": (h1T[:, c, :], HID),
                                  "h2": (h2T[:, c, :], HID), "w3": (w3T[:].rearrange("p c n -> p (c n)"), HID),
                                  "wq": (wqT[:, 4 * (c % 2):4 * (c % 2) + 4, :].rearrange("p h n -> p (h n)"), HID),
                                  "wup": (wupT[:].rearrange("p a n -> p (a n)"), 2 * LAT),
                                  "wqk": (wqk[:].rearrange("p h l -> p (h l)"), HEADS * LAT),
                                  "wvo": (wvo[:, c % KV, :], D)}[kind]
                        if kind == "w3":
                            ins = dve.tensor_tensor(w3T[:], o[:].rearrange("p (c n) -> p c n", c=NC),
                                                    s3.unsqueeze(1).broadcast_to([P, NC, D]), ALU.mult)
                        else:
                            ins = dve.tensor_copy(dst, o[:, 0:n])
                    if kind in ("w3", "wvo"):
                        w = w3T[:] if kind == "w3" else wvo[:, c:c + 1, :]
                        m = lmax[:, 0:w.shape[1]]
                        link(ins)
                        link(dve.tensor_reduce(m, w, AX.X, ALU.add))
                        link(dve.tensor_scalar(m, m, -1.0 / D, None, ALU.mult))
                        ins = dve.tensor_tensor(w, w, m.unsqueeze(2).broadcast_to([P, w.shape[1], D]), ALU.add)
                    ins.then_inc(w_cp, 1)
                    yield
                yield

            def mamba(row):
                def full(name):
                    dve.wait_ge(sem["full_m"], row("full_m", M_USE[name][2] + 1))
                    return use(name)

                links = [0]

                def link(ins):
                    links[0] += 1
                    ins.then_inc(sem["dve_m"], 1)
                    dve.wait_ge(sem["dve_m"], row("dve_m", links[0]))

                def dt_step(hf, k):
                    d, h = divmod(hf, NH)
                    if k == 0:
                        dve.wait_ge(sem["gated"], row("gated", max(hf - 1, 0)))
                        dve.wait_ge(sem["absd"], row("absd", hf + 1))
                        dve.tensor_scalar(tpos[:], use(f"dtp{hf}")[:], cols[d][:, 1, h:h + 1], 0.0,
                                          ALU.add, ALU.max).then_inc(sem["rpos"], 1)
                        dve.wait_ge(sem["expd"], row("expd", hf + 1))
                        dve.tensor_scalar(tsel[:], texp[:], SMALL, None, ALU.is_gt)
                    elif k == 1:
                        dve.wait_ge(sem["series"], row("series", hf + 1))
                        link(dve.scalar_tensor_tensor(tser[:], tser[:], 1.0, texp[:], ALU.add, ALU.mult))
                        dve.wait_ge(sem["logd"], row("logd", hf + 1))
                        dve.memset(tick[:], 0.0)
                        link(dve.copy_predicated(tser[:], tsel[:], tlog[:]))
                        dve.wait_ge(sem["lo"], row("lo", hf))
                        dve.tensor_tensor(dd[:, 0, :], tser[:], tpos[:], ALU.add).then_inc(sem["dt"], 1)
                        dve.wait_ge(sem["dt"], row("dt", hf + 1))
                        dve.tensor_tensor(dd[:, 1, :], dd[:, 0, :], u[d][:, h, :], ALU.mult
                                          ).then_inc(sem["du"], 1)

                def drive(n):
                    dve.wait_ge(sem["scan"], row("scan", max(n - 1, 0)))
                    dve.wait_ge(sem["du_full"], row("du_full", n + 1))
                    dve.tensor_tensor(dbu[:, n % 2, :], ps_du[:], brep[n // NU][:], ALU.mult
                                      ).then_inc(sem["dbu"], 1)

                def scan(n):
                    dve.wait_ge(sem["dbu"], row("dbu", n + 1))
                    dve.wait_ge(sem["dA"], row("dA", n + 1))
                    dve.wait_ge(sem["hc"], row("hc", max(n - 2, 0)))
                    dve.tensor_tensor_scan(hst[:, n % 3, :], ps_dt[n % 2][:], dbu[:, n % 2, :], 0.0,
                                           ALU.mult, ALU.add).then_inc(sem["scan"], 1)

                def gate(hf):
                    d, h = divmod(hf, NH)
                    dve.wait_ge(sem["y_red"], row("y_red", 4 * hf + 4))
                    dve.scalar_tensor_tensor(yg[:], u[d][:, h, :], cols[d][:, 2, h:h + 1], ps_y[:],
                                             ALU.mult, ALU.add).then_inc(sem["yskip"], 1)
                    dve.wait_ge(sem["yskip"], row("yskip", hf + 1))
                    o = gT[d][:, h, :] if d == 0 else gT[d][:, h, ::-1]
                    dve.tensor_tensor(o, yg[:], sz[d][:, h, :], ALU.mult).then_inc(sem["gated"], 1)

                for slot in range(SLOTS):
                    if slot in (4, 7):
                        d = slot // 3 - 1
                        dve.tensor_copy(dtin[32 * d:32 * d + R, :], full(f"dtin{d}")[32 * d:32 * d + R, :]
                                        ).then_inc(sem["dtin"], 1)
                    for hf in range(2 * NH):
                        if slot in DT_SLOTS[hf]:
                            dt_step(hf, DT_SLOTS[hf].index(slot))
                    n = slot - PREP
                    if 0 <= n < UNITS:
                        drive(n)
                    if 1 <= n <= UNITS:
                        scan(n - 1)
                    if n in GATES:
                        gate(GATES.index(n))
                    yield
                assert links[0] == PER["dve_m"], links

            def rest(row):
                def full(name):
                    dve.wait_ge(sem["full"], row("full", R_USE[name][2] + 1))
                    return use(name)

                links = [0]

                def link(ins):
                    links[0] += 1
                    ins.then_inc(sem["dve_r"], 1)
                    dve.wait_ge(sem["dve_r"], row("dve_r", links[0]))

                def scaled(n, dst):
                    dve.wait_ge(sem["rstd"], row("rstd", n + 1))
                    root = res if n == 1 else rstd
                    centred = use(f"cen{n}") if n < 4 else res
                    return dve.tensor_tensor(dst, centred[:], root[:], ALU.mult).then_inc(sem["norm"], 1)

                dve.wait_ge(sem["xkeep"], row("xkeep", 1))
                for d in range(2):
                    dve.tensor_tensor(nf[:, d, :], full(f"mo{d}")[:], xkept[:], ALU.add).then_inc(sem["resid"], 1)
                yield
                yield
                scaled(0, nf[:, 0, :])
                scaled(1, nf[:, 1, :])
                dve.wait_ge(sem["norm"], row("norm", 2))
                link(dve.tensor_tensor(nf[:, 0, :], nf[:, 0, :], nf[:, 1, :], ALU.add))
                dve.tensor_scalar(yy[:], nf[:, 0, :], nrm[:, 0:1], fwb2[:, 0:1], ALU.mult, ALU.add
                                  ).then_inc(sem["y"], 1)
                yield
                yield
                dve.wait_ge(sem["y"], row("y", 1))
                dve.scalar_tensor_tensor(res[:], full("ffo")[:], fb[:, 2:3], yy[:], ALU.add, ALU.add
                                         ).then_inc(sem["resid"], 1)
                yield
                yield
                scaled(2, nf[:, 0, :])
                dve.wait_ge(sem["norm"], row("norm", 3))
                link(dve.tensor_scalar(nf[:, 1, :], nf[:, 0, :], nrm[:, 2:3], nrm[:, 3:4], ALU.mult, ALU.add))
                dve.tensor_tensor(res[:], nf[:, 1, :], xkept[:], ALU.add).then_inc(sem["x1"], 1)
                yield
                yield
                scaled(3, xn[:, 0, :])
                yield
                for c in range(0, NC, 2):
                    yield
                    for cc in (c, c + 1):
                        dve.wait_ge(sem["a1"], row("a1", cc + 1))
                        dve.scalar_tensor_tensor(h0[:, cc, :], full(f"b{cc}")[:], sc[:, 1, cc:cc + 1], a1[:, cc % 2, :],
                                                 ALU.mult, ALU.mult).then_inc(sem["h0"], 1)
                    yield
                for _ in range(2 * NC):
                    yield
                dve.wait_ge(sem["norm"], row("norm", 4))
                dve.tensor_tensor(res[:], full("fo")[:], xn[:, 0, :], ALU.add).then_inc(sem["resid"], 1)
                yield
                scaled(4, xn[:, 1, :])
                yield
                for k in range(KV):
                    dve.tensor_copy(kT[:, k, :], full(f"k{k}")[:]).then_inc(sem["kT"], 1)
                    yield

                def place_query(i):
                    k, t, r = head(i)
                    rows = slice(LAT * r, LAT * (r + 1))
                    if t == 0 and r == 0:
                        dve.wait_ge(sem["qT"], row("qT", k + 1))
                    if i >= REP:
                        dve.wait_ge(sem["full"], row("full", R_USE[f"s{i - REP}"][2] + 1))
                    dve.tensor_copy(qz[rows, r, :], qT[rows, k, t * P:(t + 1) * P]).then_inc(sem["qz"], 1)

                place_query(0)
                yield
                for j in range(HEADS * TT + 3):
                    if j < HEADS * TT - 1:
                        place_query(j + 1)
                    if j < HEADS * TT:
                        w = (head(j)[1] + 1) * P
                        dve.tensor_reduce(nmax[:, j:j + 1], full(f"s{j}")[:, 0:w], AX.X, ALU.max, negate=True
                                          ).then_inc(sem["smax"], 1)
                    if 1 <= j <= HEADS * TT:
                        dve.wait_ge(sem["pexp"], row("pexp", j))
                        dve.reciprocal(rz[:, j - 1:j], zsum[:, j - 1:j]).then_inc(sem["rz"], 1)
                    if j in (REP * TT + 2, HEADS * TT + 2):
                        k = j // (REP * TT) - 1
                        dve.wait_ge(sem["att"], row("att", TT * (k + 1)))
                        dve.tensor_copy(yT[:, k, :], ps_att[:]).then_inc(sem["yT"], 1)
                    yield
                dve.wait_ge(sem["norm"], row("norm", 5))
                dve.tensor_tensor(res[:], full("ao")[:], xn[:, 1, :], ALU.add).then_inc(sem["resid"], 1)
                yield
                scaled(5, xn[:, 0, :])
                yield

                dve.tensor_copy(lg[:].rearrange("p n e -> p (n e)"), full("lg")[:, 0:TT * E]).then_inc(sem["lg"], 1)
                dve.wait_ge(sem["lg"], row("lg", 1))
                l_e = lg[:].unsqueeze(3).broadcast_to([P, TT, E, E])
                l_j = lg[:].unsqueeze(2).broadcast_to([P, TT, E, E])
                link(dve.tensor_reduce(lmax[:], lg[:], AX.X, ALU.max))
                dve.tensor_tensor(lsh[:], lg[:], lmax[:].unsqueeze(2).broadcast_to([P, TT, E]), ALU.subtract
                                  ).then_inc(sem["gmax"], 1)
                dve.tensor_tensor(cgt, l_j, l_e, ALU.is_gt)
                link(dve.tensor_tensor(ceq, l_j, l_e, ALU.is_equal))
                for n in range(TT):
                    ins = dve.tensor_tensor(ceq[:, n, :, :], ceq[:, n, :, :], lower, ALU.mult)
                link(ins)
                yield

                def more_gates():
                    link(dve.tensor_tensor(cgt, cgt, ceq, ALU.add))
                    link(dve.tensor_reduce(rank[:], cgt, AX.X, ALU.add))
                    dve.wait_ge(sem["gexp"], row("gexp", 1))
                    link(dve.scalar_tensor_tensor(gsel[:], rank[:], 2.0, lexp[:], ALU.is_lt, ALU.mult))
                    link(dve.tensor_reduce(gsum[:], gsel[:], AX.X, ALU.add))
                    link(dve.reciprocal(gsum[:], gsum[:]))
                    dve.tensor_tensor(gates[:], gsel[:], gsum[:].unsqueeze(2).broadcast_to([P, TT, E]), ALU.mult
                                      ).then_inc(sem["gates"], 1)

                for step, e in expert_steps():
                    if step == "gate" and e == 0:
                        more_gates()
                    elif step == "up":
                        if e >= 2:
                            dve.wait_ge(sem["full"], row("full", R_USE[f"eo{e - 2}"][2] + 1))
                        for c in range(2):
                            i = 2 * e + c
                            dve.wait_ge(sem["ea"], row("ea", i + 1))
                            dve.tensor_tensor(eh[:, e % 2, c, :], full(f"eb{e}{c}")[:], ea[:, i % 4, :], ALU.mult
                                              ).then_inc(sem["eh"], 1)
                    elif step == "down":
                        if e == 0:
                            dve.wait_ge(sem["gates"], row("gates", 1))
                        if e >= 2:
                            dve.wait_ge(sem["acc"], row("acc", e - 1))
                        gate_e = gates[:, :, e:e + 1].broadcast_to([P, TT, D])
                        dve.tensor_tensor(gy[:, e % 2, :, :], full(f"eo{e}")[:].rearrange("p (n d) -> p n d", n=TT),
                                          gate_e, ALU.mult).then_inc(sem["eo"], 1)
                    yield
                dve.wait_ge(sem["acc"], row("acc", E))
                for n in range(TT):
                    ins = dve.bn_stats(stats[:, n, :], acc[:, n, :])
                link(ins)
                dve.memset(tick[:], 0.0)
                for n in range(TT):
                    ins = dve.bn_aggr(mv[:, n, :], stats[:, n, :])
                ins.then_inc(sem["mv"], 1)
                yield
                dve.wait_ge(sem["stored"], row("stored", 0))
                dve.wait_ge(sem["trs"], row("trs", 1))
                for n in range(TT):
                    ins = dve.tensor_scalar(otok[:, n, :], acc[:, n, :], mv[:, n, 0:1], rst4[:, n:n + 1],
                                            ALU.subtract, ALU.mult)
                ins.then_inc(sem["outn"], 1)
                yield
                assert links[0] == PER["dve_r"], links

            side_by_side(mamba(counts(0)), turned_out(), TURN_STEPS)
            with dve.Fori(0, B - 1) as b:
                side_by_side(mamba(counts(b, 1)), rest(counts(b)), FOLLOW)
            alone(rest(counts(B - 1)))


        @block.gpsimd
        def _(pool):
            pool.memset(qz[:], 0.0)
            pool.memset(xpad[:], 0.0).then_inc(w_set, 1)
            def mamba(row):
                def dt_step(hf, k):
                    if k == 0:
                        pool.wait_ge(sem["third"], row("third", hf + 1))
                        pool.tensor_tensor(tser[:], tser[:], texp[:], ALU.mult).then_inc(sem["series"], 1)
                    elif k == 2:
                        pool.wait_ge(sem["hi"], row("hi", hf + 1))
                        pool.tensor_tensor(dd[:], dd[:], parts[:, 0, :, :], ALU.subtract
                                           ).then_inc(sem["res"], 1)
                    elif k == 3:
                        pool.wait_ge(sem["mid"], row("mid", hf + 1))
                        pool.tensor_tensor(parts[:, 2, :, :], dd[:], parts[:, 1, :, :], ALU.subtract
                                           ).then_inc(sem["lo"], 1)

                for slot in range(SLOTS):
                    for hf in range(2 * NH):
                        if slot in DT_SLOTS[hf]:
                            dt_step(hf, DT_SLOTS[hf].index(slot))
                    n = slot - PREP - 1
                    if 0 <= n < UNITS:
                        pool.wait_ge(sem["scan"], row("scan", n + 1))
                        pool.wait_ge(sem["y_red"], row("y_red", max((n - 6) // 4 + 1, 0)))
                        pool.tensor_tensor(hc[:, n % 6, :], hst[:, n % 3, :], crep[n // NU][:], ALU.mult
                                           ).then_inc(sem["hc"], 1)
                    yield

            def rest(row):
                for _ in range(26):
                    yield
                for j in range(HEADS * TT + 3):
                    if 1 <= j <= HEADS * TT:
                        i = j - 1
                        w = (head(i)[1] + 1) * P
                        pool.wait_ge(sem["rz"], row("rz", i + 1))
                        if i >= 2:
                            pool.wait_ge(sem["full"], row("full", R_USE[f"t{i - 2}"][2] + 1))
                        pool.tensor_tensor(pn[:, i % 2, 0:w], pexp[:, i % 2, 0:w],
                                           rz[:, i:i + 1].broadcast_to([P, w]), ALU.mult).then_inc(sem["pn"], 1)
                    yield
                for _ in range(3):
                    yield
                for step, e in expert_steps():
                    if step == "down":
                        if e == 0:
                            pool.wait_ge(sem["x3"], row("x3", 1))
                        else:
                            pool.wait_ge(sem["acc"], row("acc", e))
                        pool.wait_ge(sem["eo"], row("eo", e + 1))
                        pool.tensor_tensor(acc, gy[:, e % 2, :, :], x3 if e == 0 else acc, ALU.add
                                           ).then_inc(sem["acc"], 1)
                    yield
                yield
                yield

            alone(mamba(counts(0)))
            with pool.Fori(0, B - 1) as b:
                side_by_side(mamba(counts(b, 1)), rest(counts(b)), FOLLOW)
            alone(rest(counts(B - 1)))


_PRE = {"L0_attn_": "", "L0_ffn_": "", "L1_attn_": "", "L1_ffn_": ""}


def _short(name):
    for pre in _PRE:
        if name.startswith(pre):
            short = name[len(pre):]
            return "e" + short if pre == "L1_ffn_" and short in ("w1", "w2", "w3") else short
    return name


def kernel(**inputs):
    import numpy as _np
    import concourse.bacc as _bacc
    from concourse import mybir as _mybir
    from concourse.bass_utils import run_bass_kernel_spmd as _run

    nc = _bacc.Bacc("TRN2", target_bir_lowering=False, num_devices=1)
    arrays, args = {}, {}
    for name, value in list(inputs.items()) + [("const", constants())]:
        v = _np.ascontiguousarray(value)
        key = f"in_{name}_dram"
        arrays[key] = v
        args[_short(name)] = nc.dram_tensor(key, v.shape, _mybir.dt.from_np(v.dtype), kind="ExternalInput").ap()
    shape = inputs["L0_attn_x"].shape
    out = nc.dram_tensor("out_dram", shape, F32, kind="ExternalOutput").ap()
    two_layer_kernel(nc, args, out)
    r = _run(nc, [arrays], core_ids=[0])
    return r.results[0]["out_dram"]
```
